# Optimizing a Trainium2 kernel written in Bass

```python
import numpy as np
import jax
import jax.numpy as jnp

def _softmax(x, axis=-1):
    return jax.nn.softmax(x, axis=axis)

def _gelu(x):
    return jax.nn.gelu(x, approximate=True)

def _silu(x):
    return jax.nn.silu(x)

def _sigmoid(x):
    return jax.nn.sigmoid(x)

def _layernorm(x, axis=-1, eps=1e-05):
    m = jnp.mean(x, axis=axis, keepdims=True)
    v = jnp.var(x, axis=axis, keepdims=True)
    return (x - m) / jnp.sqrt(v + eps)

def _scatter_add(tgt, idx, src, axis=0):
    return tgt.at[idx].add(src)

def _segment_sum(src, seg, n):
    return jax.ops.segment_sum(src, seg, n)
kernel_name = 'mk_adj_ffn_d2_adj_r2_3270ae'

def setup_inputs(seed: int=0):
    np.random.seed(seed)
    _w = jnp.asarray

    def _rec_inputs():
        import jax
        import jax.numpy as jnp
        _gk = jax.random.key(seed)
        x = -0.001003 + 1 * jax.random.normal(jax.random.fold_in(_gk, 1), (2048, 128), jnp.float32)
        _a = jax.random.bernoulli(jax.random.fold_in(_gk, 2), 0.00390625, (2048, 2048))
        _a = jnp.logical_or(_a, jnp.swapaxes(_a, -1, -2))
        _a = jnp.logical_or(_a, jnp.eye(2048, dtype=bool))
        _af = _a.astype(jnp.float32)
        _af = _af * jax.random.uniform(jax.random.fold_in(_gk, 3), (2048, 2048), jnp.float32, 0.05, 0.999999)
        adj = _af
        return (x, adj)
    x, adj = _rec_inputs()

    def _L0_gnn_setup():
        import jax, jax.numpy as jnp
        import numpy as np
        N = 3072
        HID = 128
        T = 350
        DENSITY = 0.05
        key = jax.random.key(seed)
        k1, k2, k3, k4, k5, k6 = jax.random.split(key, 6)
        h = jax.random.normal(k1, (N, HID), dtype=jnp.float32)
        a = jax.random.uniform(k2, (N, N), dtype=jnp.float32)
        mask = jax.random.uniform(k3, (N, N)) < DENSITY
        adj = jnp.where(mask, a, 0.0)
        simlar = jax.random.normal(k4, (N, N), dtype=jnp.float32)
        s = 1.0 / np.sqrt(HID)
        W_proj = jax.random.uniform(k5, (HID, HID), minval=-s, maxval=s, dtype=jnp.float32)
        b_proj = jnp.zeros((HID,), dtype=jnp.float32)
        W_gcn = jax.random.uniform(k6, (HID, HID), minval=-s, maxval=s, dtype=jnp.float32)
        b_gcn = jnp.zeros((HID,), dtype=jnp.float32)
        return {'h': h, 'adj': adj, 'simlar': simlar, 'W_proj': W_proj, 'b_proj': b_proj, 'W_gcn': W_gcn, 'b_gcn': b_gcn}
    _L0_gnn_all = _L0_gnn_setup()
    _L0_gnn_in = {k: v for k, v in _L0_gnn_all.items() if k in ('W_proj', 'b_proj', 'W_gcn', 'b_gcn')}
    del _L0_gnn_all

    def _L0_ffn_setup():
        import jax, jax.numpy as jnp
        import numpy as np
        D_MODEL = 128
        EXPERT_DIM = 256
        NUM_EXPERTS = 8
        TOP_K = 2
        SEQ_LEN = 1024
        BATCH = 2
        key = jax.random.key(seed)
        ks = jax.random.split(key, 8)
        s = 0.02
        x = jax.random.normal(ks[0], (SEQ_LEN, BATCH, D_MODEL), dtype=jnp.float32)
        Wg = jax.random.normal(ks[1], (D_MODEL, NUM_EXPERTS), dtype=jnp.float32) * s
        bg = jax.random.normal(ks[2], (NUM_EXPERTS,), dtype=jnp.float32) * s
        bias = jnp.zeros((NUM_EXPERTS,), dtype=jnp.float32)
        W1 = jax.random.normal(ks[3], (NUM_EXPERTS, D_MODEL, EXPERT_DIM), dtype=jnp.float32) * s
        b1 = jax.random.normal(ks[4], (NUM_EXPERTS, EXPERT_DIM), dtype=jnp.float32) * s
        W2 = jax.random.normal(ks[5], (NUM_EXPERTS, EXPERT_DIM, D_MODEL), dtype=jnp.float32) * s
        b2 = jax.random.normal(ks[6], (NUM_EXPERTS, D_MODEL), dtype=jnp.float32) * s
        return {'x': x, 'Wg': Wg, 'bg': bg, 'bias': bias, 'W1': W1, 'b1': b1, 'W2': W2, 'b2': b2}
    _L0_ffn_all = _L0_ffn_setup()
    _L0_ffn_in = {k: v for k, v in _L0_ffn_all.items() if k in ('Wg', 'bg', 'bias', 'W1', 'b1', 'W2', 'b2')}
    del _L0_ffn_all

    def _L1_gnn_setup():
        import jax, jax.numpy as jnp
        import numpy as np
        N, IN_C, OUT_C = (4096, 128, 128)
        key = jax.random.key(seed)
        k1, k2, k3 = jax.random.split(key, 3)
        x = jax.random.normal(k1, (N, IN_C), dtype=jnp.float32)
        adj = jax.random.uniform(k2, (N, N), dtype=jnp.float32)
        w = jax.random.uniform(k3, (IN_C, OUT_C), dtype=jnp.float32)
        return {'x': x, 'adj': adj, 'w': w}
    _L1_gnn_all = _L1_gnn_setup()
    _L1_gnn_in = {k: v for k, v in _L1_gnn_all.items() if k in ('w',)}
    del _L1_gnn_all

    def _L1_ffn_setup():
        import jax, jax.numpy as jnp
        import numpy as np
        B, T, C = (64, 192, 128)
        NH, NKV = (4, 2)
        HD = C // NH
        NREP = NH // NKV
        NE, TOPK = (8, 2)
        HID = int(8 / 3 * C)
        EPS_RMS = 1e-06

        def _rope_tables(t_len):
            inv_freq = 1.0 / 10000.0 ** (np.arange(0, HD, 2, dtype=np.float32) / HD)
            t = np.arange(t_len, dtype=np.float32)
            freqs = np.outer(t, inv_freq)
            emb = np.concatenate([freqs, freqs], axis=-1)
            return (jnp.asarray(np.cos(emb)), jnp.asarray(np.sin(emb)))

        def _rotate_half(x):
            h = x.shape[-1] // 2
            return jnp.concatenate([-x[..., h:], x[..., :h]], axis=-1)

        def _rmsnorm(v, w):
            return v * jax.lax.rsqrt(jnp.mean(v * v, axis=-1, keepdims=True) + EPS_RMS) * w
        key = jax.random.key(seed)
        ks = jax.random.split(key, 10)
        s = lambda k, shape: jax.random.normal(k, shape, jnp.float32) * 0.02
        return {'x': jax.random.normal(ks[0], (B, T, C), jnp.float32), 'ln1_w': jnp.ones((C,), jnp.float32), 'ln2_w': jnp.ones((C,), jnp.float32), 'wq': s(ks[1], (NH * HD, C)), 'wk': s(ks[2], (NKV * HD, C)), 'wv': s(ks[3], (NKV * HD, C)), 'wo': s(ks[4], (C, C)), 'router_w': s(ks[5], (NE, C)), 'w1': s(ks[6], (NE, HID, C)), 'w2': s(ks[7], (NE, C, HID)), 'w3': s(ks[8], (NE, HID, C))}
    _L1_ffn_all = _L1_ffn_setup()
    _L1_ffn_in = {k: v for k, v in _L1_ffn_all.items() if k in ('ln1_w', 'ln2_w', 'wq', 'wk', 'wv', 'wo', 'router_w', 'w1', 'w2', 'w3')}
    del _L1_ffn_all
    return {'x': x, 'adj': adj, 'L0_gnn_W_proj': _L0_gnn_in['W_proj'], 'L0_gnn_b_proj': _L0_gnn_in['b_proj'], 'L0_gnn_W_gcn': _L0_gnn_in['W_gcn'], 'L0_gnn_b_gcn': _L0_gnn_in['b_gcn'], 'L0_ffn_Wg': _L0_ffn_in['Wg'], 'L0_ffn_bg': _L0_ffn_in['bg'], 'L0_ffn_bias': _L0_ffn_in['bias'], 'L0_ffn_W1': _L0_ffn_in['W1'], 'L0_ffn_b1': _L0_ffn_in['b1'], 'L0_ffn_W2': _L0_ffn_in['W2'], 'L0_ffn_b2': _L0_ffn_in['b2'], 'L1_gnn_w': _L1_gnn_in['w'], 'L1_ffn_ln1_w': _L1_ffn_in['ln1_w'], 'L1_ffn_ln2_w': _L1_ffn_in['ln2_w'], 'L1_ffn_wq': _L1_ffn_in['wq'], 'L1_ffn_wk': _L1_ffn_in['wk'], 'L1_ffn_wv': _L1_ffn_in['wv'], 'L1_ffn_wo': _L1_ffn_in['wo'], 'L1_ffn_router_w': _L1_ffn_in['router_w'], 'L1_ffn_w1': _L1_ffn_in['w1'], 'L1_ffn_w2': _L1_ffn_in['w2'], 'L1_ffn_w3': _L1_ffn_in['w3']}

def reference(x, adj, L0_gnn_W_proj, L0_gnn_b_proj, L0_gnn_W_gcn, L0_gnn_b_gcn, L0_ffn_Wg, L0_ffn_bg, L0_ffn_bias, L0_ffn_W1, L0_ffn_b1, L0_ffn_W2, L0_ffn_b2, L1_gnn_w, L1_ffn_ln1_w, L1_ffn_ln2_w, L1_ffn_wq, L1_ffn_wk, L1_ffn_wv, L1_ffn_wo, L1_ffn_router_w, L1_ffn_w1, L1_ffn_w2, L1_ffn_w3):
    import jax
    import jax.numpy as jnp

    def _L0_gnn_ref(h, adj, simlar, W_proj, b_proj, W_gcn, b_gcn):
        import jax, jax.numpy as jnp
        import numpy as np
        N = 3072
        HID = 128
        T = 350
        DENSITY = 0.05
        sim = jnp.tanh(adj * simlar)
        filt = sim * (adj > 0).astype(sim.dtype)
        vals, idx = jax.lax.top_k(filt, T)
        nnz = jnp.sum(filt != 0, axis=1)
        keep = jnp.arange(T)[None, :] < nnz[:, None]
        rows = jnp.arange(filt.shape[0])[:, None]
        new_adj = jnp.zeros_like(filt).at[rows, idx].set(jnp.where(keep, vals, 0.0))
        h2 = jnp.tanh(h @ W_proj + b_proj)
        feat = jax.nn.relu(new_adj @ (h2 @ W_gcn) + b_gcn)
        return feat

    def _L0_ffn_ref(x, Wg, bg, bias, W1, b1, W2, b2):
        import jax, jax.numpy as jnp
        import numpy as np
        D_MODEL = 128
        EXPERT_DIM = 256
        NUM_EXPERTS = 8
        TOP_K = 2
        SEQ_LEN = 1024
        BATCH = 2
        x_flat = x.reshape(-1, D_MODEL)
        gate_logits = x_flat @ Wg + bg + bias
        topk_vals, topk_idx = jax.lax.top_k(gate_logits, TOP_K)
        topk_w = jax.nn.softmax(topk_vals, axis=-1)
        combine = (jax.nn.one_hot(topk_idx, NUM_EXPERTS, dtype=x.dtype) * topk_w[..., None]).sum(axis=1)
        h = jax.nn.relu(jnp.einsum('td,edh->teh', x_flat, W1) + b1)
        y = jnp.einsum('teh,ehd->ted', h, W2) + b2
        out = jnp.einsum('ted,te->td', y, combine)
        return out.reshape(x.shape)

    def _L1_gnn_ref(x, adj, w):
        import jax, jax.numpy as jnp
        import numpy as np
        N, IN_C, OUT_C = (4096, 128, 128)
        A = adj + jnp.eye(adj.shape[0], dtype=adj.dtype)
        deg = jnp.sum(A, axis=1)
        d_isqrt = jax.lax.rsqrt(deg)
        A_hat = A * d_isqrt[:, None] * d_isqrt[None, :]
        h = jnp.matmul(A_hat, x)
        return jax.nn.elu(jnp.matmul(h, w))

    def _L1_ffn_ref(x, ln1_w, ln2_w, wq, wk, wv, wo, router_w, w1, w2, w3):
        import jax, jax.numpy as jnp
        import numpy as np
        B, T, C = (64, 192, 128)
        NH, NKV = (4, 2)
        HD = C // NH
        NREP = NH // NKV
        NE, TOPK = (8, 2)
        HID = int(8 / 3 * C)
        EPS_RMS = 1e-06

        def _rope_tables(t_len):
            inv_freq = 1.0 / 10000.0 ** (np.arange(0, HD, 2, dtype=np.float32) / HD)
            t = np.arange(t_len, dtype=np.float32)
            freqs = np.outer(t, inv_freq)
            emb = np.concatenate([freqs, freqs], axis=-1)
            return (jnp.asarray(np.cos(emb)), jnp.asarray(np.sin(emb)))

        def _rotate_half(x):
            h = x.shape[-1] // 2
            return jnp.concatenate([-x[..., h:], x[..., :h]], axis=-1)

        def _rmsnorm(v, w):
            return v * jax.lax.rsqrt(jnp.mean(v * v, axis=-1, keepdims=True) + EPS_RMS) * w
        Bx, Tx, Cx = x.shape
        h = _rmsnorm(x, ln1_w)
        q = (h @ wq.T).reshape(Bx, Tx, NH, HD).transpose(0, 2, 1, 3)
        k = (h @ wk.T).reshape(Bx, Tx, NKV, HD).transpose(0, 2, 1, 3)
        v = (h @ wv.T).reshape(Bx, Tx, NKV, HD).transpose(0, 2, 1, 3)
        cos, sin = _rope_tables(Tx)
        cos, sin = (cos[None, None], sin[None, None])
        q = q * cos + _rotate_half(q) * sin
        k = k * cos + _rotate_half(k) * sin
        k = jnp.repeat(k, NREP, axis=1)
        v = jnp.repeat(v, NREP, axis=1)
        scores = jnp.einsum('bhtd,bhsd->bhts', q, k) / jnp.sqrt(jnp.float32(HD))
        causal = jnp.tril(jnp.ones((Tx, Tx), dtype=bool))
        scores = jnp.where(causal[None, None], scores, jnp.float32(-1e+30))
        att = jax.nn.softmax(scores, axis=-1)
        y = jnp.einsum('bhts,bhsd->bhtd', att, v).transpose(0, 2, 1, 3).reshape(Bx, Tx, Cx)
        x = x + y @ wo.T
        flat = _rmsnorm(x, ln2_w).reshape(-1, Cx)
        probs = jax.nn.softmax(flat @ router_w.T, axis=-1)
        tp, ti = jax.lax.top_k(probs, TOPK)
        tp = tp / (jnp.sum(tp, axis=-1, keepdims=True) + 1e-09)
        weights = jnp.sum(tp[..., None] * jax.nn.one_hot(ti, NE, dtype=flat.dtype), axis=1)
        out = jnp.zeros_like(flat)
        for e in range(NE):
            hh = jax.nn.silu(flat @ w1[e].T) * (flat @ w3[e].T)
            out = out + weights[:, e:e + 1] * (hh @ w2[e].T)
        return x + out.reshape(Bx, Tx, Cx)
    x = x + _L0_gnn_ref(_layernorm(x, axis=-1), adj, adj, L0_gnn_W_proj, L0_gnn_b_proj, L0_gnn_W_gcn, L0_gnn_b_gcn)
    x = x + _L0_ffn_ref(_layernorm(x, axis=-1)[None], L0_ffn_Wg, L0_ffn_bg, L0_ffn_bias, L0_ffn_W1, L0_ffn_b1, L0_ffn_W2, L0_ffn_b2)[0]
    x = x + _L1_gnn_ref(_layernorm(x, axis=-1), adj, L1_gnn_w)
    x = x + _L1_ffn_ref(_layernorm(x, axis=-1)[None], L1_ffn_ln1_w, L1_ffn_ln2_w, L1_ffn_wq, L1_ffn_wk, L1_ffn_wv, L1_ffn_wo, L1_ffn_router_w, L1_ffn_w1, L1_ffn_w2, L1_ffn_w3)[0]
    return x

_drawn_inputs = setup_inputs


def setup_inputs(seed=0):
    import zlib

    import numpy as np

    out = dict(_drawn_inputs(seed))
    spreads = {'L0_gnn_b_proj': (0.0, 0.1),
     'L0_gnn_b_gcn': (0.0, 0.1),
     'L0_ffn_bias': (0.0, 0.1),
     'L1_ffn_ln1_w': (1.0, 0.6),
     'L1_ffn_ln2_w': (1.0, 0.6)}
    factors = {'L0_ffn_bg': 7.712,
     'L0_ffn_b1': 8.0,
     'L0_ffn_b2': 2.674,
     'L1_ffn_wq': 8.0,
     'L1_ffn_wk': 8.0,
     'L1_ffn_wv': 8.0,
     'L1_ffn_wo': 8.0,
     'L1_ffn_router_w': 8.0,
     'L1_ffn_w1': 8.0,
     'L1_ffn_w2': 8.0,
     'L1_ffn_w3': 8.0}
    for name, (base, spread) in spreads.items():
        noise = np.random.default_rng([zlib.crc32(name.encode()), seed]).standard_normal(out[name].shape)
        drawn = base * np.exp(spread * noise) if base else spread * noise
        out[name] = jnp.asarray(drawn.astype(out[name].dtype))
    for name, factor in factors.items():
        out[name] = (out[name] * factor).astype(out[name].dtype)
    return out
```

```python
from contextlib import ExitStack

import concourse.bass as bass
from concourse import mybir

F32 = mybir.dt.float32
F16 = mybir.dt.float16
BF16 = mybir.dt.bfloat16
I32 = mybir.dt.int32
ALU = mybir.AluOpType
ACT = mybir.ActivationFunctionType
AX_X = mybir.AxisListType.X

P = 128
T = 2048
D = 128
NT = T // P
CW = 512
NC = T // CW
TPC = CW // P
NEG = -1e30

TOP = 350
LIMIT = TOP
EPS_LN = 1e-5
EPS_RMS = 1e-6
E0 = 8
H0 = 256
K0 = H0 // P
E1 = 8
H1 = 341
KS1 = [(0, 128), (128, 128), (256, 85)]
NH = 4
NKV = 2
HD = 32

SX = 32.0
SW = 256.0
SH = 8.0
SQ = 8.0


class Chain:

    def __init__(self, eng, sem):
        self.eng, self.sem, self.done, self.here = eng, sem, 0, 0
        self.base = 0

    def __call__(self, ins):
        ins.then_inc(self.sem, 1)
        self.here += 1
        self.eng.wait_ge(self.sem, self.base + self.here)

    def turn(self, i, per):
        if self.here:
            self.done += self.here
            self.here = 0
        self.base = i * per + self.done

    def turn_ends(self, per):
        assert self.here == per, (self.here, per)
        self.here = 0

    def loop_ends(self, turns, per):
        self.done += turns * per
        self.base = self.done


def program(nc, x_in, adj_t, adj_in, w_proj, b_proj, w_gcn, b_gcn, f0_wg, f0_bg, f0_bias, f0_w1, f0_b1,
            f0_w2, f0_b2, g1_w, ln1, ln2, wq, wk, wv, wo, w_router, f1_w1, f1_w2, f1_w3, cos_t, sin_t, out):
    with ExitStack() as ctx:
        def sb(name, shape, dt=F32):
            return ctx.enter_context(nc.sbuf_tensor(name, shape, dt))

        def sem(name):
            return ctx.enter_context(nc.semaphore(name))

        A = sb("A", [P, NT, T])
        x = sb("x", [P, NT, D])
        xn = sb("xn", [P, NT, D])
        G = sb("G", [P, NT, D])
        R = sb("R", [P, 5 * T])
        xT = sb("xT", [P, T])
        ident = sb("ident", [P, P])
        ones = sb("ones", [P, 32])
        ones_b = sb("ones_b", [P, 32], BF16)
        neg_half = sb("neg_half", [P, NT])
        rev = sb("rev", [P, NT, 8])
        wmat = sb("wmat", [P, 3, P])
        cols = sb("cols", [P, 8])
        wg32 = sb("wg32", [P, 8])
        wg16 = sb("wg16", [P, 2, 8], F16)
        gbias = sb("gbias", [P, 2, 8])
        b2_sb = sb("b2_sb", [8, D])
        bst = sb("bst", [P, NT, 6])
        mv = sb("mv", [P, NT, 2])
        ve = sb("ve", [P, NT])
        rstd = sb("rstd", [P, NT])
        rd = sb("rd", [P, NT])
        deg_row = sb("deg_row", [P, CW])
        dis = sb("dis", [P, NT])
        lg = xT[:, 0:10 * NT * 8].rearrange("p (n t e) -> p n t e", n=10, e=8)
        sm = sb("sm", [P, 12, NT])
        comb = sb("comb", [P, NT, 8])
        cnt = sb("cnt", [P, 4])
        flag = sb("flag", [1, 1], I32)

        FB = 3
        fbuf = R[:, 0:FB * T].rearrange("p (b t) -> p b t", b=FB)
        mbuf = R[:, FB * T:(FB + 1) * T].bitcast(BF16).rearrange("p (b t) -> p b t", b=2)
        h2T = R[:, 4 * T:5 * T]
        a_row, f_row, e_row, c_row = (R[:, n * T:(n + 1) * T] for n in range(4))
        rT = R[:, 4 * T:4 * T + 2 * CW].rearrange("p (b t) -> p b t", b=2)
        gen = R[:, 4 * T + 2 * CW:4 * T + 2 * CW + 8]
        thr, bit, cand, ge = (gen[:, n:n + 1].bitcast(I32) for n in range(4))
        thr_f, cand_f, cnt_f, need_f = gen[:, 0:1], gen[:, 2:3], gen[:, 4:5], gen[:, 5:6]
        st_w1 = R[:, 0:512].rearrange("p (s h) -> p s h", s=2)
        st_w2 = R[:, 512:1024].rearrange("p (s k d) -> p s k d", s=2, k=K0)
        st_b1 = R[:, 1024:1028].rearrange("p (s k) -> p s k", s=2)
        w1h = R[:, 1028:1284].bitcast(F16).rearrange("p (s h) -> p s h", s=2)
        w1l = R[:, 1284:1540].bitcast(F16).rearrange("p (s h) -> p s h", s=2)
        w2h = R[:, 1540:1796].bitcast(F16).rearrange("p (s k d) -> p s k d", s=2, k=K0)
        w2l = R[:, 1796:2052].bitcast(F16).rearrange("p (s k d) -> p s k d", s=2, k=K0)
        h32 = R[:, 2052:2052 + 4 * CW].rearrange("p (b t) -> p b t", b=4)
        o = 2052 + 4 * CW
        hh_hi = R[:, o:o + 2 * K0 * CW // 2].bitcast(F16).rearrange("p (b k t) -> p b k t", b=2, k=K0)
        o += K0 * CW
        hh_lo = R[:, o:o + 2 * K0 * CW // 2].bitcast(F16).rearrange("p (b k t) -> p b k t", b=2, k=K0)
        o += K0 * CW
        combT = R[0:8, o:o + T]
        o += T
        G16 = G[:, :, :].rearrange("p t d -> p (t d)").bitcast(F16)
        xh, xl = G16[:, 0:T], G16[:, T:2 * T]
        assert o <= 5 * T

        hagg = R[:, 0:2 * CW].rearrange("p (b t) -> p b t", b=2)
        zs = R[:, 2 * CW:4 * CW].rearrange("p (b t) -> p b t", b=2)
        ez = R[:, 4 * CW:6 * CW].rearrange("p (b t) -> p b t", b=2)
        cos_sb = R[:, 2 * T:3 * T]
        sin_sb = R[:, 3 * T:4 * T]
        o = 4 * T
        wq32, wk32, wv32, wo32, wr32 = (R[:, o + a:o + b] for a, b in ((0, 128), (128, 192), (192, 256), (256, 384), (384, 392)))
        o += 392
        watt = R[:, o:o + 456].bitcast(F16).rearrange("p (s n) -> p s n", s=2)
        WQ, WQR, WK, WKR, WV, WR = 0, 128, 256, 320, 384, 448
        o += 456
        AF = A[:, :, :].rearrange("p j t -> p (j t)")
        KQ = 3 * HD
        Qs = AF[:, 0:NH * T // 2].bitcast(F16).rearrange("p (h t) -> p h t", h=NH)
        a = NH * T // 2
        Ks = AF[:, a:a + NKV * T // 2].bitcast(F16).rearrange("p (h t) -> p h t", h=NKV)
        a += NKV * T // 2
        Pb = AF[:, a:a + 2 * NH * CW].rearrange("p (b h t) -> p b h t", b=2, h=NH)
        a += 2 * NH * CW
        V = AF[:, a:a + NT * NKV * HD].rearrange("p (t d) -> p t d", t=NT)
        a += NT * NKV * HD
        yT = AF[:, a:a + T]
        a += T
        q16 = AF[:, a:a + T].bitcast(F16).rearrange("p (s t) -> p s t", s=2)
        a += T
        k16 = AF[0:NKV * HD, a:a + T].bitcast(F16).rearrange("p (s t) -> p s t", s=2)
        a += T
        rope = AF[:, a:a + 6 * CW].rearrange("p (n t) -> p n t", n=6)
        a += 6 * CW
        o_sb = AF[:, a:a + CW]
        d_sb = AF[:, a + CW:a + 2 * CW]
        r_sb = AF[:, a + 2 * CW:a + 3 * CW]
        a += 3 * CW
        pm = AF[:, a:a + NH * TPC * NC].rearrange("p (h q b) -> p h q b", h=NH, q=TPC)
        a += NH * TPC * NC
        m32 = AF[:, a:a + 16].rearrange("p (h q) -> p h q", h=NH)
        m16 = AF[:, a + 16:a + 24].bitcast(F16).rearrange("p (h q) -> p h q", h=NH)
        a += 24
        ident_b = AF[:, a:a + 64].bitcast(BF16)
        ident_h = AF[:, a + 64:a + 128].bitcast(F16)
        mask_ts = AF[:, a + 128:a + 192].bitcast(BF16)
        mask_st = AF[:, a + 192:a + 256].bitcast(BF16)
        a += 256
        v13 = AF[:, a:a + 4 * H1].rearrange("p (s m h) -> p s m h", s=2, m=2)
        a += 4 * H1
        v2 = AF[:, a:a + 2 * 3 * D].rearrange("p (s k d) -> p s k d", s=2, k=3)
        a += 6 * D
        v13h = AF[:, a:a + 2 * H1].bitcast(F16).rearrange("p (s m h) -> p s m h", s=2, m=2)
        a += 2 * H1
        v13l = AF[:, a:a + 2 * H1].bitcast(F16).rearrange("p (s m h) -> p s m h", s=2, m=2)
        a += 2 * H1
        v2h = AF[:, a:a + 3 * D].bitcast(F16).rearrange("p (s k d) -> p s k d", s=2, k=3)
        a += 3 * D
        v2l = AF[:, a:a + 3 * D].bitcast(F16).rearrange("p (s k d) -> p s k d", s=2, k=3)
        a += 3 * D
        assert a <= NT * T
        a = 0
        silu_sb = AF[:, a:a + 2 * CW].rearrange("p (b t) -> p b t", b=2)
        a += 2 * CW
        g32 = AF[:, a:a + 4 * CW].rearrange("p (b t) -> p b t", b=4)
        a += 4 * CW
        g_hi = AF[:, a:a + 3 * CW].bitcast(F16).rearrange("p (b k t) -> p b k t", b=2, k=3)
        a += 3 * CW
        g_lo = AF[:, a:a + 3 * CW].bitcast(F16).rearrange("p (b k t) -> p b k t", b=2, k=3)
        xT16 = xT[:, :].bitcast(F16)
        lg1 = G[:, :, :].rearrange("p t d -> p (t d)")[:, 0:10 * NT * 8].rearrange("p (n t e) -> p n t e", n=10, e=8)
        th, tl = xT16[:, 0:T], xT16[:, T:2 * T]

        ps = ctx.enter_context(nc.psum_tensor("ps", [P, 8, CW], F32))

        s_x = sem("x_loaded")
        s_small = sem("small_loaded")
        s_A = [sem(f"adj_tile_{j}_loaded") for j in range(NT)]
        s_const = sem("constants_made")
        s_cpool = sem("pool_steps")
        s_dve = sem("vector_steps")
        s_acts = sem("scalar_steps")
        s_var = sem("variance_ready")
        s_rstd = sem("rstd_ready")
        s_xn = sem("rows_normalised")
        s_tr = sem("rows_transposed")
        s_pre_ev = sem("transposed_copied")
        s_h2p = sem("h2_product")
        s_h2 = sem("h2_ready")
        s_gp = sem("g_product")
        s_G = sem("g_ready")
        s_sq = sem("square_ready")
        s_F = sem("filtered_ready")
        s_mask = sem("mask_ready")
        s_cntp = sem("tile_counted")
        s_aggp = sem("tile_aggregated")
        s_cmax = sem("count_max_ready")
        s_cmT = sem("count_max_transposed")
        s_flag = sem("flag_ready")
        s_feat = sem("features_ready")
        s_ftr = sem("features_transposed")
        s_x1 = sem("gnn0_added")
        s_degp = sem("deg_summed")
        s_degrow = sem("deg_row_copied")
        s_degc = sem("deg_columns")
        s_degv = sem("deg_plus_one")
        s_dis = sem("deg_isqrt_ready")
        s_xhi = sem("x_high_ready")
        s_xlo = sem("x_low_ready")
        s_wg = sem("gate_weights_split")
        s_gate = sem("gate_product")
        s_diff = sem("top_difference_ready")
        s_ediff = sem("exp_difference_ready")
        s_comb = sem("combine_weights_ready")
        s_ld0 = [sem(f"expert0_weights_slot{i}") for i in range(2)]
        s_w0 = sem("expert0_weights_split")
        s_h0 = sem("hidden0_product")
        s_relu = sem("hidden0_relu")
        s_hhi = sem("hidden0_high")
        s_hlo = sem("hidden0_low")
        s_y0 = sem("expert0_output")
        s_add0 = sem("expert0_added")
        s_cT = sem("combine_transposed")
        s_cTc = sem("combine_transposed_copied")
        s_b2 = sem("bias2_product")
        s_out = sem("output_stored")
        g_load = sem("general_rows_loaded")
        g_sq = sem("general_squares")
        g_tanh = sem("general_filtered")
        g_row = sem("general_rows_selected")
        g_tr = sem("general_transposed")
        g_cp = sem("general_transposed_copied")
        g_mm = sem("general_multiplied")
        s_gen = sem("general_vector_steps")
        s_agg1 = sem("gnn1_aggregated")
        s_hagg = sem("gnn1_aggregate_copied")
        s_z = sem("gnn1_product")
        s_zn = sem("gnn1_negative_part")
        s_ez = sem("gnn1_exp_ready")
        s_x3 = sem("gnn1_added")
        s_attw = sem("attention_weights_loaded")
        s_attws = sem("attention_weights_split")
        s_hn = sem("attention_rows_ready")
        s_qp = sem("query_product")
        s_kp = sem("key_product")
        s_vp = sem("value_product")
        s_qr = sem("query_rotated")
        s_kr = sem("key_rotated")
        s_qhi = sem("query_high_ready")
        s_khi = sem("key_high_ready")
        s_V = sem("values_ready")
        s_qlo = sem("query_low_ready")
        s_klo = sem("key_low_ready")
        s_mc = sem("masks_made")
        s_stack = [sem(f"queries_keys_stacked_half{i}") for i in range(2)]
        s_rm = sem("row_max_bank_filled")
        s_rmf = sem("row_max_bank_read")
        s_m = sem("row_max_ready")
        s_st = sem("scores_ready")
        s_p = sem("probabilities_ready")
        s_pv = sem("probabilities_used")
        s_od = sem("attention_sums_copied")
        s_yT = sem("attention_output_ready")
        s_x4 = sem("attention_added")
        s_ms = sem("mean_square_ready")
        s_r2 = sem("rms_ready")
        s_fn = sem("router_rows_ready")
        s_tr1 = sem("layer1_rows_transposed")
        s_thi = sem("layer1_high_ready")
        s_tlo = sem("layer1_low_ready")
        s_rt = sem("router_product")
        s_rl = sem("router_logits_shifted")
        s_re = sem("router_exp_ready")
        s_comb1 = sem("combine1_ready")
        s_ld1 = [sem(f"expert1_weights_slot{i}") for i in range(2)]
        s_w1 = sem("expert1_weights_split")
        s_h1 = sem("gate_unit_product")
        s_h3 = sem("up_unit_product")
        s_silu = sem("silu_ready")
        s_hh = sem("hidden1_ready")
        s_ghi = sem("hidden1_high")
        s_glo = sem("hidden1_low")
        s_y1 = sem("expert1_output")
        s_add1 = sem("expert1_added")

        steps = [(c, j) for c in range(NC) for j in [*range(TPC * c + TPC - 1, TPC * c - 1, -1), *range(TPC * c)]]

        def first_step(c, j):
            return j == TPC * c + TPC - 1

        def last_step(c, j):
            return j == (TPC * c - 1 if c else 0)

        def max_units(c):
            return ([("max", t, h, b) for t in range(TPC * c, TPC * c + TPC) for h in range(NH) for b in range(c + 1)]
                    + [("neg", c, h) for h in range(NH)])

        units_at = {}
        neg_done = []
        count = len(max_units(0))
        neg_done.append(count)
        for c in range(NC):
            todo = max_units(c + 1) if c + 1 < NC else []
            n = TPC * (c + 1)
            per_step = -(-len(todo) // n)
            for turn, (_, j) in enumerate([step for step in steps if step[0] == c]):
                units_at[(c, j)] = todo[turn * per_step:(turn + 1) * per_step]
                if turn == 3 and c:
                    units_at[(c, j)] = units_at[(c, j)] + [("out", c - 1)]
                count += len(units_at[(c, j)])
            neg_done.append(count)

        block = ctx.enter_context(nc.Block())

        small = [
            (wmat[:, 0, :], w_proj), (wmat[:, 1, :], w_gcn), (wmat[:, 2, :], g1_w),
            (cols[:, 0:1], b_proj), (cols[:, 1:2], b_gcn), (cols[:, 2:3], ln1), (cols[:, 3:4], ln2),
            (wg32[:, :], f0_wg), (gbias[:, 0, :], f0_bg.partition_broadcast(P)),
            (gbias[:, 1, :], f0_bias.partition_broadcast(P)), (b2_sb[:, :], f0_b2),
        ]

        def many_entries(eng):
            eng.wait_ge(s_flag, 1)
            return eng.If(eng.value_load(flag[0:1, 0:1], min_val=0, max_val=1) > 0)

        @block.sync
        def _(sp):
            sp.dma_start(x[:, :, :], x_in).then_inc(s_x, 16)
            for j in range(NT):
                sp.dma_start(A[:, j, :], adj_t[j]).then_inc(s_A[j], 16)

            def load_expert0(s, e):
                sp.dma_start(st_w1[:, s, :], f0_w1[bass.ds(e, 1), :, :].rearrange("a p h -> (a p) h")).then_inc(s_ld0[s], 16)
                sp.dma_start(st_w2[:, s, :, :], f0_w2[bass.ds(e, 1), :, :, :].rearrange("a p k d -> (a p) k d")).then_inc(s_ld0[s], 16)
                sp.dma_start(st_b1[:, s, :], f0_b1[bass.ds(e, 1), :, :].rearrange("a p k -> (a p) k")).then_inc(s_ld0[s], 16)

            with many_entries(sp):
                sp.dma_start(a_row, adj_in[0]).then_inc(g_load, 16)
                with sp.Fori(1, NT) as i:
                    sp.wait_ge(g_sq, i)
                    sp.dma_start(a_row, adj_in[bass.ds(i, 1), :, :].rearrange("a p t -> (a p) t")).then_inc(g_load, 16)
                sp.wait_ge(g_mm, 4 * NT + 2)
            sp.wait_ge(s_aggp, NT)
            sp.wait_ge(s_cntp, NT)
            load_expert0(0, 0)
            load_expert0(1, 1)
            with sp.Fori(1, E0 // 2) as i:
                for s in range(2):
                    sp.wait_ge(s_y0, (2 * i + s - 1) * NC + 2)
                    load_expert0(s, 2 * i + s)
            sp.wait_ge(s_add0, E0 * NC + 2)
            for dst, src in ((cos_sb, cos_t), (sin_sb, sin_t)):
                for h in range(NH):
                    sp.dma_start(dst[HD * h:HD * h + HD, :], src).then_inc(s_attw, 16)
            for dst, src in ((wq32, wq), (wk32, wk), (wv32, wv), (wo32, wo), (wr32, w_router)):
                sp.dma_start(dst, src).then_inc(s_attw, 16)

            def load_expert1(s, e):
                sp.dma_start(v13[:, s, 0, :], f1_w1[bass.ds(e, 1), :, :].rearrange("a p h -> (a p) h")).then_inc(s_ld1[s], 16)
                sp.dma_start(v13[:, s, 1, :], f1_w3[bass.ds(e, 1), :, :].rearrange("a p h -> (a p) h")).then_inc(s_ld1[s], 16)
                sp.dma_start(v2[:, s, 0:2, :], f1_w2[bass.ds(e, 1), 0:2 * P, :].rearrange("a (k p) d -> (a p) k d", p=P)
                             ).then_inc(s_ld1[s], 16)
                sp.dma_start(v2[0:KS1[2][1], s, 2, :], f1_w2[bass.ds(e, 1), 2 * P:H1, :].rearrange("a p d -> (a p) d")
                             ).then_inc(s_ld1[s], 16)

            for half in range(2):
                w = slice(2 * CW * half, 2 * CW * half + 2 * CW)
                for done, src, dst, heads, order in ((s_qlo, q16, Qs, NH, (0, 1, 0)), (s_klo, k16, Ks, NKV, (0, 0, 1))):
                    sp.wait_ge(done, 2 * half + 2)
                    for n, part in enumerate(order):
                        for h in range(heads):
                            sp.dma_start(dst[HD * n:HD * n + HD, h, w], src[HD * h:HD * h + HD, part, w]
                                         ).then_inc(s_stack[half], 16)
            load_expert1(0, 0)
            load_expert1(1, 1)
            with sp.Fori(1, E1 // 2) as i:
                for s in range(2):
                    sp.wait_ge(s_y1, (2 * i + s - 1) * NC + 2)
                    load_expert1(s, 2 * i + s)
            for g in range(NC):
                sp.wait_ge(s_add1, (E1 - 1) * NC + g + 1 + 2)
                sp.dma_start(out[:, TPC * g:TPC * g + TPC, :], x[:, TPC * g:TPC * g + TPC, :]).then_inc(s_out, 16)
            sp.wait_ge(s_out, 16 * NC)

        @block.gpsimd
        def _(pool):
            chain = Chain(pool, s_cpool)
            pool.memset(neg_half[:, :], -0.5)
            pool.memset(ones[:, :], 1.0)
            pool.memset(ones_b[:, :], 1.0)
            chain(pool.memset(ident[:, :], 0.0))
            pool.affine_select(out=ident[:, :], in_=ident[:, :], compare_op=ALU.not_equal, fill=1.0, base=0,
                               pattern=[[-1, P]], channel_multiplier=1).then_inc(s_const, 1)
            pool.iota(rev[:, :, :], pattern=[[0, NT], [-1, 8]], base=8, channel_multiplier=0,
                      allow_small_or_imprecise_dtypes=True).then_inc(s_const, 1)

            def inverse_root(n, g):
                pool.wait_ge(s_var, n)
                pool.tensor_tensor(rstd[:, TPC * g:TPC * g + TPC], ve[:, TPC * g:TPC * g + TPC],
                                   neg_half[:, 0:TPC], ALU.pow).then_inc(s_rstd, 1)

            for g in range(NC):
                inverse_root(g + 1, g)
            for g in range(NC):
                inverse_root(NC + g + 1, g)
            pool.wait_ge(s_degv, 1)
            pool.tensor_tensor(dis[:, :], sm[:, 11, :], neg_half[:, :], ALU.pow).then_inc(s_dis, 1)
            pool.wait_ge(s_dis, 1)
            for g in range(NC):
                w = slice(TPC * g, TPC * g + TPC)
                pool.wait_ge(s_var, 2 * NC + g + 1)
                chain(pool.tensor_tensor(rstd[:, w], ve[:, w], neg_half[:, 0:TPC], ALU.pow))
                pool.tensor_tensor(rd[:, w], rstd[:, w], dis[:, w], ALU.mult).then_inc(s_rstd, 1)
            pool.wait_ge(s_agg1, NC)
            chain(pool.memset(mask_ts[:, :], 0.0))
            chain(pool.memset(mask_st[:, :], 0.0))
            chain(pool.affine_select(out=mask_ts[:, :], in_=mask_ts[:, :], compare_op=ALU.is_ge, fill=NEG, base=0,
                                     pattern=[[-1, P]], channel_multiplier=1))
            chain(pool.affine_select(out=mask_st[:, :], in_=mask_st[:, :], compare_op=ALU.is_ge, fill=NEG, base=0,
                                     pattern=[[1, P]], channel_multiplier=-1))
            chain(pool.tensor_copy(ident_b[:, :], ident[:, :]))
            chain(pool.tensor_copy(ident_h[:, :], ident[:, :]))
            pool.memset(Ks[KQ:KQ + 1, :, :], 16.0).then_inc(s_mc, 1)
            pool.wait_ge(s_mc, 1)
            for g in range(NC):
                w = slice(TPC * g, TPC * g + TPC)
                pool.wait_ge(s_var, 3 * NC + g + 1)
                chain(pool.tensor_tensor(rstd[:, w], ve[:, w], neg_half[:, 0:TPC], ALU.pow))
                chain(pool.tensor_tensor(rd[:, w], rstd[:, w], rstd[:, w], ALU.mult))
                chain(pool.tensor_tensor(rd[:, w], rd[:, w], mv[:, w, 1], ALU.mult))
                chain(pool.tensor_scalar(rd[:, w], rd[:, w], EPS_RMS, None, ALU.add))
                chain(pool.tensor_tensor(rd[:, w], rd[:, w], neg_half[:, 0:TPC], ALU.pow))
                pool.tensor_tensor(rd[:, w], rd[:, w], rstd[:, w], ALU.mult).then_inc(s_rstd, 1)
            for g in range(NC):
                w = slice(TPC * g, TPC * g + TPC)
                pool.wait_ge(s_ms, g + 1)
                pool.tensor_tensor(rd[:, w], ve[:, w], neg_half[:, 0:TPC], ALU.pow).then_inc(s_r2, 1)

        @block.scalar
        def _(act):
            for dst, src in small:
                act.dma_start(dst, src).then_inc(s_small, 16)

            for g in range(NC):
                act.wait_ge(s_tr, g + 1)
                act.activation(xT[:, CW * g:CW * g + CW], ps[:, g, :], ACT.Copy).then_inc(s_pre_ev, 1)
            act.wait_ge(s_small, 16 * len(small))
            for g in range(NC):
                act.wait_ge(s_h2p, g + 1)
                act.activation(h2T[:, CW * g:CW * g + CW], ps[:, 4 + g, :], ACT.Tanh, bias=cols[:, 0:1]).then_inc(s_h2, 1)
            for g in range(NC):
                act.wait_ge(s_gp, g + 1)
                act.activation(G[:, TPC * g:TPC * g + TPC, :], ps[:, g, :], ACT.Copy).then_inc(s_G, 1)
            for j in range(NT):
                act.wait_ge(s_sq, j + 1)
                act.activation(fbuf[:, j % FB, :], fbuf[:, j % FB, :], ACT.Tanh).then_inc(s_F, 1)
            with many_entries(act):
                with act.Fori(0, NT) as i:
                    act.wait_ge(g_sq, i + 1)
                    act.activation(f_row, f_row, ACT.Tanh).then_inc(g_tanh, 1)
                    for q in range(4):
                        act.wait_ge(g_tr, 4 * i + q + 1)
                        act.wait_ge(g_mm, 4 * i + q + 1)
                        act.activation(rT[:, q % 2, :], ps[:, 6 + q % 2, :], ACT.Copy).then_inc(g_cp, 1)
                act.wait_ge(g_mm, 4 * NT + 2)
            act.wait_ge(s_aggp, NT)
            for g in range(NC):
                act.activation(xT[:, CW * g:CW * g + CW], ps[:, g, :], ACT.Relu, bias=cols[:, 1:2]).then_inc(s_feat, 1)

            def high_parts(n):
                g = n % NC
                act.wait_ge(s_tr, NC + n + 1)
                act.activation(xh[:, CW * g:CW * g + CW], ps[:, n % 2 + 6, :], ACT.Copy, scale=SX).then_inc(s_xhi, 1)

            for g in range(NC):
                high_parts(g)
            act.wait_ge(s_diff, 1)
            act.activation(sm[:, 3, :], sm[:, 2, :], ACT.Exp).then_inc(s_ediff, 1)

            act.sem_inc(s_relu, 2)

            def relu(i, u):
                s, g, k = u // (NC * K0), u // K0 % NC, u % K0
                act.wait_ge(s_h0, 8 * K0 * i + u + 1)
                act.wait_ge(s_hlo, 8 * K0 * i + u + 1)
                act.activation(h32[:, u % 4, :], ps[:, u % 2, :], ACT.Relu, bias=st_b1[:, s, k:k + 1],
                               scale=1.0 / (SX * SW)).then_inc(s_relu, 1)

            def high(i, u):
                g, k = u // K0, u % K0
                act.wait_ge(s_relu, 8 * K0 * i + u + 1 + 2)
                act.wait_ge(s_y0, 8 * i + g + 1)
                act.activation(hh_hi[:, g % 2, k, :], h32[:, u % 4, :], ACT.Copy, scale=SH).then_inc(s_hhi, 1)

            def turn(i):
                relu(i, 0)
                for u in range(1, 8 * K0):
                    relu(i, u)
                    high(i, u - 1)
                    if isinstance(i, int) and u == 3 * K0:
                        bias2_copy()
                high(i, 8 * K0 - 1)

            def bias2_copy():
                act.wait_ge(s_cT, 1)
                act.activation(combT[:, :], ps[0:8, 4:8, :], ACT.Copy).then_inc(s_cTc, 1)

            with act.Fori(0, E0 // 2 - 1) as i:
                turn(i)
            turn(E0 // 2 - 1)

            def aggregate_copy(c):
                act.wait_ge(s_agg1, c + 1)
                if c >= 2:
                    act.wait_ge(s_z, c - 1)
                act.activation(hagg[:, c % 2, :], ps[:, c, :], ACT.Copy).then_inc(s_hagg, 1)

            def elu_exp(c):
                act.wait_ge(s_zn, c + 1)
                act.activation(ez[:, c % 2, :], ez[:, c % 2, :], ACT.Exp).then_inc(s_ez, 1)

            aggregate_copy(0)
            for c in range(1, NC):
                aggregate_copy(c)
                elu_exp(c - 1)
            elu_exp(NC - 1)

            def high1(n, bank):
                g = n % NC
                act.wait_ge(s_tr1, n + 1)
                act.activation(th[:, CW * g:CW * g + CW], ps[:, bank, :], ACT.Copy, scale=SX).then_inc(s_thi, 1)

            for g in range(NC):
                high1(g, 6 + g % 2)
            for g in range(NC):
                w = slice(CW * g, CW * g + CW)
                act.wait_ge(s_qr, g + 1)
                act.activation(q16[:, 0, w], rope[:, 2, :], ACT.Copy).then_inc(s_qhi, 1)
                act.wait_ge(s_vp, g + 1)
                act.activation(V[:, TPC * g:TPC * g + TPC, :].rearrange("p t d -> p (t d)"), ps[:, 4 + g % 2, 0:TPC * NKV * HD],
                               ACT.Copy, scale=1.0 / (SX * SW)).then_inc(s_V, 1)
                act.wait_ge(s_kr, g + 1)
                act.activation(k16[:, 0, w], rope[0:NKV * HD, 5, :], ACT.Copy).then_inc(s_khi, 1)

            for n, (c, j) in enumerate(steps):
                t0 = max(0, P * (j - TPC * c))
                for pair in range(2):
                    act.wait_ge(s_st, 2 * n + pair + 1)
                    if n >= 2:
                        act.wait_ge(s_pv, n - 1)
                    act.activation(Pb[:, n % 2, 2 * pair:2 * pair + 2, t0:CW], ps[:, 2 * pair:2 * pair + 2, t0:CW], ACT.Exp,
                                   scale=1.0 / (SQ * SQ * float(HD) ** 0.5)).then_inc(s_p, 1)
                if last_step(c, j):
                    act.wait_ge(s_pv, n + 1)
                    act.activation(o_sb, ps[:, 6, :], ACT.Copy).then_inc(s_od, 1)

            for g in range(NC):
                high1(NC + g, g % 2)
            act.wait_ge(s_rl, 1)
            act.activation(lg1[:, 2], lg1[:, 1], ACT.Exp).then_inc(s_re, 1)

            act.sem_inc(s_silu, 2)

            def silu(i, u):
                k = u % 3
                rows = KS1[k][1]
                act.wait_ge(s_h1, 24 * i + u + 1)
                act.wait_ge(s_hh, 24 * i + u + 1)
                act.activation(silu_sb[0:rows, u % 2, :], ps[0:rows, u % 2, :], ACT.Silu, scale=1.0 / (SX * SW)).then_inc(s_silu, 1)

            def high_hidden(i, u):
                gg, k = u // 3, u % 3
                rows = KS1[k][1]
                act.wait_ge(s_hh, 24 * i + u + 1 + 2)
                act.wait_ge(s_y1, 8 * i + gg + 1)
                act.activation(g_hi[0:rows, gg % 2, k, :], g32[0:rows, u % 4, :], ACT.Copy).then_inc(s_ghi, 1)

            def turn1(i):
                silu(i, 0)
                for u in range(1, 24):
                    silu(i, u)
                    high_hidden(i, u - 1)
                high_hidden(i, 23)

            with act.Fori(0, E1 // 2 - 1) as i:
                turn1(i)
            turn1(E1 // 2 - 1)

        @block.tensor
        def _(pe):
            def transpose_rows(g, bank):
                for q in range(TPC):
                    last = pe.transpose(ps[:, bank, P * q:P * q + P], xn[:, TPC * g + q, :], ident[:, :])
                last.then_inc(s_tr, 1)

            def row_sums(j):
                for c in range(NC):
                    last = pe.matmul(ps[32 * c:32 * c + 32, 5, :], ones[:, :], A[:, j, CW * c:CW * c + CW],
                                     start=(j == 0), stop=(j == NT - 1))
                return last

            pe.wait_ge(s_const, 1)
            for g in range(NC):
                pe.wait_ge(s_xn, g + 1)
                transpose_rows(g, g)
            pe.wait_ge(s_small, 16 * len(small))
            for g in range(NC):
                pe.wait_ge(s_pre_ev, g + 1)
                pe.matmul(ps[:, 4 + g, :], wmat[:, 0, :], xT[:, CW * g:CW * g + CW], start=True, stop=True).then_inc(s_h2p, 1)
            for g in range(NC):
                pe.wait_ge(s_h2, g + 1)
                for q in range(TPC):
                    t = TPC * g + q
                    last = pe.matmul(ps[:, g, P * q:P * q + P], h2T[:, P * t:P * t + P], wmat[:, 1, :], start=True, stop=True)
                last.then_inc(s_gp, 1)
            for j in range(NT):
                pe.wait_ge(s_A[j], 16)
                deg = row_sums(j)
                if j == NT - 1:
                    deg.then_inc(s_degp, 1)
                if j == 0:
                    pe.wait_ge(s_G, NC)
                pe.wait_ge(s_F, j + 1)
                for c in range(NC):
                    last = pe.matmul(ps[:, c, :], G[:, j, :], fbuf[:, j % FB, CW * c:CW * c + CW],
                                     start=(j == 0), stop=(j == NT - 1))
                last.then_inc(s_aggp, 1)
                pe.wait_ge(s_mask, j + 1)
                for c in range(NC):
                    last = pe.matmul(ps[32 * c:32 * c + 32, 4, :], ones_b[:, :], mbuf[:, j % 2, CW * c:CW * c + CW],
                                     start=(j == 0), stop=(j == NT - 1))
                last.then_inc(s_cntp, 1)
            pe.wait_ge(s_cmax, 1)
            pe.transpose(ps[0:1, 6, 0:P], cnt[:, 0:1], ident[:, :]).then_inc(s_cmT, 1)
            with many_entries(pe):
                pe.sem_inc(g_mm, 2)
                pe.wait_ge(s_G, NC)
                agg = ps[:, 0:NC, :].rearrange("p c t -> p (c t)")
                with pe.Fori(0, NT) as i:
                    pe.wait_ge(g_row, i + 1)
                    for q in range(4):
                        for t in range(4 * q, 4 * q + 4):
                            last = pe.transpose(ps[:, 6 + q % 2, P * (t % 4):P * (t % 4) + P], e_row[:, P * t:P * t + P], ident[:, :])
                        last.then_inc(g_tr, 1)
                        pe.wait_ge(g_cp, 4 * i + q + 1)
                        for t in range(4 * q, 4 * q + 4):
                            last = pe.matmul(agg[:, bass.ds(P * i, P)], G[:, t, :], rT[:, q % 2, P * (t % 4):P * (t % 4) + P],
                                             start=(t == 0), stop=(t == NT - 1))
                        last.then_inc(g_mm, 1)
            for g in range(NC):
                pe.wait_ge(s_feat, g + 1)
                if g == 0:
                    pe.wait_ge(s_flag, 1)
                if g >= 2:
                    pe.wait_ge(s_x1, g - 1)
                for q in range(TPC):
                    t = TPC * g + q
                    last = pe.transpose(ps[:, 6 + g % 2, P * q:P * q + P], xT[:, P * t:P * t + P], ident[:, :])
                last.then_inc(s_ftr, 1)
            pe.wait_ge(s_degrow, 1)
            for t in range(NT):
                c, q = t // TPC, t % TPC
                last = pe.matmul(ps[:, c, q:q + 1], deg_row[32 * c:32 * c + 1, P * q:P * q + P],
                                 ones[32 * c:32 * c + 1, 0:1], start=True, stop=True)
            last.then_inc(s_degc, 1)

            for g in range(NC):
                pe.wait_ge(s_xn, NC + g + 1)
                if g >= 2:
                    pe.wait_ge(s_xlo, g - 1)
                else:
                    pe.wait_ge(s_x1, NC)
                transpose_rows(g, 6 + g % 2)
            pe.wait_ge(s_wg, 1)
            for t in range(NT):
                if t % TPC == 0:
                    pe.wait_ge(s_xlo, t // TPC + 1)
                for n, (a, b) in enumerate(((xh, 0), (xl, 0), (xh, 1))):
                    last = pe.matmul(ps[:, 4, 8 * t:8 * t + 8], a[:, P * t:P * t + P], wg16[:, b, :], start=(n == 0), stop=(n == 2))
            last.then_inc(s_gate, 1)

            pe.sem_inc(s_y0, 2)

            def hidden(i, gg):
                s, g = gg // NC, gg % NC
                if g == 0:
                    pe.wait_ge(s_w0, 2 * i + s + 1)
                for k in range(K0):
                    u = gg * K0 + k
                    pe.wait_ge(s_relu, 8 * K0 * i + u + 1)
                    for n, (w, a) in enumerate(((w1h, xh), (w1h, xl), (w1l, xh))):
                        last = pe.matmul(ps[:, u % 2, :], w[:, s, P * k:P * k + P], a[:, CW * g:CW * g + CW],
                                         start=(n == 0), stop=(n == 2))
                    last.then_inc(s_h0, 1)

            def output(i, gg):
                s = gg // NC
                pe.wait_ge(s_hlo, 8 * K0 * i + (gg + 1) * K0 + 4)
                pe.wait_ge(s_add0, 8 * i + gg + 1)
                for q in range(TPC):
                    n = 0
                    for k in range(K0):
                        for a, w in ((hh_hi, w2h), (hh_hi, w2l), (hh_lo, w2h)):
                            last = pe.matmul(ps[:, 2 + gg % 2, P * q:P * q + P], a[:, gg % 2, k, P * q:P * q + P],
                                             w[:, s, k, :], start=(n == 0), stop=(n == 3 * K0 - 1))
                            n += 1
                last.then_inc(s_y0, 1)

            def bias2_transpose():
                pe.wait_ge(s_comb, 1)
                for t in range(NT):
                    last = pe.transpose(ps[0:8, 4 + t // TPC, P * (t % TPC):P * (t % TPC) + P], comb[:, t, :], ident[:, :])
                last.then_inc(s_cT, 1)

            def bias2_product():
                pe.wait_ge(s_cTc, 1)
                for t in range(NT):
                    last = pe.matmul(ps[:, 4 + t // TPC, P * (t % TPC):P * (t % TPC) + P], combT[:, P * t:P * t + P],
                                     b2_sb[:, :], start=True, stop=True)
                last.then_inc(s_b2, 1)

            def turn(i):
                for gg in range(2 * NC):
                    hidden(i, gg)
                    if gg:
                        output(i, gg - 1)
                    if isinstance(i, int) and gg == 2:
                        bias2_transpose()
                    if isinstance(i, int) and gg == 3:
                        bias2_product()
                output(i, 2 * NC - 1)

            with pe.Fori(0, E0 // 2 - 1) as i:
                turn(i)
            turn(E0 // 2 - 1)

            def aggregate(c):
                if c == 0:
                    pe.wait_ge(s_xn, 3 * NC)
                for j in range(NT):
                    if j // TPC == c:
                        q = j % TPC
                        pe.matmul(ps[:, c, P * q:P * q + P], G[:, j, :], ident[:, :], start=(j == 0), stop=False,
                                  skip_group_check=True)
                    last = pe.matmul(ps[:, c, :], G[:, j, :], A[:, j, CW * c:CW * c + CW],
                                     start=(j == 0 and c > 0), stop=(j == NT - 1), skip_group_check=True)
                last.then_inc(s_agg1, 1)

            def times_w(c):
                pe.wait_ge(s_hagg, c + 1)
                if c >= 2:
                    pe.wait_ge(s_x3, c - 1)
                for q in range(TPC):
                    last = pe.matmul(ps[:, 4 + c % 2, P * q:P * q + P], hagg[:, c % 2, P * q:P * q + P], wmat[:, 2, :],
                                     start=True, stop=True)
                last.then_inc(s_z, 1)

            aggregate(0)
            for c in range(1, NC):
                aggregate(c)
                times_w(c - 1)
            times_w(NC - 1)

            for g in range(NC):
                pe.wait_ge(s_hn, g + 1)
                if g >= 2:
                    pe.wait_ge(s_tlo, g - 1)
                for q in range(TPC):
                    last = pe.transpose(ps[:, 6 + g % 2, P * q:P * q + P], G[:, TPC * g + q, :], ident[:, :])
                last.then_inc(s_tr1, 1)

            def product3(dst, w0, w1, g):
                for n, (b, a) in enumerate(((0, th), (0, tl), (1, th))):
                    last = pe.matmul(dst, watt[:, b, w0:w1], a[:, CW * g:CW * g + CW], start=(n == 0), stop=(n == 2))
                return last

            pe.wait_ge(s_attws, 1)
            for g in range(NC):
                pe.wait_ge(s_tlo, g + 1)
                if g:
                    pe.wait_ge(s_qr, g)
                product3(ps[:, 0, :], WQ, WQR, g)
                product3(ps[:, 1, :], WQR, WK, g).then_inc(s_qp, 1)
                if g:
                    pe.wait_ge(s_kr, g)
                product3(ps[0:NKV * HD, 2, :], WK, WKR, g)
                product3(ps[0:NKV * HD, 3, :], WKR, WV, g).then_inc(s_kp, 1)
                if g >= 2:
                    pe.wait_ge(s_V, g - 1)
                for q in range(TPC):
                    t = TPC * g + q
                    for n, (a, b) in enumerate(((th, 0), (tl, 0), (th, 1))):
                        last = pe.matmul(ps[:, 4 + g % 2, NKV * HD * q:NKV * HD * (q + 1)], a[:, P * t:P * t + P],
                                         watt[:, b, WV:WR], start=(n == 0), stop=(n == 2))
                last.then_inc(s_vp, 1)

            filled = [0]

            def unit(what):
                n = filled[0]
                bank = 4 + n % 2
                if n >= 2:
                    pe.wait_ge(s_rmf, n - 1)
                if what[0] == "max":
                    _, t, h, b = what
                    if (t, h, b) == (2 * TPC, 0, 0):
                        pe.wait_ge(s_stack[1], 16 * 3 * (NH + NKV))
                    diagonal = b == t // TPC
                    width = P * (t % TPC + 1) if diagonal else CW
                    if diagonal:
                        pe.matmul(ps[:, bank, width - P:width], ident_b[:, :], mask_ts[:, :], start=True, stop=False,
                                  skip_group_check=True)
                    last = pe.matmul(ps[:, bank, 0:width], Qs[0:KQ, h, P * t:P * t + P],
                                     Ks[0:KQ, h // (NH // NKV), CW * b:CW * b + width], start=not diagonal, stop=True,
                                     skip_group_check=True)
                elif what[0] == "neg":
                    _, c, h = what
                    pe.wait_ge(s_m, c + 1)
                    for q in range(TPC):
                        last = pe.matmul(ps[KQ:KQ + 1, bank, P * q:P * q + P], m16[:, h, q:q + 1], ident_h[:, :],
                                         start=True, stop=True)
                else:
                    c = what[1]
                    pe.wait_ge(s_yT, c + 1)
                    for q in range(TPC):
                        t = TPC * c + q
                        last = pe.matmul(ps[:, bank, P * q:P * q + P], yT[:, P * t:P * t + P], wo32, start=True, stop=True)
                last.then_inc(s_rm, 1)
                filled[0] += 1

            def scores(n):
                c, j = steps[n]
                k = j - TPC * c
                t0 = max(0, P * k)
                if first_step(c, j):
                    pe.wait_ge(s_rmf, neg_done[c])
                for h in range(NH):
                    if h % 2 == 0 and n:
                        pe.wait_ge(s_p, 2 * (n - 1) + h // 2 + 1)
                    if k >= 0:
                        pe.matmul(ps[:, h, t0:t0 + P], ident_b[:, :], mask_st[:, :], start=True, stop=False,
                                  skip_group_check=True)
                    last = pe.matmul(ps[:, h, t0:CW], Ks[0:KQ + 1, h // (NH // NKV), P * j:P * j + P],
                                     Qs[0:KQ + 1, h, CW * c + t0:CW * c + CW], start=k < 0, stop=True, skip_group_check=True)
                    if h % 2:
                        last.then_inc(s_st, 1)

            def weigh(n):
                c, j = steps[n]
                t0 = max(0, P * (j - TPC * c))
                pe.wait_ge(s_p, 2 * n + 2)
                if first_step(c, j) and c:
                    pe.wait_ge(s_od, 2 * c)
                for bank in (6, 7):
                    for h in range(NH):
                        kv = h // (NH // NKV)
                        w = V[:, j, HD * kv:HD * kv + HD] if bank == 6 else ones[:, :]
                        last = pe.matmul(ps[HD * h:HD * h + HD, bank, t0:CW], w, Pb[:, n % 2, h, t0:CW],
                                         start=first_step(c, j), stop=last_step(c, j), skip_group_check=True)
                last.then_inc(s_pv, 1)

            pe.wait_ge(s_V, NC)
            pe.wait_ge(s_stack[0], 16 * 3 * (NH + NKV))
            pe.wait_ge(s_mc, 1)
            for what in max_units(0):
                unit(what)
            scores(0)
            for n, step in enumerate(steps):
                for what in units_at[step]:
                    unit(what)
                if n + 1 < len(steps):
                    scores(n + 1)
                weigh(n)
            unit(("out", NC - 1))

            for g in range(NC):
                pe.wait_ge(s_fn, g + 1)
                if g >= 2:
                    pe.wait_ge(s_tlo, NC + g - 1)
                for q in range(TPC):
                    last = pe.transpose(ps[:, g % 2, P * q:P * q + P], G[:, TPC * g + q, :], ident[:, :])
                last.then_inc(s_tr1, 1)
            for t in range(NT):
                if t % TPC == 0:
                    pe.wait_ge(s_tlo, NC + t // TPC + 1)
                for n, (a, b) in enumerate(((th, 0), (tl, 0), (th, 1))):
                    last = pe.matmul(ps[:, 6, 8 * t:8 * t + 8], a[:, P * t:P * t + P], watt[:, b, WR:WR + 8],
                                     start=(n == 0), stop=(n == 2))
            last.then_inc(s_rt, 1)

            pe.sem_inc(s_y1, 2)

            def hidden1(i, gg):
                s, g = gg // NC, gg % NC
                if g == 0:
                    pe.wait_ge(s_w1, 2 * i + s + 1)
                for k, (k0, rows) in enumerate(KS1):
                    u = 3 * gg + k
                    for m, (free, ready) in enumerate(((s_silu, s_h1), (s_hh, s_h3))):
                        pe.wait_ge(free, 24 * i + u + 1)
                        for n, (w, a) in enumerate(((v13h, th), (v13h, tl), (v13l, th))):
                            last = pe.matmul(ps[0:rows, 2 * m + u % 2, :], w[:, s, m, k0:k0 + rows], a[:, CW * g:CW * g + CW],
                                             start=(n == 0), stop=(n == 2))
                        last.then_inc(ready, 1)

            def output1(i, gg):
                s = gg // NC
                pe.wait_ge(s_glo, 24 * i + 3 * (gg + 1) + 4)
                pe.wait_ge(s_add1, 8 * i + gg + 1)
                for q in range(TPC):
                    n = 0
                    for k, (_, rows) in enumerate(KS1):
                        for a, w in ((g_hi, v2h), (g_hi, v2l), (g_lo, v2h)):
                            last = pe.matmul(ps[:, 4 + gg % 2, P * q:P * q + P], a[0:rows, gg % 2, k, P * q:P * q + P],
                                             w[0:rows, s, k, :], start=(n == 0), stop=(n == 8))
                            n += 1
                last.then_inc(s_y1, 1)

            def turn1(i):
                for gg in range(2 * NC):
                    hidden1(i, gg)
                    if gg:
                        output1(i, gg - 1)
                output1(i, 2 * NC - 1)

            with pe.Fori(0, E1 // 2 - 1) as i:
                turn1(i)
            turn1(E1 // 2 - 1)

        @block.vector
        def _(dve):
            chain = Chain(dve, s_dve)

            def statistics(g, src):
                for t in range(TPC * g, TPC * g + TPC):
                    last = dve.bn_stats(bst[:, t, :], src[:, t, :])
                chain(last)
                for t in range(TPC * g, TPC * g + TPC):
                    last = dve.bn_aggr(mv[:, t, :], bst[:, t, :])
                chain(last)
                dve.tensor_scalar(ve[:, TPC * g:TPC * g + TPC], mv[:, TPC * g:TPC * g + TPC, 1], EPS_LN, None,
                                  ALU.add).then_inc(s_var, 1)

            def normalise(n, g, src, dst):
                dve.wait_ge(s_rstd, n)
                for t in range(TPC * g, TPC * g + TPC):
                    last = dve.tensor_scalar(dst[:, t, :], src[:, t, :], mv[:, t, 0:1], rstd[:, t:t + 1], ALU.subtract, ALU.mult)
                last.then_inc(s_xn, 1)

            dve.wait_ge(s_x, 16)
            for g in range(NC):
                statistics(g, x)
            for g in range(NC):
                normalise(g + 1, g, x, xn)

            def square(j):
                dve.wait_ge(s_A[j], 16)
                if j >= FB:
                    dve.wait_ge(s_aggp, j - FB + 1)
                    dve.wait_ge(s_mask, j - FB + 1)
                dve.scalar_tensor_tensor(out=fbuf[:, j % FB, :], in0=A[:, j, :], scalar=0.0, in1=A[:, j, :],
                                         op0=ALU.max, op1=ALU.mult).then_inc(s_sq, 1)

            def mask(j):
                dve.wait_ge(s_F, j + 1)
                if j >= 2:
                    dve.wait_ge(s_cntp, j - 1)
                dve.tensor_scalar(mbuf[:, j % 2, :], fbuf[:, j % FB, :], 0.0, None, ALU.is_gt).then_inc(s_mask, 1)

            for j in range(NT):
                square(j)
                if j:
                    mask(j - 1)
            mask(NT - 1)
            dve.wait_ge(s_cntp, NT)
            dve.reduce_max(cnt[:, 0:1], ps[:, 4, :], AX_X).then_inc(s_cmax, 1)
            dve.wait_ge(s_cmT, 1)
            chain(dve.reduce_max(cnt[0:1, 1:2], ps[0:1, 6, 0:P], AX_X))
            dve.tensor_scalar(flag[:, :], cnt[0:1, 1:2], float(LIMIT), None, ALU.is_gt).then_inc(s_flag, 1)
            with many_entries(dve):
                W = 8
                B = 5
                step = Chain(dve, s_gen)
                with dve.Fori(0, NT) as i:
                    step.turn(i, W + 31 * B)
                    dve.wait_ge(g_load, 16 * i + 16)
                    dve.scalar_tensor_tensor(out=f_row, in0=a_row, scalar=0.0, in1=a_row, op0=ALU.max, op1=ALU.mult).then_inc(g_sq, 1)
                    step(dve.memset(thr, 0))
                    dve.wait_ge(g_tanh, i + 1)
                    dve.memset(bit, 1 << 30).then_inc(s_gen, 1)
                    step.here += 1
                    with dve.Fori(0, 31) as b:
                        step.base = i * (W + 31 * B) + b * B
                        dve.wait_ge(s_gen, step.base + step.here)
                        step(dve.tensor_tensor(cand, thr, bit, ALU.bitwise_or))
                        step(dve.tensor_scalar(c_row, f_row, cand_f, 0.0, ALU.is_ge, ALU.add, accum_out=cnt_f))
                        step(dve.tensor_scalar(ge, cnt_f, float(TOP), -1.0, ALU.is_ge, ALU.mult))
                        step(dve.tensor_tensor(ge, ge, bit, ALU.bitwise_and))
                        dve.tensor_scalar(bit, bit, 1, None, ALU.logical_shift_right)
                        step(dve.tensor_tensor(thr, thr, ge, ALU.bitwise_or))
                    step.here -= B
                    step.base = i * (W + 31 * B) + 31 * B
                    step(dve.tensor_scalar(c_row, f_row, thr_f, 0.0, ALU.is_gt, ALU.add, accum_out=cnt_f))
                    step(dve.tensor_scalar(need_f, cnt_f, -1.0, float(TOP), ALU.mult, ALU.add))
                    step(dve.tensor_scalar(c_row, f_row, thr_f, None, ALU.is_equal))
                    dve.wait_ge(g_mm, 4 * i + 2)
                    step(dve.tensor_tensor_scan(e_row, c_row, c_row, 0.0, ALU.add, ALU.max))
                    step(dve.scalar_tensor_tensor(out=c_row, in0=e_row, scalar=need_f, in1=c_row, op0=ALU.is_le, op1=ALU.mult))
                    step(dve.scalar_tensor_tensor(out=c_row, in0=f_row, scalar=thr_f, in1=c_row, op0=ALU.is_gt, op1=ALU.add))
                    dve.tensor_tensor(e_row, f_row, c_row, ALU.mult).then_inc(g_row, 1)
                    dve.wait_ge(g_row, i + 1)
                    step.turn_ends(W)
            for g in range(NC):
                dve.wait_ge(s_ftr, g + 1)
                dve.tensor_tensor(x[:, TPC * g:TPC * g + TPC, :].rearrange("p a d -> p (a d)"), ps[:, 6 + g % 2, :],
                                  x[:, TPC * g:TPC * g + TPC, :].rearrange("p a d -> p (a d)"), ALU.add).then_inc(s_x1, 1)
                dve.wait_ge(s_x1, g + 1)
                statistics(g, x)
            dve.wait_ge(s_degp, 1)
            dve.tensor_copy(deg_row[:, :], ps[:, 5, :]).then_inc(s_degrow, 1)
            for g in range(NC):
                normalise(NC + g + 1, g, x, xn)
            dve.wait_ge(s_degc, 1)
            dve.tensor_scalar(sm[:, 11, :].rearrange("p (c q) -> p c q", c=NC), ps[:, 0:NC, 0:TPC], 1.0, None, ALU.add).then_inc(s_degv, 1)

            def low_parts(n):
                g = n % NC
                dve.wait_ge(s_xhi, n + 1)
                dve.scalar_tensor_tensor(out=xl[:, CW * g:CW * g + CW], in0=ps[:, n % 2 + 6, :], scalar=SX,
                                         in1=xh[:, CW * g:CW * g + CW], op0=ALU.mult, op1=ALU.subtract).then_inc(s_xlo, 1)

            def split(hi, lo, src, scale):
                chain(dve.tensor_scalar(hi, src, scale, None, ALU.mult))
                return dve.scalar_tensor_tensor(out=lo, in0=src, scalar=scale, in1=hi, op0=ALU.mult, op1=ALU.subtract)

            def split_expert0(s, count):
                dve.wait_ge(s_ld0[s], 48 * count)
                split(w2h[:, s], w2l[:, s], st_w2[:, s], SW)
                split(w1h[:, s], w1l[:, s], st_w1[:, s], SW).then_inc(s_w0, 1)

            dve.wait_ge(s_small, 16 * len(small))
            split(wg16[:, 0, :], wg16[:, 1, :], wg32[:, :], SW).then_inc(s_wg, 1)
            for g in range(NC):
                low_parts(g)
            split_expert0(0, 1)

            def top2(L, lg):
                eq, key, m, km = lg[:, 1], lg[:, 2], sm[:, 4], sm[:, 5]
                bc = lambda v: v.unsqueeze(2).broadcast_to([P, NT, 8])
                for n, (value, hot) in enumerate(((sm[:, 0], lg[:, 3]), (sm[:, 1], lg[:, 4]))):
                    chain(dve.reduce_max(value, L, AX_X))
                    chain(dve.tensor_tensor(eq, L, bc(value), ALU.is_equal))
                    chain(dve.tensor_tensor(key, eq, rev[:, :, :], ALU.mult))
                    chain(dve.reduce_max(km, key, AX_X))
                    chain(dve.tensor_tensor(hot, key, bc(km), ALU.is_equal))
                    if n == 0:
                        chain(dve.scalar_tensor_tensor(out=lg[:, 5], in0=hot, scalar=NEG, in1=L, op0=ALU.mult, op1=ALU.add))
                        L = lg[:, 5]

            def combine_weights(w1, w2, lg):
                bc = lambda v: v.unsqueeze(2).broadcast_to([P, NT, 8])
                chain(dve.tensor_tensor(lg[:, 6], lg[:, 3], bc(w1), ALU.mult))
                chain(dve.tensor_tensor(lg[:, 7], lg[:, 4], bc(w2), ALU.mult))
                return dve.tensor_tensor(comb[:, :, :], lg[:, 6], lg[:, 7], ALU.add)

            dve.wait_ge(s_const, 2)
            dve.wait_ge(s_gate, 1)
            chain(dve.tensor_tensor(lg[:, 8, 0, :], gbias[:, 0, :], gbias[:, 1, :], ALU.add))
            chain(dve.scalar_tensor_tensor(out=lg[:, 0], in0=ps[:, 4, 0:8 * NT].rearrange("p (t e) -> p t e", e=8),
                                           scalar=1.0 / (SX * SW),
                                           in1=lg[:, 8, 0, :].unsqueeze(1).broadcast_to([P, NT, 8]), op0=ALU.mult, op1=ALU.add))
            top2(lg[:, 0], lg)
            dve.tensor_tensor(sm[:, 2], sm[:, 1], sm[:, 0], ALU.subtract).then_inc(s_diff, 1)
            dve.wait_ge(s_ediff, 1)
            chain(dve.tensor_scalar(sm[:, 6], sm[:, 3], 1.0, None, ALU.add))
            chain(dve.reciprocal(sm[:, 7], sm[:, 6]))
            chain(dve.tensor_tensor(sm[:, 8], sm[:, 3], sm[:, 7], ALU.mult))
            combine_weights(sm[:, 7], sm[:, 8], lg).then_inc(s_comb, 1)
            dve.wait_ge(s_comb, 1)

            dve.sem_inc(s_hlo, 4)
            dve.sem_inc(s_add0, 2)

            def low(i, u):
                g, k = u // K0, u % K0
                dve.wait_ge(s_hhi, 8 * K0 * i + u + 1)
                dve.scalar_tensor_tensor(out=hh_lo[:, g % 2, k, :], in0=h32[:, u % 4, :], scalar=SH,
                                         in1=hh_hi[:, g % 2, k, :], op0=ALU.mult, op1=ALU.subtract).then_inc(s_hlo, 1)

            def add(i, gg):
                s, g = gg // NC, gg % NC
                dve.wait_ge(s_y0, 8 * i + gg + 1 + 2)
                if gg:
                    dve.wait_ge(s_add0, 8 * i + gg + 2)
                for q in range(TPC):
                    t = TPC * g + q
                    last = dve.scalar_tensor_tensor(out=x[:, t, :], in0=ps[:, 2 + gg % 2, P * q:P * q + P],
                                                    scalar=wcol[:, s, t:t + 1], in1=x[:, t, :], op0=ALU.mult, op1=ALU.add)
                last.then_inc(s_add0, 1)

            wcol = sm[:, 9:11, :]

            def turn(i, last):
                for s in range(2):
                    chain(dve.tensor_scalar(wcol[:, s, :], comb[:, :, bass.ds(2 * i + s, 1)].rearrange("p t a -> p (t a)"),
                                            1.0 / (SH * SW), None, ALU.mult))
                    for g in range(NC):
                        gg = NC * s + g
                        for k in range(K0):
                            low(i, gg * K0 + k)
                        if gg:
                            add(i, gg - 1)
                            if last and gg > NC:
                                statistics_of_gnn1(gg - 1 - NC)
                        if last and gg == 4:
                            dve.wait_ge(s_b2, 1)
                            dve.wait_ge(s_add0, 8 * i + gg + 2)
                            dve.tensor_tensor(x[:, :, :].rearrange("p t d -> p (t d)"), ps[:, 4:8, :].rearrange("p c t -> p (c t)"),
                                              x[:, :, :].rearrange("p t d -> p (t d)"), ALU.add).then_inc(s_x1, 1)
                            dve.wait_ge(s_x1, NC + 1)
                        if g == 1 and not (last and s == 1):
                            split_expert0(1 - s, i + 1 + s)
                add(i, 2 * NC - 1)
                if last:
                    statistics_of_gnn1(NC - 1)

            def statistics_of_gnn1(g):
                dve.wait_ge(s_add0, (E0 - 1) * NC + g + 1 + 2)
                statistics(g, x)

            per = 2 * 3
            with dve.Fori(0, E0 // 2 - 1) as i:
                chain.turn(i, per)
                turn(i, False)
                chain.turn_ends(per)
            chain.loop_ends(E0 // 2 - 1, per)
            turn(E0 // 2 - 1, True)

            for g in range(NC):
                dve.wait_ge(s_rstd, 2 * NC + g + 1)
                for t in range(TPC * g, TPC * g + TPC):
                    last = dve.tensor_scalar(G[:, t, :], x[:, t, :], mv[:, t, 0:1], rd[:, t:t + 1], ALU.subtract, ALU.mult)
                last.then_inc(s_xn, 1)

            def rows(v, g):
                return v[:, TPC * g:TPC * g + TPC, :].rearrange("p a d -> p (a d)")

            dve.wait_ge(s_attw, 16 * (2 * NH + 5))
            for src, ln, a, b in ((wq32, 2, WQ, WQR), (wk32, 2, WK, WKR), (wv32, 2, WV, WR), (wr32, 3, WR, WR + 8)):
                chain(dve.tensor_scalar(src, src, cols[:, ln:ln + 1], SW, ALU.mult, ALU.mult))
                chain(split(watt[:, 0, a:b], watt[:, 1, a:b], src, 1.0))
            for part in range(2):
                for a, b, n in ((WQ, WQR, NH), (WK, WKR, NKV)):
                    w = HD * n
                    src = watt[:, part, a:a + w].rearrange("p (h s d) -> p h s d", h=n, s=2)
                    dst = watt[:, part, b:b + w].rearrange("p (h s d) -> p h s d", h=n, s=2)
                    dve.tensor_scalar(dst[:, :, 0, :], src[:, :, 1, :], -1.0, None, ALU.mult)
                    last = dve.tensor_copy(dst[:, :, 1, :], src[:, :, 0, :])
            last.then_inc(s_attws, 1)

            for c in range(NC):
                dve.wait_ge(s_z, c + 1)
                if c >= 2:
                    dve.wait_ge(s_x3, c - 1)
                for q in range(TPC):
                    t = TPC * c + q
                    last = dve.tensor_scalar(zs[:, c % 2, P * q:P * q + P], ps[:, 4 + c % 2, P * q:P * q + P], dis[:, t:t + 1],
                                             None, ALU.mult)
                chain(last)
                if c >= 2:
                    dve.wait_ge(s_ez, c - 1)
                dve.tensor_scalar(ez[:, c % 2, :], zs[:, c % 2, :], 0.0, None, ALU.min).then_inc(s_zn, 1)
                chain(dve.scalar_tensor_tensor(out=rows(x, c), in0=zs[:, c % 2, :], scalar=0.0, in1=rows(x, c), op0=ALU.max, op1=ALU.add))
                dve.wait_ge(s_ez, c + 1)
                dve.scalar_tensor_tensor(out=rows(x, c), in0=ez[:, c % 2, :], scalar=-1.0, in1=rows(x, c), op0=ALU.add,
                                         op1=ALU.add).then_inc(s_x3, 1)
                dve.wait_ge(s_x3, c + 1)
                statistics(c, x)

            for g in range(NC):
                normalise(3 * NC + g + 1, g, x, xn)
                for t in range(TPC * g, TPC * g + TPC):
                    last = dve.tensor_scalar(G[:, t, :], x[:, t, :], mv[:, t, 0:1], rd[:, t:t + 1], ALU.subtract, ALU.mult)
                last.then_inc(s_hn, 1)

            def low1(n, bank):
                g = n % NC
                dve.wait_ge(s_thi, n + 1)
                dve.scalar_tensor_tensor(out=tl[:, CW * g:CW * g + CW], in0=ps[:, bank, :], scalar=SX,
                                         in1=th[:, CW * g:CW * g + CW], op0=ALU.mult, op1=ALU.subtract).then_inc(s_tlo, 1)

            for g in range(NC):
                low1(g, 6 + g % 2)
            for g in range(NC):
                w = slice(CW * g, CW * g + CW)
                for (bank, parts, b0, ready, done, hi_done, lo_done, dst) in (
                        (0, P, 0, s_qp, s_qr, s_qhi, s_qlo, q16), (2, NKV * HD, 3, s_kp, s_kr, s_khi, s_klo, k16)):
                    dve.wait_ge(ready, g + 1)
                    for n, table in enumerate((cos_sb, sin_sb)):
                        last = dve.scalar_tensor_tensor(out=rope[0:parts, b0 + n, :], in0=ps[0:parts, bank + n, :],
                                                        scalar=SQ / (SX * SW), in1=table[0:parts, w], op0=ALU.mult, op1=ALU.mult)
                    chain(last)
                    dve.tensor_tensor(rope[0:parts, b0 + 2, :], rope[0:parts, b0, :], rope[0:parts, b0 + 1, :],
                                      ALU.add).then_inc(done, 1)
                for (parts, b0, hi_done, lo_done, dst) in ((P, 0, s_qhi, s_qlo, q16), (NKV * HD, 3, s_khi, s_klo, k16)):
                    dve.wait_ge(hi_done, g + 1)
                    dve.tensor_tensor(dst[:, 1, w], rope[0:parts, b0 + 2, :], dst[:, 0, w], ALU.subtract).then_inc(lo_done, 1)
                dve.wait_ge(s_klo, g + 1)

            read = [0]

            def unit(what):
                n = read[0]
                bank = 4 + n % 2
                dve.wait_ge(s_rm, n + 1)
                if what[0] == "max":
                    _, t, h, b = what
                    width = P * (t % TPC + 1) if b == t // TPC else CW
                    dve.reduce_max(pm[:, h, t % TPC, b:b + 1], ps[:, bank, 0:width], AX_X).then_inc(s_rmf, 1)
                elif what[0] == "neg":
                    _, c, h = what
                    dve.tensor_copy(Qs[KQ:KQ + 1, h, CW * c:CW * c + CW], ps[KQ:KQ + 1, bank, :]).then_inc(s_rmf, 1)
                else:
                    c = what[1]
                    dve.tensor_tensor(rows(xn, c), ps[:, bank, :], rows(xn, c), ALU.add).then_inc(s_rmf, 1)
                read[0] += 1
                last_max = ("max", what[1], NH - 1, what[1] // TPC) if what[0] == "max" else None
                if what == last_max and what[1] % TPC == TPC - 1:
                    c = what[1] // TPC
                    dve.wait_ge(s_rmf, n + 1)
                    chain(dve.reduce_max(m32[:, :, :], pm[:, :, :, 0:c + 1], AX_X))
                    dve.tensor_scalar(m16[:, :, :], m32[:, :, :], -1.0 / 16.0, None, ALU.mult).then_inc(s_m, 1)
                    dve.wait_ge(s_m, c + 1)

            for what in max_units(0):
                unit(what)
            for n, (c, j) in enumerate(steps):
                for what in units_at[(c, j)]:
                    unit(what)
                if last_step(c, j):
                    dve.wait_ge(s_pv, n + 1)
                    dve.tensor_copy(d_sb, ps[:, 7, :]).then_inc(s_od, 1)
                    dve.wait_ge(s_od, 2 * c + 2)
                    chain(dve.reciprocal(r_sb, d_sb))
                    dve.tensor_tensor(yT[:, CW * c:CW * c + CW], o_sb, r_sb, ALU.mult).then_inc(s_yT, 1)
                    dve.wait_ge(s_yT, c + 1)
            unit(("out", NC - 1))
            dve.wait_ge(s_rmf, read[0])

            for g in range(NC):
                w = slice(TPC * g, TPC * g + TPC)
                for t in range(TPC * g, TPC * g + TPC):
                    last = dve.bn_stats(bst[:, t, :], xn[:, t, :])
                chain(last)
                for t in range(TPC * g, TPC * g + TPC):
                    last = dve.bn_aggr(mv[:, t, :], bst[:, t, :])
                chain(last)
                chain(dve.tensor_tensor(ve[:, w], mv[:, w, 0], mv[:, w, 0], ALU.mult))
                dve.scalar_tensor_tensor(out=ve[:, w], in0=ve[:, w], scalar=EPS_RMS, in1=mv[:, w, 1], op0=ALU.add,
                                         op1=ALU.add).then_inc(s_ms, 1)
            for g in range(NC):
                dve.wait_ge(s_r2, g + 1)
                for t in range(TPC * g, TPC * g + TPC):
                    last = dve.tensor_scalar(G[:, t, :], xn[:, t, :], rd[:, t:t + 1], None, ALU.mult)
                last.then_inc(s_fn, 1)
            for g in range(NC):
                low1(NC + g, g % 2)

            def split_expert1(s, count):
                dve.wait_ge(s_ld1[s], 64 * count)
                chain(dve.tensor_scalar(v13[:, s], v13[:, s], cols[:, 3:4], SW, ALU.mult, ALU.mult))
                chain(dve.tensor_copy(v13h[:, s], v13[:, s]))
                dve.tensor_tensor(v13l[:, s], v13[:, s], v13h[:, s], ALU.subtract)
                chain(dve.tensor_scalar(v2h[:, s, 0:2], v2[:, s, 0:2], SW, None, ALU.mult))
                dve.scalar_tensor_tensor(out=v2l[:, s, 0:2], in0=v2[:, s, 0:2], scalar=SW, in1=v2h[:, s, 0:2], op0=ALU.mult, op1=ALU.subtract)
                r = KS1[2][1]
                chain(dve.tensor_scalar(v2h[0:r, s, 2], v2[0:r, s, 2], SW, None, ALU.mult))
                dve.scalar_tensor_tensor(out=v2l[0:r, s, 2], in0=v2[0:r, s, 2], scalar=SW, in1=v2h[0:r, s, 2], op0=ALU.mult,
                                         op1=ALU.subtract).then_inc(s_w1, 1)

            split_expert1(0, 1)
            chain(dve.tensor_tensor(x[:, :, :].rearrange("p t d -> p (t d)"), x[:, :, :].rearrange("p t d -> p (t d)"),
                                    xn[:, :, :].rearrange("p t d -> p (t d)"), ALU.add))
            bc = lambda v: v.unsqueeze(2).broadcast_to([P, NT, 8])
            dve.wait_ge(s_rt, 1)
            chain(dve.tensor_scalar(lg1[:, 0], ps[:, 6, 0:8 * NT].rearrange("p (t e) -> p t e", e=8), 1.0 / (SX * SW), None, ALU.mult))
            chain(dve.reduce_max(sm[:, 0], lg1[:, 0], AX_X))
            dve.tensor_tensor(lg1[:, 1], lg1[:, 0], bc(sm[:, 0]), ALU.subtract).then_inc(s_rl, 1)
            dve.wait_ge(s_re, 1)
            chain(dve.reduce_sum(sm[:, 6], lg1[:, 2], AX_X))
            chain(dve.reciprocal(sm[:, 7], sm[:, 6]))
            chain(dve.tensor_tensor(lg1[:, 0], lg1[:, 2], bc(sm[:, 7]), ALU.mult))
            top2(lg1[:, 0], lg1)
            chain(dve.tensor_tensor(sm[:, 2], sm[:, 0], sm[:, 1], ALU.add))
            chain(dve.tensor_scalar(sm[:, 2], sm[:, 2], 1e-9, None, ALU.add))
            chain(dve.reciprocal(sm[:, 3], sm[:, 2]))
            chain(dve.tensor_tensor(sm[:, 6], sm[:, 0], sm[:, 3], ALU.mult))
            chain(dve.tensor_tensor(sm[:, 7], sm[:, 1], sm[:, 3], ALU.mult))
            combine_weights(sm[:, 6], sm[:, 7], lg1).then_inc(s_comb1, 1)
            dve.wait_ge(s_comb1, 1)

            dve.sem_inc(s_hh, 2)
            dve.sem_inc(s_glo, 4)
            dve.sem_inc(s_add1, 2)

            def hidden(i, u):
                rows_ = KS1[u % 3][1]
                dve.wait_ge(s_silu, 24 * i + u + 1 + 2)
                dve.wait_ge(s_h3, 24 * i + u + 1)
                dve.wait_ge(s_glo, 24 * i + u + 1)
                dve.scalar_tensor_tensor(out=g32[0:rows_, u % 4, :], in0=ps[0:rows_, 2 + u % 2, :], scalar=SH / (SX * SW),
                                         in1=silu_sb[0:rows_, u % 2, :], op0=ALU.mult, op1=ALU.mult).then_inc(s_hh, 1)

            def low_hidden(i, u):
                gg, k = u // 3, u % 3
                rows_ = KS1[k][1]
                dve.wait_ge(s_ghi, 24 * i + u + 1)
                dve.tensor_tensor(g_lo[0:rows_, gg % 2, k, :], g32[0:rows_, u % 4, :], g_hi[0:rows_, gg % 2, k, :],
                                  ALU.subtract).then_inc(s_glo, 1)

            def add1(i, gg):
                s, g = gg // NC, gg % NC
                dve.wait_ge(s_y1, 8 * i + gg + 1 + 2)
                dve.wait_ge(s_add1, 8 * i + gg + 2)
                for q in range(TPC):
                    t = TPC * g + q
                    last = dve.scalar_tensor_tensor(out=x[:, t, :], in0=ps[:, 4 + gg % 2, P * q:P * q + P],
                                                    scalar=wcol[:, s, t:t + 1], in1=x[:, t, :], op0=ALU.mult, op1=ALU.add)
                last.then_inc(s_add1, 1)

            def turn1(i, last):
                for s in range(2):
                    chain(dve.tensor_scalar(wcol[:, s, :], comb[:, :, bass.ds(2 * i + s, 1)].rearrange("p t a -> p (t a)"),
                                            1.0 / (SH * SW), None, ALU.mult))
                    for g in range(NC):
                        gg = NC * s + g
                        for k in range(3):
                            u = 3 * gg + k
                            hidden(i, u)
                            if u:
                                low_hidden(i, u - 1)
                        if gg:
                            add1(i, gg - 1)
                        if g == 1 and not (last and s == 1):
                            split_expert1(1 - s, i + 1 + s)
                low_hidden(i, 23)
                add1(i, 2 * NC - 1)

            per = 2 * 5
            with dve.Fori(0, E1 // 2 - 1) as i:
                chain.turn(i, per)
                turn1(i, False)
                chain.turn_ends(per)
            chain.loop_ends(E1 // 2 - 1, per)
            turn1(E1 // 2 - 1, True)


_NAMES = ["x_in", "adj_t", "adj_in", "w_proj", "b_proj", "w_gcn", "b_gcn", "f0_wg", "f0_bg", "f0_bias", "f0_w1", "f0_b1",
          "f0_w2", "f0_b2", "g1_w", "ln1", "ln2", "wq", "wk", "wv", "wo", "w_router", "f1_w1", "f1_w2", "f1_w3",
          "cos_t", "sin_t"]


def lay_out(a):
    import numpy as np

    def rows(v):
        return v.reshape(NT, P, -1).transpose(1, 0, 2)

    freq = np.float32(1.0) / np.float32(10000.0) ** (np.arange(0, HD, 2, dtype=np.float32) / HD)
    emb = np.outer(np.arange(T, dtype=np.float32), np.concatenate([freq, freq]))
    col = lambda v: v.reshape(P, 1)
    d = {
        "x_in": rows(a["x"]), "adj_t": a["adj"].T.reshape(NT, P, T), "adj_in": a["adj"].reshape(NT, P, T),
        "w_proj": a["L0_gnn_W_proj"], "b_proj": col(a["L0_gnn_b_proj"]), "w_gcn": a["L0_gnn_W_gcn"],
        "b_gcn": col(a["L0_gnn_b_gcn"]), "f0_wg": a["L0_ffn_Wg"], "f0_bg": a["L0_ffn_bg"], "f0_bias": a["L0_ffn_bias"],
        "f0_w1": a["L0_ffn_W1"], "f0_b1": a["L0_ffn_b1"].reshape(E0, K0, P).transpose(0, 2, 1),
        "f0_w2": a["L0_ffn_W2"].reshape(E0, K0, P, D).transpose(0, 2, 1, 3), "f0_b2": a["L0_ffn_b2"],
        "g1_w": a["L1_gnn_w"], "ln1": col(a["L1_ffn_ln1_w"]), "ln2": col(a["L1_ffn_ln2_w"]),
        "wq": a["L1_ffn_wq"].T, "wk": a["L1_ffn_wk"].T, "wv": a["L1_ffn_wv"].T, "wo": a["L1_ffn_wo"].T,
        "w_router": a["L1_ffn_router_w"].T, "f1_w1": a["L1_ffn_w1"].transpose(0, 2, 1),
        "f1_w2": a["L1_ffn_w2"].transpose(0, 2, 1), "f1_w3": a["L1_ffn_w3"].transpose(0, 2, 1),
        "cos_t": np.cos(emb).T, "sin_t": np.sin(emb).T,
    }
    return {k: np.ascontiguousarray(v) for k, v in d.items()}


def kernel(**inputs):
    import numpy as np
    import concourse.bacc as bacc
    from concourse.bass_utils import run_bass_kernel_spmd

    arrays = lay_out({k: np.asarray(v) for k, v in inputs.items()})
    nc = bacc.Bacc("TRN2", target_bir_lowering=False, num_devices=1)
    args = [nc.dram_tensor(f"in_{n}", arrays[n].shape, mybir.dt.from_np(arrays[n].dtype), kind="ExternalInput").ap()
            for n in _NAMES]
    args.append(nc.dram_tensor("out", (P, NT, D), F32, kind="ExternalOutput").ap())
    program(nc, *args)
    r = run_bass_kernel_spmd(nc, [{f"in_{n}": arrays[n] for n in _NAMES}], core_ids=[0])
    return np.ascontiguousarray(r.results[0]["out"].transpose(1, 0, 2).reshape(T, D))
```

```python
from contextlib import ExitStack

import concourse.bass as bass
from concourse import mybir

F32 = mybir.dt.float32
F16 = mybir.dt.float16
BF16 = mybir.dt.bfloat16
I32 = mybir.dt.int32
ALU = mybir.AluOpType
ACT = mybir.ActivationFunctionType
AX_X = mybir.AxisListType.X

P = 128
T = 2048
D = 128
NT = T // P
CW = 512
NC = T // CW
TPC = CW // P
NEG = -1e30

TOP = 350
LIMIT = TOP
EPS_LN = 1e-5
EPS_RMS = 1e-6
E0 = 8
H0 = 256
K0 = H0 // P
E1 = 8
H1 = 341
KS1 = [(0, 128), (128, 128), (256, 85)]
NH = 4
NKV = 2
HD = 32

SX = 32.0
SW = 256.0
SH = 8.0
SQ = 8.0


class Chain:

    def __init__(self, eng, sem):
        self.eng, self.sem, self.done, self.here = eng, sem, 0, 0
        self.base = 0

    def __call__(self, ins):
        ins.then_inc(self.sem, 1)
        self.here += 1
        self.eng.wait_ge(self.sem, self.base + self.here)

    def turn(self, i, per):
        if self.here:
            self.done += self.here
            self.here = 0
        self.base = i * per + self.done

    def turn_ends(self, per):
        assert self.here == per, (self.here, per)
        self.here = 0

    def loop_ends(self, turns, per):
        self.done += turns * per
        self.base = self.done


def program(nc, x_in, adj_t, adj_in, w_proj, b_proj, w_gcn, b_gcn, f0_wg, f0_bg, f0_bias, f0_w1, f0_b1,
            f0_w2, f0_b2, g1_w, ln1, ln2, wq, wk, wv, wo, w_router, f1_w1, f1_w2, f1_w3, cos_t, sin_t, out):
    with ExitStack() as ctx:
        def sb(name, shape, dt=F32):
            return ctx.enter_context(nc.sbuf_tensor(name, shape, dt))

        def sem(name):
            return ctx.enter_context(nc.semaphore(name))

        A = sb("A", [P, NT, T])
        x = sb("x", [P, NT, D])
        xn = sb("xn", [P, NT, D])
        G = sb("G", [P, NT, D])
        R = sb("R", [P, 5 * T])
        xT = sb("xT", [P, T])
        ident = sb("ident", [P, P])
        ones = sb("ones", [P, 32])
        ones_b = sb("ones_b", [P, 32], BF16)
        neg_half = sb("neg_half", [P, NT])
        rev = sb("rev", [P, NT, 8])
        wmat = sb("wmat", [P, 3, P])
        cols = sb("cols", [P, 8])
        wg32 = sb("wg32", [P, 8])
        wg16 = sb("wg16", [P, 2, 8], F16)
        gbias = sb("gbias", [P, 2, 8])
        b2_sb = sb("b2_sb", [8, D])
        bst = sb("bst", [P, NT, 6])
        mv = sb("mv", [P, NT, 2])
        ve = sb("ve", [P, NT])
        rstd = sb("rstd", [P, NT])
        rd = sb("rd", [P, NT])
        dis = sb("dis", [P, NT])
        lg = xT[:, 0:10 * NT * 8].rearrange("p (n t e) -> p n t e", n=10, e=8)
        sm = sb("sm", [P, 12, NT])
        comb = sb("comb", [P, NT, 8])
        cnt = sb("cnt", [P, 4])
        factor = sb("factor", [P, 4])
        st_b1 = sb("st_b1", [P, 2, K0])
        b1 = sb("b1", [P, 2, K0])
        b1s = sb("b1s", [P, 2, K0])
        flag = sb("flag", [1, 1], I32)

        FB = 3
        fbuf = R[:, 0:FB * T].rearrange("p (b t) -> p b t", b=FB)
        mbuf = R[:, FB * T:(FB + 1) * T].bitcast(BF16).rearrange("p (b t) -> p b t", b=2)
        h2T = R[:, 4 * T:5 * T]
        asum = h2T
        a_row, f_row, e_row, c_row = (R[:, n * T:(n + 1) * T] for n in range(4))
        rT = xT[:, 0:2 * CW].rearrange("p (b t) -> p b t", b=2)
        gen = xT[:, 2 * CW:2 * CW + 8]
        thr, bit, cand, ge = (gen[:, n:n + 1].bitcast(I32) for n in range(4))
        thr_f, cand_f, cnt_f, need_f = gen[:, 0:1], gen[:, 2:3], gen[:, 4:5], gen[:, 5:6]
        st_w1 = R[:, 0:512].rearrange("p (s h) -> p s h", s=2)
        st_w2 = R[:, 512:1024].rearrange("p (s k d) -> p s k d", s=2, k=K0)
        w1h = R[:, 1024:1280].bitcast(F16).rearrange("p (s h) -> p s h", s=2)
        w1l = R[:, 1280:1536].bitcast(F16).rearrange("p (s h) -> p s h", s=2)
        w2h = R[:, 1536:1792].bitcast(F16).rearrange("p (s k d) -> p s k d", s=2, k=K0)
        w2l = R[:, 1792:2048].bitcast(F16).rearrange("p (s k d) -> p s k d", s=2, k=K0)
        h32 = R[:, 2048:2048 + 4 * CW].rearrange("p (b t) -> p b t", b=4)
        o = 2048 + 4 * CW
        hh_hi = R[:, o:o + 4 * K0 * CW // 2].bitcast(F16).rearrange("p (b k t) -> p b k t", b=4, k=K0)
        o += 2 * K0 * CW
        hh_lo = R[:, o:o + 4 * K0 * CW // 2].bitcast(F16).rearrange("p (b k t) -> p b k t", b=4, k=K0)
        o += 2 * K0 * CW
        combT = xT[0:8, :]
        G16 = G[:, :, :].rearrange("p t d -> p (t d)").bitcast(F16)
        xh, xl = G16[:, 0:T], G16[:, T:2 * T]
        assert o <= 5 * T

        hagg = R[:, 0:2 * CW].rearrange("p (b t) -> p b t", b=2)
        zs = R[:, 2 * CW:4 * CW].rearrange("p (b t) -> p b t", b=2)
        ez = R[:, 4 * CW:6 * CW].rearrange("p (b t) -> p b t", b=2)
        cos_sb = R[:, 2 * T:3 * T]
        sin_sb = R[:, 3 * T:4 * T]
        o = 4 * T
        wq32, wk32, wv32, wo32, wr32 = (R[:, o + a:o + b] for a, b in ((0, 128), (128, 192), (192, 256), (256, 384), (384, 392)))
        o += 392
        watt = R[:, o:o + 456].bitcast(F16).rearrange("p (s n) -> p s n", s=2)
        WQ, WQR, WK, WKR, WV, WR = 0, 128, 256, 320, 384, 448
        o += 456
        AF = A[:, :, :].rearrange("p j t -> p (j t)")
        KQ = 3 * HD
        Qs = AF[:, 0:NH * T // 2].bitcast(F16).rearrange("p (h t) -> p h t", h=NH)
        a = NH * T // 2
        Ks = AF[:, a:a + NKV * T // 2].bitcast(F16).rearrange("p (h t) -> p h t", h=NKV)
        a += NKV * T // 2
        Pb = AF[:, a:a + 2 * NH * CW].rearrange("p (b h t) -> p b h t", b=2, h=NH)
        a += 2 * NH * CW
        V = AF[:, a:a + NT * NKV * HD].rearrange("p (t d) -> p t d", t=NT)
        a += NT * NKV * HD
        yT = AF[:, a:a + T]
        a += T
        q16 = AF[:, a:a + T].bitcast(F16).rearrange("p (s t) -> p s t", s=2)
        a += T
        k16 = AF[0:NKV * HD, a:a + T].bitcast(F16).rearrange("p (s t) -> p s t", s=2)
        a += T
        rope = AF[:, a:a + 6 * CW].rearrange("p (n t) -> p n t", n=6)
        a += 6 * CW
        o_sb = AF[:, a:a + CW]
        d_sb = AF[:, a + CW:a + 2 * CW]
        r_sb = AF[:, a + 2 * CW:a + 3 * CW]
        a += 3 * CW
        pm = AF[:, a:a + NH * TPC * NC].rearrange("p (h q b) -> p h q b", h=NH, q=TPC)
        a += NH * TPC * NC
        m32 = AF[:, a:a + 16].rearrange("p (h q) -> p h q", h=NH)
        m16 = AF[:, a + 16:a + 24].bitcast(F16).rearrange("p (h q) -> p h q", h=NH)
        a += 24
        ident_b = AF[:, a:a + 64].bitcast(BF16)
        ident_h = AF[:, a + 64:a + 128].bitcast(F16)
        mask_ts = AF[:, a + 128:a + 192].bitcast(BF16)
        mask_st = AF[:, a + 192:a + 256].bitcast(BF16)
        a += 256
        v13 = AF[:, a:a + 4 * H1].rearrange("p (s m h) -> p s m h", s=2, m=2)
        a += 4 * H1
        v2 = AF[:, a:a + 2 * 3 * D].rearrange("p (s k d) -> p s k d", s=2, k=3)
        a += 6 * D
        v13h = AF[:, a:a + 2 * H1].bitcast(F16).rearrange("p (s m h) -> p s m h", s=2, m=2)
        a += 2 * H1
        v13l = AF[:, a:a + 2 * H1].bitcast(F16).rearrange("p (s m h) -> p s m h", s=2, m=2)
        a += 2 * H1
        v2h = AF[:, a:a + 3 * D].bitcast(F16).rearrange("p (s k d) -> p s k d", s=2, k=3)
        a += 3 * D
        v2l = AF[:, a:a + 3 * D].bitcast(F16).rearrange("p (s k d) -> p s k d", s=2, k=3)
        a += 3 * D
        assert a <= NT * T
        a = 0
        silu_sb = AF[:, a:a + 3 * CW].rearrange("p (b t) -> p b t", b=3)
        a += 3 * CW
        g32 = AF[:, a:a + 6 * CW].rearrange("p (b t) -> p b t", b=6)
        a += 6 * CW
        g_hi = AF[:, a:a + 6 * CW].bitcast(F16).rearrange("p (b k t) -> p b k t", b=4, k=3)
        a += 6 * CW
        g_lo = AF[:, a:a + 6 * CW].bitcast(F16).rearrange("p (b k t) -> p b k t", b=4, k=3)
        xT16 = xT[:, :].bitcast(F16)
        lg1 = G[:, :, :].rearrange("p t d -> p (t d)")[:, 0:10 * NT * 8].rearrange("p (n t e) -> p n t e", n=10, e=8)
        th, tl = xT16[:, 0:T], xT16[:, T:2 * T]

        ps = ctx.enter_context(nc.psum_tensor("ps", [P, 8, CW], F32))

        s_x = [sem(f"x_chunk{g}_loaded") for g in range(NC)]
        s_first = sem("first_operands_loaded")
        s_small = sem("small_loaded")
        s_A = [sem(f"adj_tile_{j}_loaded") for j in range(NT)]
        s_const = sem("constants_made")
        s_cpool = sem("pool_steps")
        s_dve = sem("vector_steps")
        s_acts = sem("scalar_steps")
        s_var = sem("variance_ready")
        s_rstd = sem("rstd_ready")
        s_xn = sem("rows_normalised")
        s_tr = sem("rows_transposed")
        s_pre_ev = sem("transposed_copied")
        s_h2p = sem("h2_product")
        s_h2 = sem("h2_ready")
        s_gp = sem("g_product")
        s_G = sem("g_ready")
        s_sq = sem("square_ready")
        s_F = sem("filtered_ready")
        s_mask = sem("mask_ready")
        s_cntp = sem("tile_counted")
        s_aggp = sem("tile_aggregated")
        s_cmax = sem("count_max_ready")
        s_cmT = sem("count_max_transposed")
        s_flag = sem("flag_ready")
        s_feat = sem("features_ready")
        s_ftr = sem("features_transposed")
        s_x1 = sem("gnn0_added")
        s_asum = sem("adj_tiles_summed")
        s_degc = sem("deg_columns")
        s_degv = sem("deg_plus_one")
        s_dis = sem("deg_isqrt_ready")
        s_xhi = sem("x_high_ready")
        s_xlo = sem("x_low_ready")
        s_wg = sem("gate_weights_split")
        s_gate = sem("gate_product")
        s_diff = sem("top_difference_ready")
        s_ediff = sem("exp_difference_ready")
        s_comb = sem("combine_weights_ready")
        s_ld0 = [sem(f"expert0_weights_slot{i}") for i in range(2)]
        s_w1s = sem("expert0_first_weights_split")
        s_w2 = sem("expert0_second_weights_split")
        s_w00 = sem("expert0_number0_split")
        s_h0 = sem("hidden0_product")
        s_relu = sem("hidden0_relu")
        s_hhi = sem("hidden0_high")
        s_hlo = sem("hidden0_low")
        s_y0 = sem("expert0_output")
        s_add0 = sem("expert0_added")
        s_cT = sem("combine_transposed")
        s_cTc = sem("combine_transposed_copied")
        s_b2 = sem("bias2_product")
        s_b2a = sem("bias2_added")
        s_b1s = sem("first_bias_scaled")
        s_logit = sem("gate_logits_ready")
        s_out = sem("output_stored")
        g_load = sem("general_rows_loaded")
        g_sq = sem("general_squares")
        g_tanh = sem("general_filtered")
        g_row = sem("general_rows_selected")
        g_tr = sem("general_transposed")
        g_cp = sem("general_transposed_copied")
        g_feat = sem("general_features_ready")
        g_mm = sem("general_multiplied")
        s_gen = sem("general_vector_steps")
        s_agg1 = sem("gnn1_aggregated")
        s_hagg = sem("gnn1_aggregate_copied")
        s_z = sem("gnn1_product")
        s_zn = sem("gnn1_negative_part")
        s_ez = sem("gnn1_exp_ready")
        s_x3 = sem("gnn1_added")
        s_attw = sem("attention_weights_loaded")
        s_attws = sem("attention_weights_split")
        s_hn = sem("attention_rows_ready")
        s_qp = sem("query_product")
        s_kp = sem("key_product")
        s_vp = sem("value_product")
        s_qr = sem("query_rotated")
        s_kr = sem("key_rotated")
        s_qhi = sem("query_high_ready")
        s_khi = sem("key_high_ready")
        s_V = sem("values_ready")
        s_qlo = sem("query_low_ready")
        s_klo = sem("key_low_ready")
        s_mc = sem("masks_made")
        s_stack = [sem(f"queries_keys_stacked_half{i}") for i in range(2)]
        s_rm = sem("row_max_bank_filled")
        s_rmf = sem("row_max_bank_read")
        s_m = sem("row_max_ready")
        s_st = sem("scores_ready")
        s_p = sem("probabilities_ready")
        s_pv = sem("probabilities_used")
        s_od = sem("attention_sums_copied")
        s_yT = sem("attention_output_ready")
        s_x4 = sem("attention_added")
        s_ms = sem("mean_square_ready")
        s_r2 = sem("rms_ready")
        s_fn = sem("router_rows_ready")
        s_tr1 = sem("layer1_rows_transposed")
        s_thi = sem("layer1_high_ready")
        s_tlo = sem("layer1_low_ready")
        s_rt = sem("router_product")
        s_rl = sem("router_logits_shifted")
        s_re = sem("router_exp_ready")
        s_comb1 = sem("combine1_ready")
        s_ld1 = [sem(f"expert1_weights_slot{i}") for i in range(2)]
        s_w13 = sem("expert1_first_weights_split")
        s_w22 = sem("expert1_second_weights_split")
        s_tail = sem("expert1_tail_rows_cleared")
        s_h1 = sem("gate_unit_product")
        s_h3 = sem("up_unit_product")
        s_silu = sem("silu_ready")
        s_hh = sem("hidden1_ready")
        s_ghi = sem("hidden1_high")
        s_glo = sem("hidden1_low")
        s_y1 = sem("expert1_output")
        s_add1 = sem("expert1_added")

        steps = [(c, j) for c in range(NC) for j in [*range(TPC * c + TPC - 1, TPC * c - 1, -1), *range(TPC * c)]]

        def first_step(c, j):
            return j == TPC * c + TPC - 1

        def last_step(c, j):
            return j == (TPC * c - 1 if c else 0)

        def max_units(c):
            return ([("max", t, h, b) for t in range(TPC * c, TPC * c + TPC) for h in range(NH) for b in range(c + 1)]
                    + [("neg", c, h) for h in range(NH)])

        units_at = {}
        neg_done = []
        count = len(max_units(0))
        neg_done.append(count)
        for c in range(NC):
            todo = max_units(c + 1) if c + 1 < NC else []
            n = TPC * (c + 1)
            per_step = -(-len(todo) // n)
            for turn, (_, j) in enumerate([step for step in steps if step[0] == c]):
                units_at[(c, j)] = todo[turn * per_step:(turn + 1) * per_step]
                if turn == 3 and c:
                    units_at[(c, j)] = units_at[(c, j)] + [("out", c - 1)]
                count += len(units_at[(c, j)])
            neg_done.append(count)

        H_BANKS = (0, 1, 6, 7)

        block = ctx.enter_context(nc.Block())

        first = [(wmat[:, 0, :], w_proj), (wmat[:, 1, :], w_gcn), (cols[:, 0:1], b_proj)]
        small = [
            (wmat[:, 2, :], g1_w), (cols[:, 1:2], b_gcn), (cols[:, 2:3], ln1), (cols[:, 3:4], ln2),
            (wg32[:, :], f0_wg), (gbias[:, 0, :], f0_bg.partition_broadcast(P)),
            (gbias[:, 1, :], f0_bias.partition_broadcast(P)), (b2_sb[:, :], f0_b2),
        ]

        def many_entries(eng):
            eng.wait_ge(s_flag, 1)
            return eng.If(eng.value_load(flag[0:1, 0:1], min_val=0, max_val=1) > 0)

        def pick(chain, dve, n, L, lg):
            eq, key, km = lg[:, 1], lg[:, 2], sm[:, 5]
            value, hot = sm[:, n], lg[:, 3 + n]
            bc = lambda v: v.unsqueeze(2).broadcast_to([P, NT, 8])
            chain(dve.reduce_max(value, L, AX_X))
            chain(dve.tensor_tensor(eq, L, bc(value), ALU.is_equal))
            chain(dve.tensor_tensor(key, eq, rev[:, :, :], ALU.mult))
            chain(dve.reduce_max(km, key, AX_X))
            chain(dve.tensor_tensor(hot, key, bc(km), ALU.is_equal))
            if n == 0:
                chain(dve.scalar_tensor_tensor(out=lg[:, 5], in0=hot, scalar=NEG, in1=L, op0=ALU.mult, op1=ALU.add))

        def combine_weights(chain, eng, w1, w2, lg):
            bc = lambda v: v.unsqueeze(2).broadcast_to([P, NT, 8])
            chain(eng.tensor_tensor(lg[:, 6], lg[:, 3], bc(w1), ALU.mult))
            chain(eng.tensor_tensor(lg[:, 7], lg[:, 4], bc(w2), ALU.mult))
            return eng.tensor_tensor(comb[:, :, :], lg[:, 6], lg[:, 7], ALU.add)

        @block.sync
        def _(sp):
            for g in range(NC):
                w = slice(TPC * g, TPC * g + TPC)
                sp.dma_start(x[:, w, :], x_in[:, w, :]).then_inc(s_x[g], 16)
            for j in range(NT):
                sp.dma_start(A[:, j, :], adj_t[j]).then_inc(s_A[j], 16)

            def load_expert0(s, e):
                sp.dma_start(st_w1[:, s, :], f0_w1[bass.ds(e, 1), :, :].rearrange("a p h -> (a p) h")).then_inc(s_ld0[s], 16)
                sp.dma_start(st_w2[:, s, :, :], f0_w2[bass.ds(e, 1), :, :, :].rearrange("a p k d -> (a p) k d")).then_inc(s_ld0[s], 16)
                sp.dma_start(st_b1[:, s, :], f0_b1[bass.ds(e, 1), :, :].rearrange("a p k -> (a p) k")).then_inc(s_ld0[s], 16)

            with many_entries(sp):
                sp.dma_start(a_row, adj_in[0]).then_inc(g_load, 16)
                with sp.Fori(1, NT) as i:
                    sp.wait_ge(g_sq, i)
                    sp.dma_start(a_row, adj_in[bass.ds(i, 1), :, :].rearrange("a p t -> (a p) t")).then_inc(g_load, 16)
                sp.wait_ge(g_mm, 4 * NT + 2)
            sp.wait_ge(s_aggp, NT)
            sp.wait_ge(s_cntp, NT)
            load_expert0(0, 0)
            load_expert0(1, 1)
            sp.wait_ge(s_w00, 2)
            with sp.Fori(1, E0 // 2) as i:
                for s in range(2):
                    sp.wait_ge(s_w2, 2 * i + s - 1)
                    load_expert0(s, 2 * i + s)
            sp.wait_ge(s_add0, E0 * NC + 2)
            for dst, src in ((cos_sb, cos_t), (sin_sb, sin_t)):
                for h in range(NH):
                    sp.dma_start(dst[HD * h:HD * h + HD, :], src).then_inc(s_attw, 16)
            for dst, src in ((wq32, wq), (wk32, wk), (wv32, wv), (wo32, wo), (wr32, w_router)):
                sp.dma_start(dst, src).then_inc(s_attw, 16)

            def load_expert1(s, e):
                sp.dma_start(v13[:, s, 0, :], f1_w1[bass.ds(e, 1), :, :].rearrange("a p h -> (a p) h")).then_inc(s_ld1[s], 16)
                sp.dma_start(v13[:, s, 1, :], f1_w3[bass.ds(e, 1), :, :].rearrange("a p h -> (a p) h")).then_inc(s_ld1[s], 16)
                sp.dma_start(v2[:, s, 0:2, :], f1_w2[bass.ds(e, 1), 0:2 * P, :].rearrange("a (k p) d -> (a p) k d", p=P)
                             ).then_inc(s_ld1[s], 16)
                sp.dma_start(v2[0:KS1[2][1], s, 2, :], f1_w2[bass.ds(e, 1), 2 * P:H1, :].rearrange("a p d -> (a p) d")
                             ).then_inc(s_ld1[s], 16)

            sp.wait_ge(s_tail, 1)
            load_expert1(0, 0)
            load_expert1(1, 1)
            for half in range(2):
                w = slice(2 * CW * half, 2 * CW * half + 2 * CW)
                for done, src, dst, heads, order in ((s_qlo, q16, Qs, NH, (0, 1, 0)), (s_klo, k16, Ks, NKV, (0, 0, 1))):
                    sp.wait_ge(done, 2 * half + 2)
                    for n, part in enumerate(order):
                        for h in range(heads):
                            sp.dma_start(dst[HD * n:HD * n + HD, h, w], src[HD * h:HD * h + HD, part, w]
                                         ).then_inc(s_stack[half], 16)
            with sp.Fori(1, E1 // 2) as i:
                for s in range(2):
                    sp.wait_ge(s_w22, 2 * i + s)
                    load_expert1(s, 2 * i + s)
            for g in range(NC):
                sp.wait_ge(s_add1, (E1 - 1) * NC + g + 1 + 2)
                sp.dma_start(out[:, TPC * g:TPC * g + TPC, :], x[:, TPC * g:TPC * g + TPC, :]).then_inc(s_out, 16)
            sp.wait_ge(s_out, 16 * NC)

        @block.gpsimd
        def _(pool):
            chain = Chain(pool, s_cpool)
            pool.memset(neg_half[:, :], -0.5)
            pool.memset(ones[:, :], 1.0)
            for n, v in enumerate((SW, 1.0, SH)):
                pool.memset(factor[:, n:n + 1], v)
            pool.memset(ones_b[:, :], 1.0)
            chain(pool.memset(ident[:, :], 0.0))
            pool.affine_select(out=ident[:, :], in_=ident[:, :], compare_op=ALU.not_equal, fill=1.0, base=0,
                               pattern=[[-1, P]], channel_multiplier=1).then_inc(s_const, 1)
            pool.iota(rev[:, :, :], pattern=[[0, NT], [-1, 8]], base=8, channel_multiplier=0,
                      allow_small_or_imprecise_dtypes=True).then_inc(s_const, 1)

            def inverse_root(n, g):
                pool.wait_ge(s_var, n)
                pool.tensor_tensor(rstd[:, TPC * g:TPC * g + TPC], ve[:, TPC * g:TPC * g + TPC],
                                   neg_half[:, 0:TPC], ALU.pow).then_inc(s_rstd, 1)

            for g in range(NC):
                inverse_root(g + 1, g)
            pool.wait_ge(s_gp, NC)
            pool.wait_ge(s_A[0], 16)
            for j in range(1, NT):
                pool.wait_ge(s_A[j], 16)
                pool.tensor_tensor(asum, A[:, 0, :] if j == 1 else asum, A[:, j, :], ALU.add).then_inc(s_asum, 1)
                pool.wait_ge(s_asum, j)
            for g in range(NC):
                inverse_root(NC + g + 1, g)
            def times(out, v, n):
                return pool.tensor_tensor(out, v, factor[:, n:n + 1].broadcast_to([P, v.shape[1]]), ALU.mult)

            flat0 = lambda v, s: v[:, s].rearrange("p k d -> p (k d)")

            def split_expert0(s, count, free):
                pool.wait_ge(s_ld0[s], 48 * count)
                times(st_w1[:, s], st_w1[:, s], 0)
                chain(times(flat0(st_w2, s), flat0(st_w2, s), 0))
                if free is not None:
                    pool.wait_ge(s_y0, free)
                chain(times(w1h[:, s], st_w1[:, s], 1))
                times(b1[:, s, :], st_b1[:, s, :], 1)
                times(b1s[:, s, :], st_b1[:, s, :], 2)
                pool.tensor_tensor(w1l[:, s], st_w1[:, s], w1h[:, s], ALU.subtract).then_inc(s_w1s, 1)
                chain(times(flat0(w2h, s), flat0(st_w2, s), 1))
                pool.tensor_tensor(w2l[:, s], st_w2[:, s], w2h[:, s], ALU.subtract).then_inc(s_w2, 1)

            split_expert0(1, 1, None)
            with pool.Fori(1, E0 // 2) as i:
                chain.turn(i - 1, 6)
                for s in range(2):
                    split_expert0(s, i + 1, (2 * i + s - 1) * NC + 4)
                chain.turn_ends(6)
            chain.loop_ends(E0 // 2 - 1, 6)
            pool.wait_ge(s_degv, 1)
            pool.tensor_tensor(dis[:, :], sm[:, 11, :], neg_half[:, :], ALU.pow).then_inc(s_dis, 1)
            pool.wait_ge(s_dis, 1)
            for g in range(NC):
                w = slice(TPC * g, TPC * g + TPC)
                pool.wait_ge(s_var, 2 * NC + g + 1)
                chain(pool.tensor_tensor(rstd[:, w], ve[:, w], neg_half[:, 0:TPC], ALU.pow))
                pool.tensor_tensor(rd[:, w], rstd[:, w], dis[:, w], ALU.mult).then_inc(s_rstd, 1)
            pool.wait_ge(s_agg1, NC)
            pool.memset(v2[:, :, 2, :], 0.0).then_inc(s_tail, 1)
            chain(pool.memset(mask_ts[:, :], 0.0))
            chain(pool.memset(mask_st[:, :], 0.0))
            chain(pool.affine_select(out=mask_ts[:, :], in_=mask_ts[:, :], compare_op=ALU.is_ge, fill=NEG, base=0,
                                     pattern=[[-1, P]], channel_multiplier=1))
            chain(pool.affine_select(out=mask_st[:, :], in_=mask_st[:, :], compare_op=ALU.is_ge, fill=NEG, base=0,
                                     pattern=[[1, P]], channel_multiplier=-1))
            chain(pool.tensor_copy(ident_b[:, :], ident[:, :]))
            chain(pool.tensor_copy(ident_h[:, :], ident[:, :]))
            pool.memset(Ks[KQ:KQ + 1, :, :], 16.0).then_inc(s_mc, 1)
            pool.wait_ge(s_mc, 1)
            for g in range(NC):
                w = slice(TPC * g, TPC * g + TPC)
                pool.wait_ge(s_var, 3 * NC + g + 1)
                chain(pool.tensor_tensor(rstd[:, w], ve[:, w], neg_half[:, 0:TPC], ALU.pow))
                chain(pool.tensor_tensor(rd[:, w], rstd[:, w], rstd[:, w], ALU.mult))
                chain(pool.tensor_tensor(rd[:, w], rd[:, w], mv[:, w, 1], ALU.mult))
                chain(pool.tensor_scalar(rd[:, w], rd[:, w], EPS_RMS, None, ALU.add))
                chain(pool.tensor_tensor(rd[:, w], rd[:, w], neg_half[:, 0:TPC], ALU.pow))
                pool.tensor_tensor(rd[:, w], rd[:, w], rstd[:, w], ALU.mult).then_inc(s_rstd, 1)
            flat13 = lambda v, s: v[:, s].rearrange("p m h -> p (m h)")
            chain(pool.tensor_scalar(factor[:, 3:4], cols[:, 3:4], SW, None, ALU.mult))

            def split_expert1(s, count, free):
                pool.wait_ge(s_ld1[s], 64 * count)
                times(flat13(v13, s), flat13(v13, s), 3)
                chain(times(flat0(v2, s), flat0(v2, s), 0))
                if free is not None:
                    pool.wait_ge(s_y1, free)
                chain(times(flat13(v13h, s), flat13(v13, s), 1))
                pool.tensor_tensor(v13l[:, s], v13[:, s], v13h[:, s], ALU.subtract).then_inc(s_w13, 1)
                chain(times(flat0(v2h, s), flat0(v2, s), 1))
                pool.tensor_tensor(v2l[:, s], v2[:, s], v2h[:, s], ALU.subtract).then_inc(s_w22, 1)

            split_expert1(0, 1, None)
            split_expert1(1, 1, None)
            for g in range(NC):
                w = slice(TPC * g, TPC * g + TPC)
                pool.wait_ge(s_ms, g + 1)
                pool.tensor_tensor(rd[:, w], ve[:, w], neg_half[:, 0:TPC], ALU.pow).then_inc(s_r2, 1)
            with pool.Fori(1, E1 // 2) as i:
                chain.turn(i - 1, 6)
                for s in range(2):
                    split_expert1(s, i + 1, (2 * i + s - 1) * NC + 4)
                chain.turn_ends(6)
            chain.loop_ends(E1 // 2 - 1, 6)

        @block.scalar
        def _(act):
            for dst, src in first:
                act.dma_start(dst, src).then_inc(s_first, 16)
            for dst, src in small:
                act.dma_start(dst, src).then_inc(s_small, 16)

            act.wait_ge(s_first, 16 * len(first))
            for g in range(NC):
                act.wait_ge(s_h2p, g + 1)
                act.activation(h2T[:, CW * g:CW * g + CW], ps[:, 4 + g, :], ACT.Tanh, bias=cols[:, 0:1]).then_inc(s_h2, 1)
            for j in range(NT):
                act.wait_ge(s_sq, j + 1)
                act.activation(fbuf[:, j % FB, :], fbuf[:, j % FB, :], ACT.Tanh).then_inc(s_F, 1)
            def features(done):
                for g in range(NC):
                    act.activation(xT[:, CW * g:CW * g + CW], ps[:, g, :], ACT.Relu, bias=cols[:, 1:2]).then_inc(done, 1)

            act.wait_ge(s_aggp, NT)
            act.wait_ge(s_small, 16 * len(small))
            features(s_feat)
            with many_entries(act):
                with act.Fori(0, NT) as i:
                    act.wait_ge(g_sq, i + 1)
                    act.activation(f_row, f_row, ACT.Tanh).then_inc(g_tanh, 1)
                    for q in range(4):
                        act.wait_ge(g_tr, 4 * i + q + 1)
                        act.wait_ge(g_mm, 4 * i + q + 1)
                        act.activation(rT[:, q % 2, :], ps[:, 6 + q % 2, :], ACT.Copy).then_inc(g_cp, 1)
                act.wait_ge(g_mm, 4 * NT + 2)
                features(g_feat)

            def high_parts(n):
                g = n % NC
                act.wait_ge(s_tr, NC + n + 1)
                act.activation(xh[:, CW * g:CW * g + CW], ps[:, n % 2 + 6, :], ACT.Copy, scale=SX).then_inc(s_xhi, 1)

            for g in range(NC):
                high_parts(g)

            act.sem_inc(s_relu, 4)

            def relu(i, gg, k):
                s, u = gg // NC, gg * K0 + k
                act.wait_ge(s_h0, 8 * K0 * i + u + 1)
                act.wait_ge(s_hlo, 8 * K0 * i + u + 1)
                act.wait_ge(s_y0, 8 * i + gg + 1)
                act.activation(h32[:, u % 4, :], ps[:, H_BANKS[u % 4], :], ACT.Relu, bias=b1[:, s, k:k + 1],
                               scale=1.0 / (SX * SW))
                act.activation(hh_hi[:, gg % 4, k, :], ps[:, H_BANKS[u % 4], :], ACT.Relu, bias=b1s[:, s, k:k + 1],
                               scale=SH / (SX * SW)).then_inc(s_relu, 1)

            def bias2_copy(half):
                act.wait_ge(s_cT, half + 1)
                act.activation(combT[:, 2 * CW * half:2 * CW * half + 2 * CW], ps[0:8, 4:6, :], ACT.Copy).then_inc(s_cTc, 1)

            act.wait_ge(s_b1s, 1)
            for gg in range(2 * NC):
                if gg == NC:
                    act.wait_ge(s_w1s, 1)
                for k in range(K0):
                    relu(0, gg, k)
                if gg == 1:
                    act.wait_ge(s_diff, 1)
                    act.activation(sm[:, 3, :], sm[:, 2, :], ACT.Exp).then_inc(s_ediff, 1)
                if gg in (4, 5):
                    bias2_copy(gg - 4)
            with act.Fori(1, E0 // 2) as i:
                for gg in range(2 * NC):
                    for k in range(K0):
                        relu(i, gg, k)

            def aggregate_copy(c):
                act.wait_ge(s_agg1, c + 1)
                if c >= 2:
                    act.wait_ge(s_z, c - 1)
                act.activation(hagg[:, c % 2, :], ps[:, c, :], ACT.Copy).then_inc(s_hagg, 1)

            def elu_exp(c):
                act.wait_ge(s_zn, c + 1)
                act.activation(ez[:, c % 2, :], ez[:, c % 2, :], ACT.Exp).then_inc(s_ez, 1)

            aggregate_copy(0)
            for c in range(1, NC):
                aggregate_copy(c)
                elu_exp(c - 1)
            elu_exp(NC - 1)

            def high1(n, bank):
                g = n % NC
                act.wait_ge(s_tr1, n + 1)
                act.activation(th[:, CW * g:CW * g + CW], ps[:, bank, :], ACT.Copy, scale=SX).then_inc(s_thi, 1)

            for g in range(NC):
                high1(g, 6 + g % 2)
            for g in range(NC):
                w = slice(CW * g, CW * g + CW)
                act.wait_ge(s_qr, g + 1)
                act.activation(q16[:, 0, w], rope[:, 2, :], ACT.Copy).then_inc(s_qhi, 1)
                act.wait_ge(s_vp, g + 1)
                act.activation(V[:, TPC * g:TPC * g + TPC, :].rearrange("p t d -> p (t d)"), ps[:, 4 + g % 2, 0:TPC * NKV * HD],
                               ACT.Copy, scale=1.0 / (SX * SW)).then_inc(s_V, 1)
                act.wait_ge(s_kr, g + 1)
                act.activation(k16[:, 0, w], rope[0:NKV * HD, 5, :], ACT.Copy).then_inc(s_khi, 1)

            for n, (c, j) in enumerate(steps):
                t0 = max(0, P * (j - TPC * c))
                for pair in range(2):
                    act.wait_ge(s_st, 2 * n + pair + 1)
                    if n >= 2:
                        act.wait_ge(s_pv, n - 1)
                    act.activation(Pb[:, n % 2, 2 * pair:2 * pair + 2, t0:CW], ps[:, 2 * pair:2 * pair + 2, t0:CW], ACT.Exp,
                                   scale=1.0 / (SQ * SQ * float(HD) ** 0.5)).then_inc(s_p, 1)
                if last_step(c, j):
                    act.wait_ge(s_pv, n + 1)
                    act.activation(o_sb, ps[:, 6, :], ACT.Copy).then_inc(s_od, 1)

            for g in range(NC):
                high1(NC + g, g % 2)
            act.wait_ge(s_rl, 1)
            act.activation(lg1[:, 2], lg1[:, 1], ACT.Exp).then_inc(s_re, 1)

            act.sem_inc(s_silu, 3)

            def silu(i, u):
                k = u % 3
                r = KS1[k][1]
                act.wait_ge(s_h1, 24 * i + u + 1)
                act.wait_ge(s_hh, 24 * i + u + 1)
                act.activation(silu_sb[0:r, k, :], ps[0:r, k, :], ACT.Silu, scale=1.0 / (SX * SW)).then_inc(s_silu, 1)

            def high_hidden(i, u):
                gg, k = u // 3, u % 3
                r = KS1[k][1]
                act.wait_ge(s_hh, 24 * i + u + 1 + 3)
                act.wait_ge(s_y1, 8 * i + gg + 1)
                act.activation(g_hi[0:r, gg % 4, k, :], g32[0:r, u % 6, :], ACT.Copy).then_inc(s_ghi, 1)

            silu(0, 0)
            for u in range(1, 24):
                silu(0, u)
                high_hidden(0, u - 1)
            with act.Fori(1, E1 // 2) as i:
                for u in range(24):
                    silu(i, u)
                    high_hidden(i, u - 1)
            high_hidden(E1 // 2 - 1, 23)

        @block.tensor
        def _(pe):
            def transpose_rows(g, bank):
                for q in range(TPC):
                    last = pe.transpose(ps[:, bank, P * q:P * q + P], xn[:, TPC * g + q, :], ident[:, :])
                last.then_inc(s_tr, 1)

            pe.wait_ge(s_const, 1)
            for g in range(NC):
                pe.wait_ge(s_xn, g + 1)
                transpose_rows(g, g)
            pe.wait_ge(s_first, 16 * len(first))
            for g in range(NC):
                pe.wait_ge(s_pre_ev, g + 1)
                pe.matmul(ps[:, 4 + g, :], wmat[:, 0, :], xT[:, CW * g:CW * g + CW], start=True, stop=True).then_inc(s_h2p, 1)
            for g in range(NC):
                pe.wait_ge(s_h2, g + 1)
                for q in range(TPC):
                    t = TPC * g + q
                    last = pe.matmul(ps[:, g, P * q:P * q + P], h2T[:, P * t:P * t + P], wmat[:, 1, :], start=True, stop=True)
                last.then_inc(s_gp, 1)
            for j in range(NT):
                if j == 0:
                    pe.wait_ge(s_G, NC)
                pe.wait_ge(s_F, j + 1)
                for c in range(NC):
                    last = pe.matmul(ps[:, c, :], G[:, j, :], fbuf[:, j % FB, CW * c:CW * c + CW],
                                     start=(j == 0), stop=(j == NT - 1))
                last.then_inc(s_aggp, 1)
                pe.wait_ge(s_mask, j + 1)
                for c in range(NC):
                    last = pe.matmul(ps[32 * c:32 * c + 32, 4, :], ones_b[:, :], mbuf[:, j % 2, CW * c:CW * c + CW],
                                     start=(j == 0), stop=(j == NT - 1))
                last.then_inc(s_cntp, 1)
            pe.wait_ge(s_cmax, 1)
            pe.transpose(ps[0:1, 6, 0:P], cnt[:, 0:1], ident[:, :]).then_inc(s_cmT, 1)
            with many_entries(pe):
                pe.sem_inc(g_mm, 2)
                pe.wait_ge(s_G, NC)
                agg = ps[:, 0:NC, :].rearrange("p c t -> p (c t)")
                with pe.Fori(0, NT) as i:
                    pe.wait_ge(g_row, i + 1)
                    for q in range(4):
                        for t in range(4 * q, 4 * q + 4):
                            last = pe.transpose(ps[:, 6 + q % 2, P * (t % 4):P * (t % 4) + P], e_row[:, P * t:P * t + P], ident[:, :])
                        last.then_inc(g_tr, 1)
                        pe.wait_ge(g_cp, 4 * i + q + 1)
                        for t in range(4 * q, 4 * q + 4):
                            last = pe.matmul(agg[:, bass.ds(P * i, P)], G[:, t, :], rT[:, q % 2, P * (t % 4):P * (t % 4) + P],
                                             start=(t == 0), stop=(t == NT - 1))
                        last.then_inc(g_mm, 1)
                pe.wait_ge(g_feat, NC)
            for g in range(NC):
                pe.wait_ge(s_feat, g + 1)
                if g == 0:
                    pe.wait_ge(s_flag, 1)
                if g >= 2:
                    pe.wait_ge(s_x1, g - 1)
                for q in range(TPC):
                    t = TPC * g + q
                    last = pe.transpose(ps[:, 6 + g % 2, P * q:P * q + P], xT[:, P * t:P * t + P], ident[:, :])
                last.then_inc(s_ftr, 1)
            def degrees():
                pe.wait_ge(s_asum, NT - 1)
                for t in range(NT):
                    last = pe.matmul(ps[:, 5, t:t + 1], asum[:, P * t:P * t + P], ones[:, 0:1], start=True, stop=True)
                last.then_inc(s_degc, 1)

            for g in range(NC):
                pe.wait_ge(s_xn, NC + g + 1)
                if g >= 2:
                    pe.wait_ge(s_xlo, g - 1)
                else:
                    pe.wait_ge(s_x1, NC - 1 + g)
                transpose_rows(g, 6 + g % 2)
            pe.wait_ge(s_wg, 1)
            for t in range(NT):
                if t % TPC == 0:
                    pe.wait_ge(s_xlo, t // TPC + 1)
                for n, (a, b) in enumerate(((xh, 0), (xl, 0), (xh, 1))):
                    last = pe.matmul(ps[:, 4, 8 * t:8 * t + 8], a[:, P * t:P * t + P], wg16[:, b, :], start=(n == 0), stop=(n == 2))
            last.then_inc(s_gate, 1)

            pe.sem_inc(s_y0, 4)

            def hidden(i, gg):
                s, g = gg // NC, gg % NC
                if g == 0:
                    if isinstance(i, int) and gg == 0:
                        pe.wait_ge(s_w00, 1)
                    else:
                        pe.wait_ge(s_w1s, 2 * i + s)
                for k in range(K0):
                    u = gg * K0 + k
                    pe.wait_ge(s_relu, 8 * K0 * i + u + 1)
                    for n, (w, a) in enumerate(((w1h, xh), (w1h, xl), (w1l, xh))):
                        last = pe.matmul(ps[:, H_BANKS[u % 4], :], w[:, s, P * k:P * k + P], a[:, CW * g:CW * g + CW],
                                         start=(n == 0), stop=(n == 2))
                    last.then_inc(s_h0, 1)

            def output(i, gg):
                s = gg // NC % 2
                if isinstance(i, int) and 8 * i + gg == 0:
                    pe.wait_ge(s_w00, 2)
                elif gg % NC == 0:
                    pe.wait_ge(s_w2, 2 * i + gg // NC)
                pe.wait_ge(s_hlo, 8 * K0 * i + (gg + 1) * K0 + 4)
                pe.wait_ge(s_add0, 8 * i + gg + 1)
                for q in range(TPC):
                    n = 0
                    for k in range(K0):
                        for a, w in ((hh_hi, w2h), (hh_hi, w2l), (hh_lo, w2h)):
                            last = pe.matmul(ps[:, 2 + gg % 2, P * q:P * q + P], a[:, gg % 4, k, P * q:P * q + P],
                                             w[:, s, k, :], start=(n == 0), stop=(n == 3 * K0 - 1))
                            n += 1
                last.then_inc(s_y0, 1)

            def bias2_transpose(half):
                pe.wait_ge(s_comb, 1)
                pe.wait_ge(s_degv, 1)
                if half:
                    pe.wait_ge(s_cTc, 1)
                for t in range(2 * TPC):
                    last = pe.transpose(ps[0:8, 4 + t // TPC, P * (t % TPC):P * (t % TPC) + P], comb[:, 2 * TPC * half + t, :],
                                        ident[:, :])
                last.then_inc(s_cT, 1)

            def bias2_product(half):
                pe.wait_ge(s_cTc, 2)
                if half:
                    pe.wait_ge(s_b2a, 1)
                for t in range(2 * TPC):
                    tt = 2 * TPC * half + t
                    last = pe.matmul(ps[:, 4 + t // TPC, P * (t % TPC):P * (t % TPC) + P], combT[:, P * tt:P * tt + P],
                                     b2_sb[:, :], start=True, stop=True)
                last.then_inc(s_b2, 1)

            for gg in range(2 * NC):
                hidden(0, gg)
                if gg >= 2:
                    output(0, gg - 2)
                if gg == 1:
                    degrees()
                if gg in (4, 5):
                    bias2_transpose(gg - 4)
                if gg in (6, 7):
                    bias2_product(gg - 6)
            with pe.Fori(1, E0 // 2) as i:
                for gg in range(2 * NC):
                    hidden(i, gg)
                    output(i, gg - 2)
            for gg in (2 * NC - 2, 2 * NC - 1):
                output(E0 // 2 - 1, gg)

            def aggregate(c):
                if c == 0:
                    pe.wait_ge(s_xn, 3 * NC)
                for j in range(NT):
                    if j // TPC == c:
                        q = j % TPC
                        pe.matmul(ps[:, c, P * q:P * q + P], G[:, j, :], ident[:, :], start=(j == 0), stop=False,
                                  skip_group_check=True)
                    last = pe.matmul(ps[:, c, :], G[:, j, :], A[:, j, CW * c:CW * c + CW],
                                     start=(j == 0 and c > 0), stop=(j == NT - 1), skip_group_check=True)
                last.then_inc(s_agg1, 1)

            def times_w(c):
                pe.wait_ge(s_hagg, c + 1)
                if c >= 2:
                    pe.wait_ge(s_x3, c - 1)
                for q in range(TPC):
                    last = pe.matmul(ps[:, 4 + c % 2, P * q:P * q + P], hagg[:, c % 2, P * q:P * q + P], wmat[:, 2, :],
                                     start=True, stop=True)
                last.then_inc(s_z, 1)

            aggregate(0)
            for c in range(1, NC):
                aggregate(c)
                times_w(c - 1)
            times_w(NC - 1)

            for g in range(NC):
                pe.wait_ge(s_hn, g + 1)
                if g >= 2:
                    pe.wait_ge(s_tlo, g - 1)
                for q in range(TPC):
                    last = pe.transpose(ps[:, 6 + g % 2, P * q:P * q + P], G[:, TPC * g + q, :], ident[:, :])
                last.then_inc(s_tr1, 1)

            def product3(dst, w0, w1, g):
                for n, (b, a) in enumerate(((0, th), (0, tl), (1, th))):
                    last = pe.matmul(dst, watt[:, b, w0:w1], a[:, CW * g:CW * g + CW], start=(n == 0), stop=(n == 2))
                return last

            pe.wait_ge(s_attws, 1)
            for g in range(NC):
                pe.wait_ge(s_tlo, g + 1)
                if g:
                    pe.wait_ge(s_qr, g)
                product3(ps[:, 0, :], WQ, WQR, g)
                product3(ps[:, 1, :], WQR, WK, g).then_inc(s_qp, 1)
                if g:
                    pe.wait_ge(s_kr, g)
                product3(ps[0:NKV * HD, 2, :], WK, WKR, g)
                product3(ps[0:NKV * HD, 3, :], WKR, WV, g).then_inc(s_kp, 1)
                if g >= 2:
                    pe.wait_ge(s_V, g - 1)
                for q in range(TPC):
                    t = TPC * g + q
                    for n, (a, b) in enumerate(((th, 0), (tl, 0), (th, 1))):
                        last = pe.matmul(ps[:, 4 + g % 2, NKV * HD * q:NKV * HD * (q + 1)], a[:, P * t:P * t + P],
                                         watt[:, b, WV:WR], start=(n == 0), stop=(n == 2))
                last.then_inc(s_vp, 1)

            filled = [0]

            def unit(what):
                n = filled[0]
                bank = 4 + n % 2
                if n >= 2:
                    pe.wait_ge(s_rmf, n - 1)
                if what[0] == "max":
                    _, t, h, b = what
                    if (t, h, b) == (2 * TPC, 0, 0):
                        pe.wait_ge(s_stack[1], 16 * 3 * (NH + NKV))
                    diagonal = b == t // TPC
                    width = P * (t % TPC + 1) if diagonal else CW
                    if diagonal:
                        pe.matmul(ps[:, bank, width - P:width], ident_b[:, :], mask_ts[:, :], start=True, stop=False,
                                  skip_group_check=True)
                    last = pe.matmul(ps[:, bank, 0:width], Qs[0:KQ, h, P * t:P * t + P],
                                     Ks[0:KQ, h // (NH // NKV), CW * b:CW * b + width], start=not diagonal, stop=True,
                                     skip_group_check=True)
                elif what[0] == "neg":
                    _, c, h = what
                    pe.wait_ge(s_m, c + 1)
                    for q in range(TPC):
                        last = pe.matmul(ps[KQ:KQ + 1, bank, P * q:P * q + P], m16[:, h, q:q + 1], ident_h[:, :],
                                         start=True, stop=True)
                else:
                    c = what[1]
                    pe.wait_ge(s_yT, c + 1)
                    for q in range(TPC):
                        t = TPC * c + q
                        last = pe.matmul(ps[:, bank, P * q:P * q + P], yT[:, P * t:P * t + P], wo32, start=True, stop=True)
                last.then_inc(s_rm, 1)
                filled[0] += 1

            def scores(n):
                c, j = steps[n]
                k = j - TPC * c
                t0 = max(0, P * k)
                if first_step(c, j):
                    pe.wait_ge(s_rmf, neg_done[c])
                for h in range(NH):
                    if h % 2 == 0 and n:
                        pe.wait_ge(s_p, 2 * (n - 1) + h // 2 + 1)
                    if k >= 0:
                        pe.matmul(ps[:, h, t0:t0 + P], ident_b[:, :], mask_st[:, :], start=True, stop=False,
                                  skip_group_check=True)
                    last = pe.matmul(ps[:, h, t0:CW], Ks[0:KQ + 1, h // (NH // NKV), P * j:P * j + P],
                                     Qs[0:KQ + 1, h, CW * c + t0:CW * c + CW], start=k < 0, stop=True, skip_group_check=True)
                    if h % 2:
                        last.then_inc(s_st, 1)

            def weigh(n):
                c, j = steps[n]
                t0 = max(0, P * (j - TPC * c))
                pe.wait_ge(s_p, 2 * n + 2)
                if first_step(c, j) and c:
                    pe.wait_ge(s_od, 2 * c)
                for bank in (6, 7):
                    for h in range(NH):
                        kv = h // (NH // NKV)
                        w = V[:, j, HD * kv:HD * kv + HD] if bank == 6 else ones[:, :]
                        last = pe.matmul(ps[HD * h:HD * h + HD, bank, t0:CW], w, Pb[:, n % 2, h, t0:CW],
                                         start=first_step(c, j), stop=last_step(c, j), skip_group_check=True)
                last.then_inc(s_pv, 1)

            pe.wait_ge(s_V, NC)
            pe.wait_ge(s_stack[0], 16 * 3 * (NH + NKV))
            pe.wait_ge(s_mc, 1)
            for what in max_units(0):
                unit(what)
            scores(0)
            for n, step in enumerate(steps):
                for what in units_at[step]:
                    unit(what)
                if n + 1 < len(steps):
                    scores(n + 1)
                weigh(n)
            unit(("out", NC - 1))

            for g in range(NC):
                pe.wait_ge(s_fn, g + 1)
                if g >= 2:
                    pe.wait_ge(s_tlo, NC + g - 1)
                for q in range(TPC):
                    last = pe.transpose(ps[:, g % 2, P * q:P * q + P], G[:, TPC * g + q, :], ident[:, :])
                last.then_inc(s_tr1, 1)
            for t in range(NT):
                if t % TPC == 0:
                    pe.wait_ge(s_tlo, NC + t // TPC + 1)
                for n, (a, b) in enumerate(((th, 0), (tl, 0), (th, 1))):
                    last = pe.matmul(ps[:, 6, 8 * t:8 * t + 8], a[:, P * t:P * t + P], watt[:, b, WR:WR + 8],
                                     start=(n == 0), stop=(n == 2))
            last.then_inc(s_rt, 1)

            pe.sem_inc(s_y1, 4)

            def hidden1(i, gg):
                s, g = gg // NC, gg % NC
                if g == 0:
                    pe.wait_ge(s_w13, 2 * i + s + 1)
                for k, (k0, r) in enumerate(KS1):
                    u = 3 * gg + k
                    for m, (free, ready) in enumerate(((s_silu, s_h1), (s_hh, s_h3))):
                        pe.wait_ge(free, 24 * i + u + 1)
                        for n, (w, a) in enumerate(((v13h, th), (v13h, tl), (v13l, th))):
                            last = pe.matmul(ps[0:r, 3 * m + k, :], w[:, s, m, k0:k0 + r], a[:, CW * g:CW * g + CW],
                                             start=(n == 0), stop=(n == 2))
                        last.then_inc(ready, 1)

            def output1(i, gg):
                s = gg // NC % 2
                if gg % NC == 0:
                    pe.wait_ge(s_w22, 2 * i + gg // NC + 1)
                pe.wait_ge(s_glo, 24 * i + 3 * (gg + 1) + 6)
                pe.wait_ge(s_add1, 8 * i + gg + 1)
                for q in range(TPC):
                    n = 0
                    for k, (_, r) in enumerate(KS1):
                        for a, w in ((g_hi, v2h), (g_hi, v2l), (g_lo, v2h)):
                            last = pe.matmul(ps[:, 6 + gg % 2, P * q:P * q + P], a[0:r, gg % 4, k, P * q:P * q + P],
                                             w[0:r, s, k, :], start=(n == 0), stop=(n == 8))
                            n += 1
                last.then_inc(s_y1, 1)

            hidden1(0, 0)
            for gg in range(1, 2 * NC):
                hidden1(0, gg)
                output1(0, gg - 1)
            with pe.Fori(1, E1 // 2) as i:
                for gg in range(2 * NC):
                    hidden1(i, gg)
                    output1(i, gg - 1)
            output1(E1 // 2 - 1, 2 * NC - 1)

        @block.vector
        def _(dve):
            chain = Chain(dve, s_dve)

            def rows(v, g):
                return v[:, TPC * g:TPC * g + TPC, :].rearrange("p a d -> p (a d)")

            def statistics(g, src):
                for t in range(TPC * g, TPC * g + TPC):
                    last = dve.bn_stats(bst[:, t, :], src[:, t, :])
                chain(last)
                for t in range(TPC * g, TPC * g + TPC):
                    last = dve.bn_aggr(mv[:, t, :], bst[:, t, :])
                chain(last)
                dve.tensor_scalar(ve[:, TPC * g:TPC * g + TPC], mv[:, TPC * g:TPC * g + TPC, 1], EPS_LN, None,
                                  ALU.add).then_inc(s_var, 1)

            def normalise(n, g, src, dst):
                dve.wait_ge(s_rstd, n)
                for t in range(TPC * g, TPC * g + TPC):
                    last = dve.tensor_scalar(dst[:, t, :], src[:, t, :], mv[:, t, 0:1], rstd[:, t:t + 1], ALU.subtract, ALU.mult)
                last.then_inc(s_xn, 1)

            for g in range(NC):
                dve.wait_ge(s_x[g], 16)
                statistics(g, x)
            for g in range(NC):
                normalise(g + 1, g, x, xn)
            for g in range(NC):
                dve.wait_ge(s_tr, g + 1)
                dve.tensor_copy(xT[:, CW * g:CW * g + CW], ps[:, g, :]).then_inc(s_pre_ev, 1)

            def square(j):
                dve.wait_ge(s_A[j], 16)
                if j >= FB:
                    dve.wait_ge(s_aggp, j - FB + 1)
                    dve.wait_ge(s_mask, j - FB + 1)
                dve.scalar_tensor_tensor(out=fbuf[:, j % FB, :], in0=A[:, j, :], scalar=0.0, in1=A[:, j, :],
                                         op0=ALU.max, op1=ALU.mult).then_inc(s_sq, 1)

            def mask(j):
                dve.wait_ge(s_F, j + 1)
                if j >= 2:
                    dve.wait_ge(s_cntp, j - 1)
                dve.tensor_scalar(mbuf[:, j % 2, :], fbuf[:, j % FB, :], 0.0, None, ALU.is_gt).then_inc(s_mask, 1)

            square(0)
            for g in range(NC):
                dve.wait_ge(s_gp, g + 1)
                dve.tensor_copy(rows(G, g), ps[:, g, :]).then_inc(s_G, 1)
            for j in range(1, NT):
                square(j)
                mask(j - 1)
            mask(NT - 1)
            dve.wait_ge(s_cntp, NT)
            dve.reduce_max(cnt[:, 0:1], ps[:, 4, :], AX_X).then_inc(s_cmax, 1)
            dve.wait_ge(s_cmT, 1)
            chain(dve.reduce_max(cnt[0:1, 1:2], ps[0:1, 6, 0:P], AX_X))
            dve.tensor_scalar(flag[:, :], cnt[0:1, 1:2], float(LIMIT), None, ALU.is_gt).then_inc(s_flag, 1)
            with many_entries(dve):
                W = 8
                B = 5
                step = Chain(dve, s_gen)
                dve.wait_ge(s_feat, NC)
                with dve.Fori(0, NT) as i:
                    step.turn(i, W + 31 * B)
                    dve.wait_ge(g_load, 16 * i + 16)
                    dve.scalar_tensor_tensor(out=f_row, in0=a_row, scalar=0.0, in1=a_row, op0=ALU.max, op1=ALU.mult).then_inc(g_sq, 1)
                    step(dve.memset(thr, 0))
                    dve.wait_ge(g_tanh, i + 1)
                    dve.memset(bit, 1 << 30).then_inc(s_gen, 1)
                    step.here += 1
                    with dve.Fori(0, 31) as b:
                        step.base = i * (W + 31 * B) + b * B
                        dve.wait_ge(s_gen, step.base + step.here)
                        step(dve.tensor_tensor(cand, thr, bit, ALU.bitwise_or))
                        step(dve.tensor_scalar(c_row, f_row, cand_f, 0.0, ALU.is_ge, ALU.add, accum_out=cnt_f))
                        step(dve.tensor_scalar(ge, cnt_f, float(TOP), -1.0, ALU.is_ge, ALU.mult))
                        step(dve.tensor_tensor(ge, ge, bit, ALU.bitwise_and))
                        dve.tensor_scalar(bit, bit, 1, None, ALU.logical_shift_right)
                        step(dve.tensor_tensor(thr, thr, ge, ALU.bitwise_or))
                    step.here -= B
                    step.base = i * (W + 31 * B) + 31 * B
                    step(dve.tensor_scalar(c_row, f_row, thr_f, 0.0, ALU.is_gt, ALU.add, accum_out=cnt_f))
                    step(dve.tensor_scalar(need_f, cnt_f, -1.0, float(TOP), ALU.mult, ALU.add))
                    step(dve.tensor_scalar(c_row, f_row, thr_f, None, ALU.is_equal))
                    dve.wait_ge(g_mm, 4 * i + 2)
                    step(dve.tensor_tensor_scan(e_row, c_row, c_row, 0.0, ALU.add, ALU.max))
                    step(dve.scalar_tensor_tensor(out=c_row, in0=e_row, scalar=need_f, in1=c_row, op0=ALU.is_le, op1=ALU.mult))
                    step(dve.scalar_tensor_tensor(out=c_row, in0=f_row, scalar=thr_f, in1=c_row, op0=ALU.is_gt, op1=ALU.add))
                    dve.tensor_tensor(e_row, f_row, c_row, ALU.mult).then_inc(g_row, 1)
                    dve.wait_ge(g_row, i + 1)
                    step.turn_ends(W)
            for g in range(NC):
                dve.wait_ge(s_ftr, g + 1)
                dve.tensor_tensor(x[:, TPC * g:TPC * g + TPC, :].rearrange("p a d -> p (a d)"), ps[:, 6 + g % 2, :],
                                  x[:, TPC * g:TPC * g + TPC, :].rearrange("p a d -> p (a d)"), ALU.add).then_inc(s_x1, 1)
                dve.wait_ge(s_x1, g + 1)
                statistics(g, x)
                if g:
                    normalise(NC + g, g - 1, x, xn)
            normalise(2 * NC, NC - 1, x, xn)

            def low_parts(n):
                g = n % NC
                dve.wait_ge(s_xhi, n + 1)
                dve.scalar_tensor_tensor(out=xl[:, CW * g:CW * g + CW], in0=ps[:, n % 2 + 6, :], scalar=SX,
                                         in1=xh[:, CW * g:CW * g + CW], op0=ALU.mult, op1=ALU.subtract).then_inc(s_xlo, 1)

            def split(hi, lo, src, scale):
                chain(dve.tensor_scalar(hi, src, scale, None, ALU.mult))
                return dve.scalar_tensor_tensor(out=lo, in0=src, scalar=scale, in1=hi, op0=ALU.mult, op1=ALU.subtract)

            dve.wait_ge(s_small, 16 * len(small))
            split(wg16[:, 0, :], wg16[:, 1, :], wg32[:, :], SW).then_inc(s_wg, 1)
            for g in range(NC):
                low_parts(g)
            dve.wait_ge(s_ld0[0], 48)
            dve.tensor_copy(b1[:, 0, :], st_b1[:, 0, :])
            dve.tensor_scalar(b1s[:, 0, :], st_b1[:, 0, :], SH, None, ALU.mult).then_inc(s_b1s, 1)
            split(w1h[:, 0], w1l[:, 0], st_w1[:, 0], SW).then_inc(s_w00, 1)
            split(w2h[:, 0], w2l[:, 0], st_w2[:, 0], SW).then_inc(s_w00, 1)
            dve.wait_ge(s_gate, 1)
            chain(dve.tensor_tensor(lg[:, 8, 0, :], gbias[:, 0, :], gbias[:, 1, :], ALU.add))
            dve.scalar_tensor_tensor(out=lg[:, 0], in0=ps[:, 4, 0:8 * NT].rearrange("p (t e) -> p t e", e=8),
                                     scalar=1.0 / (SX * SW), in1=lg[:, 8, 0, :].unsqueeze(1).broadcast_to([P, NT, 8]),
                                     op0=ALU.mult, op1=ALU.add).then_inc(s_logit, 1)
            dve.wait_ge(s_const, 2)
            dve.wait_ge(s_logit, 1)
            pick(chain, dve, 0, lg[:, 0], lg)

            dve.sem_inc(s_hlo, 4)
            dve.sem_inc(s_add0, 2)

            def low(i, gg):
                for k in range(K0):
                    u = gg * K0 + k
                    dve.wait_ge(s_relu, 8 * K0 * i + u + 1 + 4)
                    dve.wait_ge(s_y0, 8 * i + gg + 1)
                    dve.scalar_tensor_tensor(out=hh_lo[:, gg % 4, k, :], in0=h32[:, u % 4, :], scalar=SH,
                                             in1=hh_hi[:, gg % 4, k, :], op0=ALU.mult, op1=ALU.subtract).then_inc(s_hlo, 1)

            wcol = sm[:, 9:11, :]

            def weight_column(i, gg):
                s = gg // NC
                chain(dve.tensor_scalar(wcol[:, s, :], comb[:, :, bass.ds(2 * i + s, 1)].rearrange("p t a -> p (t a)"),
                                        1.0 / (SH * SW), None, ALU.mult))

            def add(i, gg):
                s, g = gg // NC % 2, gg % NC
                dve.wait_ge(s_y0, 8 * i + gg + 1 + 4)
                if not (isinstance(i, int) and 8 * i + gg == 0):
                    dve.wait_ge(s_add0, 8 * i + gg + 2)
                for q in range(TPC):
                    t = TPC * g + q
                    last = dve.scalar_tensor_tensor(out=x[:, t, :], in0=ps[:, 2 + gg % 2, P * q:P * q + P],
                                                    scalar=wcol[:, s, t:t + 1], in1=x[:, t, :], op0=ALU.mult, op1=ALU.add)
                last.then_inc(s_add0, 1)

            def statistics_of_gnn1(g):
                dve.wait_ge(s_add0, (E0 - 1) * NC + g + 1 + 2)
                statistics(g, x)

            def turn(i, first, last):
                for gg in range(2 * NC):
                    low(i, gg)
                    if first and gg == 0:
                        pick(chain, dve, 1, lg[:, 5], lg)
                        dve.tensor_tensor(sm[:, 2], sm[:, 1], sm[:, 0], ALU.subtract).then_inc(s_diff, 1)
                    if first and gg == 1:
                        dve.wait_ge(s_ediff, 1)
                        chain(dve.tensor_scalar(sm[:, 6], sm[:, 3], 1.0, None, ALU.add))
                        chain(dve.reciprocal(sm[:, 7], sm[:, 6]))
                        chain(dve.tensor_tensor(sm[:, 8], sm[:, 3], sm[:, 7], ALU.mult))
                        combine_weights(chain, dve, sm[:, 7], sm[:, 8], lg).then_inc(s_comb, 1)
                        dve.wait_ge(s_comb, 1)
                        dve.wait_ge(s_degc, 1)
                        dve.tensor_scalar(sm[:, 11, :], ps[:, 5, 0:NT], 1.0, None, ALU.add).then_inc(s_degv, 1)
                    if gg in (2, 6):
                        weight_column(i, gg - 2)
                    if not first or gg >= 2:
                        add(i, gg - 2)
                    if last and gg >= NC + 2:
                        statistics_of_gnn1(gg - 2 - NC)
                    if first and gg in (6, 7):
                        half = gg - 6
                        w = slice(2 * TPC * half, 2 * TPC * half + 2 * TPC)
                        dve.wait_ge(s_b2, half + 1)
                        dve.wait_ge(s_add0, gg - 1 + 2)
                        dve.tensor_tensor(x[:, w, :].rearrange("p t d -> p (t d)"), ps[:, 4:6, :].rearrange("p c t -> p (c t)"),
                                          x[:, w, :].rearrange("p t d -> p (t d)"), ALU.add).then_inc(s_b2a, 1)
                        dve.wait_ge(s_b2a, half + 1)

            turn(0, True, False)
            with dve.Fori(1, E0 // 2 - 1) as i:
                chain.turn(i - 1, 2)
                turn(i, False, False)
                chain.turn_ends(2)
            chain.loop_ends(E0 // 2 - 2, 2)
            turn(E0 // 2 - 1, False, True)
            for gg in (2 * NC - 2, 2 * NC - 1):
                add(E0 // 2 - 1, gg)
                statistics_of_gnn1(gg - NC)

            for g in range(NC):
                dve.wait_ge(s_rstd, 2 * NC + g + 1)
                for t in range(TPC * g, TPC * g + TPC):
                    last = dve.tensor_scalar(G[:, t, :], x[:, t, :], mv[:, t, 0:1], rd[:, t:t + 1], ALU.subtract, ALU.mult)
                last.then_inc(s_xn, 1)

            dve.wait_ge(s_attw, 16 * (2 * NH + 5))
            for src, ln, a, b in ((wq32, 2, WQ, WQR), (wk32, 2, WK, WKR), (wv32, 2, WV, WR), (wr32, 3, WR, WR + 8)):
                chain(dve.tensor_scalar(src, src, cols[:, ln:ln + 1], SW, ALU.mult, ALU.mult))
                chain(split(watt[:, 0, a:b], watt[:, 1, a:b], src, 1.0))
            for part in range(2):
                for a, b, n in ((WQ, WQR, NH), (WK, WKR, NKV)):
                    w = HD * n
                    src = watt[:, part, a:a + w].rearrange("p (h s d) -> p h s d", h=n, s=2)
                    dst = watt[:, part, b:b + w].rearrange("p (h s d) -> p h s d", h=n, s=2)
                    dve.tensor_scalar(dst[:, :, 0, :], src[:, :, 1, :], -1.0, None, ALU.mult)
                    last = dve.tensor_copy(dst[:, :, 1, :], src[:, :, 0, :])
            last.then_inc(s_attws, 1)

            for c in range(NC):
                dve.wait_ge(s_z, c + 1)
                if c >= 2:
                    dve.wait_ge(s_x3, c - 1)
                for q in range(TPC):
                    t = TPC * c + q
                    last = dve.tensor_scalar(zs[:, c % 2, P * q:P * q + P], ps[:, 4 + c % 2, P * q:P * q + P], dis[:, t:t + 1],
                                             None, ALU.mult)
                chain(last)
                if c >= 2:
                    dve.wait_ge(s_ez, c - 1)
                dve.tensor_scalar(ez[:, c % 2, :], zs[:, c % 2, :], 0.0, None, ALU.min).then_inc(s_zn, 1)
                chain(dve.scalar_tensor_tensor(out=rows(x, c), in0=zs[:, c % 2, :], scalar=0.0, in1=rows(x, c), op0=ALU.max, op1=ALU.add))
                dve.wait_ge(s_ez, c + 1)
                dve.scalar_tensor_tensor(out=rows(x, c), in0=ez[:, c % 2, :], scalar=-1.0, in1=rows(x, c), op0=ALU.add,
                                         op1=ALU.add).then_inc(s_x3, 1)
                dve.wait_ge(s_x3, c + 1)
                statistics(c, x)

            for g in range(NC):
                normalise(3 * NC + g + 1, g, x, xn)
                for t in range(TPC * g, TPC * g + TPC):
                    last = dve.tensor_scalar(G[:, t, :], x[:, t, :], mv[:, t, 0:1], rd[:, t:t + 1], ALU.subtract, ALU.mult)
                last.then_inc(s_hn, 1)

            def low1(n, bank):
                g = n % NC
                dve.wait_ge(s_thi, n + 1)
                dve.scalar_tensor_tensor(out=tl[:, CW * g:CW * g + CW], in0=ps[:, bank, :], scalar=SX,
                                         in1=th[:, CW * g:CW * g + CW], op0=ALU.mult, op1=ALU.subtract).then_inc(s_tlo, 1)

            for g in range(NC):
                low1(g, 6 + g % 2)
            for g in range(NC):
                w = slice(CW * g, CW * g + CW)
                for (bank, parts, b0, ready, done, hi_done, lo_done, dst) in (
                        (0, P, 0, s_qp, s_qr, s_qhi, s_qlo, q16), (2, NKV * HD, 3, s_kp, s_kr, s_khi, s_klo, k16)):
                    dve.wait_ge(ready, g + 1)
                    for n, table in enumerate((cos_sb, sin_sb)):
                        last = dve.scalar_tensor_tensor(out=rope[0:parts, b0 + n, :], in0=ps[0:parts, bank + n, :],
                                                        scalar=SQ / (SX * SW), in1=table[0:parts, w], op0=ALU.mult, op1=ALU.mult)
                    chain(last)
                    dve.tensor_tensor(rope[0:parts, b0 + 2, :], rope[0:parts, b0, :], rope[0:parts, b0 + 1, :],
                                      ALU.add).then_inc(done, 1)
                for (parts, b0, hi_done, lo_done, dst) in ((P, 0, s_qhi, s_qlo, q16), (NKV * HD, 3, s_khi, s_klo, k16)):
                    dve.wait_ge(hi_done, g + 1)
                    dve.tensor_tensor(dst[:, 1, w], rope[0:parts, b0 + 2, :], dst[:, 0, w], ALU.subtract).then_inc(lo_done, 1)
                dve.wait_ge(s_klo, g + 1)

            read = [0]

            def unit(what):
                n = read[0]
                bank = 4 + n % 2
                dve.wait_ge(s_rm, n + 1)
                if what[0] == "max":
                    _, t, h, b = what
                    width = P * (t % TPC + 1) if b == t // TPC else CW
                    dve.reduce_max(pm[:, h, t % TPC, b:b + 1], ps[:, bank, 0:width], AX_X).then_inc(s_rmf, 1)
                elif what[0] == "neg":
                    _, c, h = what
                    dve.tensor_copy(Qs[KQ:KQ + 1, h, CW * c:CW * c + CW], ps[KQ:KQ + 1, bank, :]).then_inc(s_rmf, 1)
                else:
                    c = what[1]
                    dve.tensor_tensor(rows(xn, c), ps[:, bank, :], rows(xn, c), ALU.add).then_inc(s_rmf, 1)
                read[0] += 1
                last_max = ("max", what[1], NH - 1, what[1] // TPC) if what[0] == "max" else None
                if what == last_max and what[1] % TPC == TPC - 1:
                    c = what[1] // TPC
                    dve.wait_ge(s_rmf, n + 1)
                    chain(dve.reduce_max(m32[:, :, :], pm[:, :, :, 0:c + 1], AX_X))
                    dve.tensor_scalar(m16[:, :, :], m32[:, :, :], -1.0 / 16.0, None, ALU.mult).then_inc(s_m, 1)
                    dve.wait_ge(s_m, c + 1)

            for what in max_units(0):
                unit(what)
            for n, (c, j) in enumerate(steps):
                for what in units_at[(c, j)]:
                    unit(what)
                if last_step(c, j):
                    dve.wait_ge(s_pv, n + 1)
                    dve.tensor_copy(d_sb, ps[:, 7, :]).then_inc(s_od, 1)
                    dve.wait_ge(s_od, 2 * c + 2)
                    chain(dve.reciprocal(r_sb, d_sb))
                    dve.tensor_tensor(yT[:, CW * c:CW * c + CW], o_sb, r_sb, ALU.mult).then_inc(s_yT, 1)
                    dve.wait_ge(s_yT, c + 1)
            unit(("out", NC - 1))
            dve.wait_ge(s_rmf, read[0])

            for g in range(NC):
                w = slice(TPC * g, TPC * g + TPC)
                for t in range(TPC * g, TPC * g + TPC):
                    last = dve.bn_stats(bst[:, t, :], xn[:, t, :])
                chain(last)
                for t in range(TPC * g, TPC * g + TPC):
                    last = dve.bn_aggr(mv[:, t, :], bst[:, t, :])
                chain(last)
                chain(dve.tensor_tensor(ve[:, w], mv[:, w, 0], mv[:, w, 0], ALU.mult))
                dve.scalar_tensor_tensor(out=ve[:, w], in0=ve[:, w], scalar=EPS_RMS, in1=mv[:, w, 1], op0=ALU.add,
                                         op1=ALU.add).then_inc(s_ms, 1)
            for g in range(NC):
                dve.wait_ge(s_r2, g + 1)
                for t in range(TPC * g, TPC * g + TPC):
                    last = dve.tensor_scalar(G[:, t, :], xn[:, t, :], rd[:, t:t + 1], None, ALU.mult)
                last.then_inc(s_fn, 1)
            for g in range(NC):
                low1(NC + g, g % 2)

            chain(dve.tensor_tensor(x[:, :, :].rearrange("p t d -> p (t d)"), x[:, :, :].rearrange("p t d -> p (t d)"),
                                    xn[:, :, :].rearrange("p t d -> p (t d)"), ALU.add))
            bc = lambda v: v.unsqueeze(2).broadcast_to([P, NT, 8])
            dve.wait_ge(s_rt, 1)
            chain(dve.tensor_scalar(lg1[:, 0], ps[:, 6, 0:8 * NT].rearrange("p (t e) -> p t e", e=8), 1.0 / (SX * SW), None, ALU.mult))
            chain(dve.reduce_max(sm[:, 0], lg1[:, 0], AX_X))
            dve.tensor_tensor(lg1[:, 1], lg1[:, 0], bc(sm[:, 0]), ALU.subtract).then_inc(s_rl, 1)
            dve.wait_ge(s_re, 1)
            chain(dve.reduce_sum(sm[:, 6], lg1[:, 2], AX_X))
            chain(dve.reciprocal(sm[:, 7], sm[:, 6]))
            chain(dve.tensor_tensor(lg1[:, 0], lg1[:, 2], bc(sm[:, 7]), ALU.mult))
            pick(chain, dve, 0, lg1[:, 0], lg1)
            pick(chain, dve, 1, lg1[:, 5], lg1)
            chain(dve.tensor_tensor(sm[:, 2], sm[:, 0], sm[:, 1], ALU.add))
            chain(dve.tensor_scalar(sm[:, 2], sm[:, 2], 1e-9, None, ALU.add))
            chain(dve.reciprocal(sm[:, 3], sm[:, 2]))
            chain(dve.tensor_tensor(sm[:, 6], sm[:, 0], sm[:, 3], ALU.mult))
            chain(dve.tensor_tensor(sm[:, 7], sm[:, 1], sm[:, 3], ALU.mult))
            combine_weights(chain, dve, sm[:, 6], sm[:, 7], lg1).then_inc(s_comb1, 1)
            dve.wait_ge(s_comb1, 1)

            dve.sem_inc(s_hh, 3)
            dve.sem_inc(s_glo, 6)
            dve.sem_inc(s_add1, 2)

            def hidden(i, u):
                k = u % 3
                r = KS1[k][1]
                dve.wait_ge(s_silu, 24 * i + u + 1 + 3)
                dve.wait_ge(s_h3, 24 * i + u + 1)
                dve.wait_ge(s_glo, 24 * i + u + 1)
                dve.scalar_tensor_tensor(out=g32[0:r, u % 6, :], in0=ps[0:r, 3 + k, :], scalar=SH / (SX * SW),
                                         in1=silu_sb[0:r, k, :], op0=ALU.mult, op1=ALU.mult).then_inc(s_hh, 1)

            def low_hidden(i, u):
                gg, k = u // 3, u % 3
                r = KS1[k][1]
                dve.wait_ge(s_ghi, 24 * i + u + 1)
                dve.tensor_tensor(g_lo[0:r, gg % 4, k, :], g32[0:r, u % 6, :], g_hi[0:r, gg % 4, k, :],
                                  ALU.subtract).then_inc(s_glo, 1)

            def add1(i, gg):
                s, g = gg // NC % 2, gg % NC
                if g == 0:
                    weight_column(i, gg)
                dve.wait_ge(s_y1, 8 * i + gg + 1 + 4)
                dve.wait_ge(s_add1, 8 * i + gg + 2)
                for q in range(TPC):
                    t = TPC * g + q
                    last = dve.scalar_tensor_tensor(out=x[:, t, :], in0=ps[:, 6 + gg % 2, P * q:P * q + P],
                                                    scalar=wcol[:, s, t:t + 1], in1=x[:, t, :], op0=ALU.mult, op1=ALU.add)
                last.then_inc(s_add1, 1)

            def turn1(i, first):
                for u in range(24):
                    hidden(i, u)
                    if u or not first:
                        low_hidden(i, u - 1)
                    if u % 3 == 0 and (u // 3 >= 2 or not first):
                        add1(i, u // 3 - 2)

            turn1(0, True)
            with dve.Fori(1, E1 // 2) as i:
                chain.turn(i - 1, 2)
                turn1(i, False)
                chain.turn_ends(2)
            chain.loop_ends(E1 // 2 - 1, 2)
            low_hidden(E1 // 2 - 1, 23)
            add1(E1 // 2 - 1, 2 * NC - 2)
            add1(E1 // 2 - 1, 2 * NC - 1)


_NAMES = ["x_in", "adj_t", "adj_in", "w_proj", "b_proj", "w_gcn", "b_gcn", "f0_wg", "f0_bg", "f0_bias", "f0_w1", "f0_b1",
          "f0_w2", "f0_b2", "g1_w", "ln1", "ln2", "wq", "wk", "wv", "wo", "w_router", "f1_w1", "f1_w2", "f1_w3",
          "cos_t", "sin_t"]


def lay_out(a):
    import numpy as np

    def rows(v):
        return v.reshape(NT, P, -1).transpose(1, 0, 2)

    freq = np.float32(1.0) / np.float32(10000.0) ** (np.arange(0, HD, 2, dtype=np.float32) / HD)
    emb = np.outer(np.arange(T, dtype=np.float32), np.concatenate([freq, freq]))
    col = lambda v: v.reshape(P, 1)
    d = {
        "x_in": rows(a["x"]), "adj_t": a["adj"].T.reshape(NT, P, T), "adj_in": a["adj"].reshape(NT, P, T),
        "w_proj": a["L0_gnn_W_proj"], "b_proj": col(a["L0_gnn_b_proj"]), "w_gcn": a["L0_gnn_W_gcn"],
        "b_gcn": col(a["L0_gnn_b_gcn"]), "f0_wg": a["L0_ffn_Wg"], "f0_bg": a["L0_ffn_bg"], "f0_bias": a["L0_ffn_bias"],
        "f0_w1": a["L0_ffn_W1"], "f0_b1": a["L0_ffn_b1"].reshape(E0, K0, P).transpose(0, 2, 1),
        "f0_w2": a["L0_ffn_W2"].reshape(E0, K0, P, D).transpose(0, 2, 1, 3), "f0_b2": a["L0_ffn_b2"],
        "g1_w": a["L1_gnn_w"], "ln1": col(a["L1_ffn_ln1_w"]), "ln2": col(a["L1_ffn_ln2_w"]),
        "wq": a["L1_ffn_wq"].T, "wk": a["L1_ffn_wk"].T, "wv": a["L1_ffn_wv"].T, "wo": a["L1_ffn_wo"].T,
        "w_router": a["L1_ffn_router_w"].T, "f1_w1": a["L1_ffn_w1"].transpose(0, 2, 1),
        "f1_w2": a["L1_ffn_w2"].transpose(0, 2, 1), "f1_w3": a["L1_ffn_w3"].transpose(0, 2, 1),
        "cos_t": np.cos(emb).T, "sin_t": np.sin(emb).T,
    }
    return {k: np.ascontiguousarray(v) for k, v in d.items()}


def kernel(**inputs):
    import numpy as np
    import concourse.bacc as bacc
    from concourse.bass_utils import run_bass_kernel_spmd

    arrays = lay_out({k: np.asarray(v) for k, v in inputs.items()})
    nc = bacc.Bacc("TRN2", target_bir_lowering=False, num_devices=1)
    args = [nc.dram_tensor(f"in_{n}", arrays[n].shape, mybir.dt.from_np(arrays[n].dtype), kind="ExternalInput").ap()
            for n in _NAMES]
    args.append(nc.dram_tensor("out", (P, NT, D), F32, kind="ExternalOutput").ap())
    program(nc, *args)
    r = run_bass_kernel_spmd(nc, [{f"in_{n}": arrays[n] for n in _NAMES}], core_ids=[0])
    return np.ascontiguousarray(r.results[0]["out"].transpose(1, 0, 2).reshape(T, D))
```

```python
from contextlib import ExitStack

import concourse.bass as bass
from concourse import mybir

F32 = mybir.dt.float32
F16 = mybir.dt.float16
BF16 = mybir.dt.bfloat16
I32 = mybir.dt.int32
ALU = mybir.AluOpType
ACT = mybir.ActivationFunctionType
AX_X = mybir.AxisListType.X

P = 128
T = 2048
D = 128
NT = T // P
CW = 512
NC = T // CW
TPC = CW // P
NEG = -1e30

TOP = 350
LIMIT = TOP
EPS_LN = 1e-5
EPS_RMS = 1e-6
E0 = 8
H0 = 256
K0 = H0 // P
E1 = 8
H1 = 341
KS1 = [(0, 128), (128, 128), (256, 85)]
NH = 4
NKV = 2
HD = 32

SX = 32.0
SW = 256.0
SH = 8.0
SQ = 8.0


class Chain:

    def __init__(self, eng, sem):
        self.eng, self.sem, self.done, self.here = eng, sem, 0, 0
        self.base = 0

    def __call__(self, ins):
        ins.then_inc(self.sem, 1)
        self.here += 1
        self.eng.wait_ge(self.sem, self.base + self.here)

    def turn(self, i, per):
        if self.here:
            self.done += self.here
            self.here = 0
        self.base = i * per + self.done

    def turn_ends(self, per):
        assert self.here == per, (self.here, per)
        self.here = 0

    def loop_ends(self, turns, per):
        self.done += turns * per
        self.base = self.done


def program(nc, x_in, adj_t, adj_in, w_proj, b_proj, w_gcn, b_gcn, f0_wg, f0_bg, f0_bias, f0_w1, f0_b1,
            f0_w2, f0_b2, g1_w, ln1, ln2, wq, wk, wv, wo, w_router, f1_w1, f1_w2, f1_w3, cos_t, sin_t, out):
    with ExitStack() as ctx:
        def sb(name, shape, dt=F32):
            return ctx.enter_context(nc.sbuf_tensor(name, shape, dt))

        def sem(name):
            return ctx.enter_context(nc.semaphore(name))

        A = sb("A", [P, NT, T])
        x = sb("x", [P, NT, D])
        xn = sb("xn", [P, NT, D])
        G = sb("G", [P, NT, D])
        R = sb("R", [P, 5 * T])
        xT = sb("xT", [P, T])
        ident = sb("ident", [P, P])
        ones = sb("ones", [P, 32])
        ones_b = sb("ones_b", [P, 32], BF16)
        neg_half = sb("neg_half", [P, NT])
        rev = sb("rev", [P, NT, 8])
        wmat = sb("wmat", [P, 3, P])
        cols = sb("cols", [P, 8])
        wg32 = sb("wg32", [P, 8])
        wg16 = sb("wg16", [P, 2, 8], F16)
        gbias = sb("gbias", [P, 2, 8])
        b2_sb = sb("b2_sb", [8, D])
        bst = sb("bst", [P, NT, 6])
        mv = sb("mv", [P, NT, 2])
        ve = sb("ve", [P, NT])
        rstd = sb("rstd", [P, NT])
        rd = sb("rd", [P, NT])
        dis = sb("dis", [P, NT])
        lg = xT[:, 0:10 * NT * 8].rearrange("p (n t e) -> p n t e", n=10, e=8)
        sm = sb("sm", [P, 12, NT])
        comb = sb("comb", [P, NT, 8])
        cnt = sb("cnt", [P, 4])
        factor = sb("factor", [P, 4])
        st_b1 = sb("st_b1", [P, 2, K0])
        b1 = sb("b1", [P, 2, K0])
        b1s = sb("b1s", [P, 2, K0])
        flag = sb("flag", [1, 1], I32)

        FB = 3
        fbuf = R[:, 0:FB * T].rearrange("p (b t) -> p b t", b=FB)
        mbuf = R[:, FB * T:(FB + 1) * T].bitcast(BF16).rearrange("p (b t) -> p b t", b=2)
        h2T = R[:, 4 * T:5 * T]
        asum = h2T
        a_row, f_row, e_row, c_row = (R[:, n * T:(n + 1) * T] for n in range(4))
        rT = xT[:, 0:2 * CW].rearrange("p (b t) -> p b t", b=2)
        gen = xT[:, 2 * CW:2 * CW + 8]
        thr, bit, cand, ge = (gen[:, n:n + 1].bitcast(I32) for n in range(4))
        thr_f, cand_f, cnt_f, need_f = gen[:, 0:1], gen[:, 2:3], gen[:, 4:5], gen[:, 5:6]
        st_w1 = R[:, 0:512].rearrange("p (s h) -> p s h", s=2)
        st_w2 = R[:, 512:1024].rearrange("p (s k d) -> p s k d", s=2, k=K0)
        w1h = R[:, 1024:1280].bitcast(F16).rearrange("p (s h) -> p s h", s=2)
        w1l = R[:, 1280:1536].bitcast(F16).rearrange("p (s h) -> p s h", s=2)
        w2h = R[:, 1536:1792].bitcast(F16).rearrange("p (s k d) -> p s k d", s=2, k=K0)
        w2l = R[:, 1792:2048].bitcast(F16).rearrange("p (s k d) -> p s k d", s=2, k=K0)
        h32 = R[:, 2048:2048 + 4 * CW].rearrange("p (b t) -> p b t", b=4)
        o = 2048 + 4 * CW
        hh_hi = R[:, o:o + 4 * K0 * CW // 2].bitcast(F16).rearrange("p (b k t) -> p b k t", b=4, k=K0)
        o += 2 * K0 * CW
        hh_lo = R[:, o:o + 4 * K0 * CW // 2].bitcast(F16).rearrange("p (b k t) -> p b k t", b=4, k=K0)
        o += 2 * K0 * CW
        combT = xT[0:8, :]
        G16 = G[:, :, :].rearrange("p t d -> p (t d)").bitcast(F16)
        xh, xl = G16[:, 0:T], G16[:, T:2 * T]
        assert o <= 5 * T

        hagg = R[:, 0:2 * CW].rearrange("p (b t) -> p b t", b=2)
        zs = R[:, 2 * CW:4 * CW].rearrange("p (b t) -> p b t", b=2)
        ez = R[:, 4 * CW:6 * CW].rearrange("p (b t) -> p b t", b=2)
        frow = R[:, 6 * CW:8 * CW].rearrange("p (b t) -> p b t", b=2)
        cos_sb = R[:, 2 * T:3 * T]
        sin_sb = R[:, 3 * T:4 * T]
        o = 4 * T
        wq32, wk32, wv32, wo32, wr32 = (R[:, o + a:o + b] for a, b in ((0, 128), (128, 192), (192, 256), (256, 384), (384, 392)))
        o += 392
        watt = R[:, o:o + 456].bitcast(F16).rearrange("p (s n) -> p s n", s=2)
        WQ, WQR, WK, WKR, WV, WR = 0, 128, 256, 320, 384, 448
        o += 456
        A16 = A[:, :, :].bitcast(F16)
        KQ = 3 * HD

        def slot(c, j, n=1):
            return A[:, j:j + n, CW * c:CW * c + CW]

        def half(c, j, k):
            return A16[:, j, 2 * CW * c + CW * k:2 * CW * c + CW * k + CW]

        def queries(c, h):
            return half(c, h // 2, h % 2)

        def keys(c, kv):
            return half(c, 2, kv)

        def values(t, kv):
            o = CW * (t // TPC) + NKV * HD * (t % TPC) + HD * kv
            return A[:, 3, o:o + HD]

        def q16(c, part):
            return half(c, 4, part)

        def k16(c, part):
            return half(c, 5, part)[0:NKV * HD]

        rope = slot(0, 6, 6)
        yT = slot(1, 6, 4)
        r_sb = A[:, 12, CW:2 * CW]
        o_sb = [A[:, j, CW * c:CW * c + CW] for c, j in ((1, 10), (1, 13), (1, 15), (3, 14))]
        d_sb = [A[:, j, CW * c:CW * c + CW] for c, j in ((1, 11), (1, 14), (0, 14), (3, 15))]
        Pb = slot(3, 6, 8).rearrange("p (b h) t -> p b h t", b=2)
        o = 0
        pm = A[:, 15, o:o + NH * TPC * NC].rearrange("p (h q b) -> p h q b", h=NH, q=TPC)
        o += NH * TPC * NC
        m32 = A[:, 15, o:o + 16].rearrange("p (h q) -> p h q", h=NH)
        m16 = A[:, 15, o + 16:o + 24].bitcast(F16).rearrange("p (h q) -> p h q", h=NH)
        o = 4 * T + 848
        ident_b = R[:, o:o + 64].bitcast(BF16)
        ident_h = R[:, o + 64:o + 128].bitcast(F16)
        mask_ts = R[:, o + 128:o + 192].bitcast(BF16)
        mask_st = R[:, o + 192:o + 256].bitcast(BF16)
        v13 = A[:, 6:10, 2 * CW:2 * CW + H1].rearrange("p (s m) h -> p s m h", s=2)
        v2 = A[:, 10:12, 2 * CW:2 * CW + 3 * D].rearrange("p s (k d) -> p s k d", k=3)
        v13h = A16[:, 12:16, 4 * CW:4 * CW + H1].rearrange("p (s m) h -> p s m h", s=2)
        v13l = A16[:, 12:16, 5 * CW:5 * CW + H1].rearrange("p (s m) h -> p s m h", s=2)
        v2h = A16[:, 12:14, 0:3 * D].rearrange("p s (k d) -> p s k d", k=3)
        v2l = A16[:, 12:14, CW:CW + 3 * D].rearrange("p s (k d) -> p s k d", k=3)
        silu_sb = slot(0, 6, 3)
        g32 = slot(0, 0, 6)

        def g_hi(b, k):
            n = 3 * b + k
            return half(3, 6 + n // 2, n % 2)

        def g_lo(b, k):
            n = 3 * b + k
            return half(3, n // 2, n % 2)

        xT16 = xT[:, :].bitcast(F16)
        lg1 = R[:, 2 * T:2 * T + 10 * NT * 8].rearrange("p (n t e) -> p n t e", n=10, e=8)
        th, tl = xT16[:, 0:T], xT16[:, T:2 * T]

        ps = ctx.enter_context(nc.psum_tensor("ps", [P, 8, CW], F32))

        s_x = [sem(f"x_chunk{g}_loaded") for g in range(NC)]
        s_first = sem("first_operands_loaded")
        s_small = sem("small_loaded")
        s_A = [sem(f"adj_tile_{j}_loaded") for j in range(NT)]
        s_const = sem("constants_made")
        s_cpool = sem("pool_steps")
        s_dve = sem("vector_steps")
        s_acts = sem("scalar_steps")
        s_var = sem("variance_ready")
        s_rstd = sem("rstd_ready")
        s_xn = sem("rows_normalised")
        s_tr = sem("rows_transposed")
        s_pre_ev = sem("transposed_copied")
        s_h2p = sem("h2_product")
        s_h2 = sem("h2_ready")
        s_gp = sem("g_product")
        s_G = sem("g_ready")
        s_sq = sem("square_ready")
        s_F = sem("filtered_ready")
        s_mask = sem("mask_ready")
        s_cntp = sem("tile_counted")
        s_aggp = sem("tile_aggregated")
        s_cmax = sem("count_max_ready")
        s_cmT = sem("count_max_transposed")
        s_flag = sem("flag_ready")
        s_feat = sem("features_ready")
        s_ftr = sem("features_transposed")
        s_x1 = sem("gnn0_added")
        s_asum = sem("adj_tiles_summed")
        s_degc = sem("deg_columns")
        s_degv = sem("deg_plus_one")
        s_dis = sem("deg_isqrt_ready")
        s_xhi = sem("x_high_ready")
        s_xlo = sem("x_low_ready")
        s_wg = sem("gate_weights_split")
        s_gate = sem("gate_product")
        s_diff = sem("top_difference_ready")
        s_ediff = sem("exp_difference_ready")
        s_comb = sem("combine_weights_ready")
        s_ld0 = [sem(f"expert0_weights_slot{i}") for i in range(2)]
        s_w1s = sem("expert0_first_weights_split")
        s_w2 = sem("expert0_second_weights_split")
        s_w00 = sem("expert0_number0_split")
        s_h0 = sem("hidden0_product")
        s_relu = sem("hidden0_relu")
        s_hhi = sem("hidden0_high")
        s_hlo = sem("hidden0_low")
        s_y0 = sem("expert0_output")
        s_add0 = sem("expert0_added")
        s_cT = sem("combine_transposed")
        s_cTc = sem("combine_transposed_copied")
        s_b2 = sem("bias2_product")
        s_b2a = sem("bias2_added")
        s_b1s = sem("first_bias_scaled")
        s_logit = sem("gate_logits_ready")
        s_out = sem("output_stored")
        g_load = sem("general_rows_loaded")
        g_sq = sem("general_squares")
        g_tanh = sem("general_filtered")
        g_row = sem("general_rows_selected")
        g_tr = sem("general_transposed")
        g_cp = sem("general_transposed_copied")
        g_feat = sem("general_features_ready")
        g_mm = sem("general_multiplied")
        s_gen = sem("general_vector_steps")
        s_agg1 = sem("gnn1_aggregated")
        s_hagg = sem("gnn1_aggregate_copied")
        s_z = sem("gnn1_product")
        s_zn = sem("gnn1_negative_part")
        s_ez = sem("gnn1_exp_ready")
        s_x3 = sem("gnn1_added")
        s_attw = sem("attention_weights_loaded")
        s_attws = sem("attention_weights_split")
        s_hn = sem("attention_rows_ready")
        s_qp = sem("query_product")
        s_kp = sem("key_product")
        s_vp = sem("value_product")
        s_qr = sem("query_rotated")
        s_kr = sem("key_rotated")
        s_qhi = sem("query_high_ready")
        s_khi = sem("key_high_ready")
        s_V = sem("values_ready")
        s_qlo = sem("query_low_ready")
        s_klo = sem("key_low_ready")
        s_mc = sem("masks_made")
        s_stack = [sem(f"queries_keys_stacked_chunk{i}") for i in range(NC)]
        s_rm = sem("row_max_bank_filled")
        s_rmf = sem("row_max_bank_read")
        s_m = sem("row_max_ready")
        s_st = sem("scores_ready")
        s_p = sem("probabilities_ready")
        s_pv = sem("probabilities_used")
        s_od = sem("attention_sums_copied")
        s_yT = sem("attention_output_ready")
        s_x4 = sem("attention_added")
        s_ms = sem("mean_square_ready")
        s_r2 = sem("rms_ready")
        s_fn = sem("router_rows_ready")
        s_tr1 = sem("layer1_rows_transposed")
        s_thi = sem("layer1_high_ready")
        s_tlo = sem("layer1_low_ready")
        s_route = sem("router_steps")
        s_re = sem("router_exp_ready")
        s_ld1 = [sem(f"expert1_weights_slot{i}") for i in range(2)]
        s_w13 = sem("expert1_first_weights_split")
        s_w22 = sem("expert1_second_weights_split")
        s_tail = sem("expert1_tail_rows_cleared")
        s_h1 = sem("gate_unit_product")
        s_h3 = sem("up_unit_product")
        s_silu = sem("silu_ready")
        s_hh = sem("hidden1_ready")
        s_ghi = sem("hidden1_high")
        s_glo = sem("hidden1_low")
        s_y1 = sem("expert1_output")
        s_add1 = sem("expert1_added")

        steps = [(c, j) for c in range(NC) for j in [*range(TPC * c + TPC - 1, TPC * c - 1, -1), *range(TPC * c)]]

        def first_step(c, j):
            return j == TPC * c + TPC - 1

        def last_step(c, j):
            return j == (TPC * c - 1 if c else 0)

        def max_units(c):
            return [("max", t, h, b) for t in range(TPC * c, TPC * c + TPC) for h in range(NH) for b in range(c + 1)]

        def neg_units(c):
            return [("neg", c, h) for h in range(NH)]

        def filled_by_pe(what):
            return what[0] in ("max", "neg", "out", "tr", "logit", "w", "t", "qa", "qb", "ka", "kb", "v")

        before = {(0, 0): [("w", 3)],
                  (0, 1): [("v", 2), ("qa", 2), ("qb", 2), ("qsum", 2)],
                  (0, 2): [("qlow", 2), ("ka", 2), ("kb", 2), ("ksum", 2)],
                  (0, 3): [("klow", 2)],
                  (1, 0): [("qa", 3), ("qb", 3), ("qsum", 3)],
                  (1, 1): [("qlow", 3), ("ka", 3), ("kb", 3), ("ksum", 3)],
                  (1, 2): [("klow", 3), ("v", 3)]}
        behind = {(0, 0): [("elu", 3), ("t", 2)], (0, 1): [("stat", 3)], (0, 2): [("rows1", 3)], (0, 3): [("t", 3)]}

        follow = {2: [("div", 0)], 3: [("out", 0)], 4: [("div", 1)], 5: [("rows", 0), ("out", 1)], 6: [("tr", 0), ("div", 2)],
                  7: [("rows", 1), ("out", 2)], 8: [("tr", 1), ("logit", 0)], 9: [("rows", 2)], 10: [("tr", 2), ("logit", 1)],
                  11: [("logit", 2)], 12: [("choose", 0)], 13: [("choose", 1)], 14: [("choose", 2)]}
        units_at = {}
        unit_no = {}
        for what in max_units(0) + neg_units(0):
            unit_no[what] = len(unit_no)
        for c in range(NC):
            own = [step for step in steps if step[0] == c]
            todo = max_units(c + 1) if c + 1 < NC else []
            late = 1 if c == 1 else 0
            per_step = -(-len(todo) // (len(own) - 1 - late))
            for turn, step in enumerate(own):
                units = todo[(turn - late) * per_step:(turn + 1 - late) * per_step] if turn >= late else []
                if turn == len(own) - 1 and todo:
                    units = neg_units(c + 1)
                if c == NC - 1:
                    units = follow.get(turn, [])
                units = before.get((c, turn), []) + units + behind.get((c, turn), [])
                units_at[step] = units
                for what in units:
                    if filled_by_pe(what):
                        unit_no[what] = len(unit_no)
        for name in ("out", "tr", "logit"):
            unit_no[(name, NC - 1)] = len(unit_no)
        TAIL_BANK = 7
        EARLY, LATE = slice(0, NT - TPC), slice(NT - TPC, NT)

        def unit_bank(what):
            return TAIL_BANK if what[0] in ("out", "tr", "logit") and what[1] == NC - 1 else 4 + unit_no[what] % 2

        H_BANKS = (0, 1, 6, 7)

        ROUTE_STEPS = 23

        block = ctx.enter_context(nc.Block())

        first = [(wmat[:, 0, :], w_proj), (wmat[:, 1, :], w_gcn), (cols[:, 0:1], b_proj)]
        small = [
            (wmat[:, 2, :], g1_w), (cols[:, 1:2], b_gcn), (cols[:, 2:3], ln1), (cols[:, 3:4], ln2),
            (wg32[:, :], f0_wg), (gbias[:, 0, :], f0_bg.partition_broadcast(P)),
            (gbias[:, 1, :], f0_bias.partition_broadcast(P)), (b2_sb[:, :], f0_b2),
        ]

        def many_entries(eng):
            eng.wait_ge(s_flag, 1)
            return eng.If(eng.value_load(flag[0:1, 0:1], min_val=0, max_val=1) > 0)

        def pick(chain, dve, n, L, lg):
            eq, key, km = lg[:, 1], lg[:, 2], sm[:, 5]
            value, hot = sm[:, n], lg[:, 3 + n]
            bc = lambda v: v.unsqueeze(2).broadcast_to([P, NT, 8])
            chain(dve.reduce_max(value, L, AX_X))
            chain(dve.tensor_tensor(eq, L, bc(value), ALU.is_equal))
            chain(dve.tensor_tensor(key, eq, rev[:, :, :], ALU.mult))
            chain(dve.reduce_max(km, key, AX_X))
            chain(dve.tensor_tensor(hot, key, bc(km), ALU.is_equal))
            if n == 0:
                chain(dve.scalar_tensor_tensor(out=lg[:, 5], in0=hot, scalar=NEG, in1=L, op0=ALU.mult, op1=ALU.add))

        def combine_weights(chain, eng, w1, w2, lg):
            bc = lambda v: v.unsqueeze(2).broadcast_to([P, NT, 8])
            chain(eng.tensor_tensor(lg[:, 6], lg[:, 3], bc(w1), ALU.mult))
            chain(eng.tensor_tensor(lg[:, 7], lg[:, 4], bc(w2), ALU.mult))
            return eng.tensor_tensor(comb[:, :, :], lg[:, 6], lg[:, 7], ALU.add)

        @block.sync
        def _(sp):
            for g in range(NC):
                w = slice(TPC * g, TPC * g + TPC)
                sp.dma_start(x[:, w, :], x_in[:, w, :]).then_inc(s_x[g], 16)
            for j in range(NT):
                sp.dma_start(A[:, j, :], adj_t[j]).then_inc(s_A[j], 16)

            def load_expert0(s, e):
                sp.dma_start(st_w1[:, s, :], f0_w1[bass.ds(e, 1), :, :].rearrange("a p h -> (a p) h")).then_inc(s_ld0[s], 16)
                sp.dma_start(st_w2[:, s, :, :], f0_w2[bass.ds(e, 1), :, :, :].rearrange("a p k d -> (a p) k d")).then_inc(s_ld0[s], 16)
                sp.dma_start(st_b1[:, s, :], f0_b1[bass.ds(e, 1), :, :].rearrange("a p k -> (a p) k")).then_inc(s_ld0[s], 16)

            with many_entries(sp):
                sp.dma_start(a_row, adj_in[0]).then_inc(g_load, 16)
                with sp.Fori(1, NT) as i:
                    sp.wait_ge(g_sq, i)
                    sp.dma_start(a_row, adj_in[bass.ds(i, 1), :, :].rearrange("a p t -> (a p) t")).then_inc(g_load, 16)
                sp.wait_ge(g_mm, 4 * NT + 2)
            sp.wait_ge(s_aggp, NT)
            sp.wait_ge(s_cntp, NT)
            load_expert0(0, 0)
            load_expert0(1, 1)
            sp.wait_ge(s_w00, 2)
            with sp.Fori(1, E0 // 2) as i:
                for s in range(2):
                    sp.wait_ge(s_w2, 2 * i + s - 1)
                    load_expert0(s, 2 * i + s)
            sp.wait_ge(s_add0, E0 * NC + 2)
            for dst, src in ((cos_sb, cos_t), (sin_sb, sin_t)):
                for h in range(NH):
                    sp.dma_start(dst[HD * h:HD * h + HD, :], src).then_inc(s_attw, 16)
            for dst, src in ((wq32, wq), (wk32, wk), (wv32, wv), (wo32, wo), (wr32, w_router)):
                sp.dma_start(dst, src).then_inc(s_attw, 16)

            def load_expert1(s, e):
                sp.dma_start(v13[:, s, 0, :], f1_w1[bass.ds(e, 1), :, :].rearrange("a p h -> (a p) h")).then_inc(s_ld1[s], 16)
                sp.dma_start(v13[:, s, 1, :], f1_w3[bass.ds(e, 1), :, :].rearrange("a p h -> (a p) h")).then_inc(s_ld1[s], 16)
                sp.dma_start(v2[:, s, 0:2, :], f1_w2[bass.ds(e, 1), 0:2 * P, :].rearrange("a (k p) d -> (a p) k d", p=P)
                             ).then_inc(s_ld1[s], 16)
                sp.dma_start(v2[0:KS1[2][1], s, 2, :], f1_w2[bass.ds(e, 1), 2 * P:H1, :].rearrange("a p d -> (a p) d")
                             ).then_inc(s_ld1[s], 16)

            for c in range(NC):
                for done, src, dst, heads, order in ((s_qlo, q16, queries, NH, (0, 1, 0)), (s_klo, k16, keys, NKV, (0, 0, 1))):
                    sp.wait_ge(done, c + 1)
                    for n, part in enumerate(order):
                        for h in range(heads):
                            sp.dma_start(dst(c, h)[HD * n:HD * n + HD], src(c, part)[HD * h:HD * h + HD]
                                         ).then_inc(s_stack[c], 16)
            sp.wait_ge(s_tail, 1)
            load_expert1(0, 0)
            load_expert1(1, 1)
            with sp.Fori(1, E1 // 2) as i:
                for s in range(2):
                    sp.wait_ge(s_w22, 2 * i + s)
                    load_expert1(s, 2 * i + s)
            for g in range(NC):
                sp.wait_ge(s_add1, (E1 - 1) * NC + g + 1 + 2)
                sp.dma_start(out[:, TPC * g:TPC * g + TPC, :], x[:, TPC * g:TPC * g + TPC, :]).then_inc(s_out, 16)
            sp.wait_ge(s_out, 16 * NC)

        @block.gpsimd
        def _(pool):
            chain = Chain(pool, s_cpool)
            pool.memset(neg_half[:, :], -0.5)
            pool.memset(ones[:, :], 1.0)
            for n, v in enumerate((SW, 1.0, SH)):
                pool.memset(factor[:, n:n + 1], v)
            pool.memset(ones_b[:, :], 1.0)
            chain(pool.memset(ident[:, :], 0.0))
            pool.affine_select(out=ident[:, :], in_=ident[:, :], compare_op=ALU.not_equal, fill=1.0, base=0,
                               pattern=[[-1, P]], channel_multiplier=1).then_inc(s_const, 1)
            pool.iota(rev[:, :, :], pattern=[[0, NT], [-1, 8]], base=8, channel_multiplier=0,
                      allow_small_or_imprecise_dtypes=True).then_inc(s_const, 1)

            def inverse_root(n, g):
                pool.wait_ge(s_var, n)
                pool.tensor_tensor(rstd[:, TPC * g:TPC * g + TPC], ve[:, TPC * g:TPC * g + TPC],
                                   neg_half[:, 0:TPC], ALU.pow).then_inc(s_rstd, 1)

            for g in range(NC):
                inverse_root(g + 1, g)
            pool.wait_ge(s_gp, NC)
            pool.wait_ge(s_A[0], 16)
            for j in range(1, NT):
                pool.wait_ge(s_A[j], 16)
                pool.tensor_tensor(asum, A[:, 0, :] if j == 1 else asum, A[:, j, :], ALU.add).then_inc(s_asum, 1)
                pool.wait_ge(s_asum, j)
            for g in range(NC):
                inverse_root(NC + g + 1, g)

            def times(out, v, n):
                f = factor[:, n:n + 1]
                if len(v.shape) == 3:
                    f = f.unsqueeze(2)
                return pool.tensor_tensor(out, v, f.broadcast_to(list(v.shape)), ALU.mult)

            flat0 = lambda v, s: v[:, s].rearrange("p k d -> p (k d)")

            def split_expert0(s, count, free):
                pool.wait_ge(s_ld0[s], 48 * count)
                times(st_w1[:, s], st_w1[:, s], 0)
                chain(times(flat0(st_w2, s), flat0(st_w2, s), 0))
                if free is not None:
                    pool.wait_ge(s_y0, free)
                chain(times(w1h[:, s], st_w1[:, s], 1))
                times(b1[:, s, :], st_b1[:, s, :], 1)
                times(b1s[:, s, :], st_b1[:, s, :], 2)
                pool.tensor_tensor(w1l[:, s], st_w1[:, s], w1h[:, s], ALU.subtract).then_inc(s_w1s, 1)
                chain(times(flat0(w2h, s), flat0(st_w2, s), 1))
                pool.tensor_tensor(w2l[:, s], st_w2[:, s], w2h[:, s], ALU.subtract).then_inc(s_w2, 1)

            split_expert0(1, 1, None)
            with pool.Fori(1, E0 // 2) as i:
                chain.turn(i - 1, 6)
                for s in range(2):
                    split_expert0(s, i + 1, (2 * i + s - 1) * NC + 4)
                chain.turn_ends(6)
            chain.loop_ends(E0 // 2 - 1, 6)
            pool.wait_ge(s_degv, 1)
            pool.tensor_tensor(dis[:, :], sm[:, 11, :], neg_half[:, :], ALU.pow).then_inc(s_dis, 1)

            pool.wait_ge(s_dis, 1)
            chain(pool.memset(mask_ts[:, :], 0.0))
            chain(pool.memset(mask_st[:, :], 0.0))
            chain(pool.affine_select(out=mask_ts[:, :], in_=mask_ts[:, :], compare_op=ALU.is_ge, fill=NEG, base=0,
                                     pattern=[[-1, P]], channel_multiplier=1))
            chain(pool.affine_select(out=mask_st[:, :], in_=mask_st[:, :], compare_op=ALU.is_ge, fill=NEG, base=0,
                                     pattern=[[1, P]], channel_multiplier=-1))
            chain(pool.tensor_copy(ident_b[:, :], ident[:, :]))
            pool.tensor_copy(ident_h[:, :], ident[:, :]).then_inc(s_mc, 1)
            pool.wait_ge(s_mc, 1)
            for g in range(NC):
                w = slice(TPC * g, TPC * g + TPC)
                pool.wait_ge(s_var, 2 * NC + g + 1)
                chain(pool.tensor_tensor(rstd[:, w], ve[:, w], neg_half[:, 0:TPC], ALU.pow))
                pool.tensor_tensor(rd[:, w], rstd[:, w], dis[:, w], ALU.mult).then_inc(s_rstd, 1)

            for g in range(NC):
                w = slice(TPC * g, TPC * g + TPC)
                pool.wait_ge(s_var, 3 * NC + g + 1)
                chain(pool.tensor_tensor(rstd[:, w], ve[:, w], neg_half[:, 0:TPC], ALU.pow))
                chain(pool.tensor_tensor(rd[:, w], rstd[:, w], rstd[:, w], ALU.mult))
                chain(pool.tensor_tensor(rd[:, w], rd[:, w], mv[:, w, 1], ALU.mult))
                chain(pool.tensor_scalar(rd[:, w], rd[:, w], EPS_RMS, None, ALU.add))
                chain(pool.tensor_tensor(rd[:, w], rd[:, w], neg_half[:, 0:TPC], ALU.pow))
                pool.tensor_tensor(rd[:, w], rd[:, w], rstd[:, w], ALU.mult).then_inc(s_rstd, 1)
                pool.wait_ge(s_rstd, 3 * NC + g + 1)
                for kv in range(NKV):
                    last = pool.memset(keys(g, kv)[KQ:KQ + 1], 16.0)
                last.then_inc(s_mc, 1)
                pool.wait_ge(s_mc, g + 2)
            pool.memset(v2[:, :, 2, :], 0.0).then_inc(s_tail, 1)
            chain(pool.tensor_scalar(factor[:, 3:4], cols[:, 3:4], SW, None, ALU.mult))

            def split_expert1(s, count, free):
                pool.wait_ge(s_ld1[s], 64 * count)
                times(v13[:, s], v13[:, s], 3)
                chain(times(flat0(v2, s), flat0(v2, s), 0))
                if free is not None:
                    pool.wait_ge(s_y1, free)
                chain(times(v13h[:, s], v13[:, s], 1))
                pool.tensor_tensor(v13l[:, s], v13[:, s], v13h[:, s], ALU.subtract).then_inc(s_w13, 1)
                chain(times(flat0(v2h, s), flat0(v2, s), 1))
                pool.tensor_tensor(v2l[:, s], v2[:, s], v2h[:, s], ALU.subtract).then_inc(s_w22, 1)

            split_expert1(0, 1, None)
            split_expert1(1, 1, None)
            for g in range(NC):
                w = slice(TPC * g, TPC * g + TPC)
                pool.wait_ge(s_ms, g + 1)
                pool.tensor_tensor(rd[:, w], ve[:, w], neg_half[:, 0:TPC], ALU.pow).then_inc(s_r2, 1)
            with pool.Fori(1, E1 // 2) as i:
                chain.turn(i - 1, 6)
                for s in range(2):
                    split_expert1(s, i + 1, (2 * i + s - 1) * NC + 4)
                chain.turn_ends(6)
            chain.loop_ends(E1 // 2 - 1, 6)

        @block.scalar
        def _(act):
            for dst, src in first:
                act.dma_start(dst, src).then_inc(s_first, 16)
            for dst, src in small:
                act.dma_start(dst, src).then_inc(s_small, 16)

            act.wait_ge(s_first, 16 * len(first))
            for g in range(NC):
                act.wait_ge(s_h2p, g + 1)
                act.activation(h2T[:, CW * g:CW * g + CW], ps[:, 4 + g, :], ACT.Tanh, bias=cols[:, 0:1]).then_inc(s_h2, 1)
            for j in range(NT):
                act.wait_ge(s_sq, j + 1)
                act.activation(fbuf[:, j % FB, :], fbuf[:, j % FB, :], ACT.Tanh).then_inc(s_F, 1)
            def features(done):
                for g in range(NC):
                    act.activation(xT[:, CW * g:CW * g + CW], ps[:, g, :], ACT.Relu, bias=cols[:, 1:2]).then_inc(done, 1)

            act.wait_ge(s_aggp, NT)
            act.wait_ge(s_small, 16 * len(small))
            features(s_feat)
            with many_entries(act):
                with act.Fori(0, NT) as i:
                    act.wait_ge(g_sq, i + 1)
                    act.activation(f_row, f_row, ACT.Tanh).then_inc(g_tanh, 1)
                    for q in range(4):
                        act.wait_ge(g_tr, 4 * i + q + 1)
                        act.wait_ge(g_mm, 4 * i + q + 1)
                        act.activation(rT[:, q % 2, :], ps[:, 6 + q % 2, :], ACT.Copy).then_inc(g_cp, 1)
                act.wait_ge(g_mm, 4 * NT + 2)
                features(g_feat)

            def high_parts(n):
                g = n % NC
                act.wait_ge(s_tr, NC + n + 1)
                act.activation(xh[:, CW * g:CW * g + CW], ps[:, n % 2 + 6, :], ACT.Copy, scale=SX).then_inc(s_xhi, 1)


            for g in range(NC):
                high_parts(g)

            act.sem_inc(s_relu, 4)

            def relu(i, gg, k):
                s, u = gg // NC, gg * K0 + k
                act.wait_ge(s_h0, 8 * K0 * i + u + 1)
                act.wait_ge(s_hlo, 8 * K0 * i + u + 1)
                act.wait_ge(s_y0, 8 * i + gg + 1)
                act.activation(h32[:, u % 4, :], ps[:, H_BANKS[u % 4], :], ACT.Relu, bias=b1[:, s, k:k + 1],
                               scale=1.0 / (SX * SW))
                act.activation(hh_hi[:, gg % 4, k, :], ps[:, H_BANKS[u % 4], :], ACT.Relu, bias=b1s[:, s, k:k + 1],
                               scale=SH / (SX * SW)).then_inc(s_relu, 1)

            def bias2_copy(half):
                act.wait_ge(s_cT, half + 1)
                act.activation(combT[:, 2 * CW * half:2 * CW * half + 2 * CW], ps[0:8, 4:6, :], ACT.Copy).then_inc(s_cTc, 1)

            act.wait_ge(s_b1s, 1)
            for gg in range(2 * NC):
                if gg == NC:
                    act.wait_ge(s_w1s, 1)
                for k in range(K0):
                    relu(0, gg, k)
                if gg == 1:
                    act.wait_ge(s_diff, 1)
                    act.activation(sm[:, 3, :], sm[:, 2, :], ACT.Exp).then_inc(s_ediff, 1)
                if gg in (4, 5):
                    bias2_copy(gg - 4)
            with act.Fori(1, E0 // 2) as i:
                for gg in range(2 * NC):
                    for k in range(K0):
                        relu(i, gg, k)

            def aggregate_copy(c):
                act.wait_ge(s_agg1, c + 1)
                if c >= 2:
                    act.wait_ge(s_z, c - 1)
                act.activation(hagg[:, c % 2, :], ps[:, c % 2, :], ACT.Copy).then_inc(s_hagg, 1)

            def elu_exp(c):
                act.wait_ge(s_zn, c + 1)
                act.activation(ez[:, c % 2, :], ez[:, c % 2, :], ACT.Exp).then_inc(s_ez, 1)

            def high1(c):
                act.wait_ge(s_tr1, c + 1)
                act.activation(th[:, CW * c:CW * c + CW], ps[:, 3, :], ACT.Copy, scale=SX).then_inc(s_thi, 1)

            def high_queries(c):
                act.wait_ge(s_qr, c + 1)
                act.activation(q16(c, 0), rope[:, 2, :], ACT.Copy).then_inc(s_qhi, 1)

            def values_and_high_keys(c):
                act.wait_ge(s_vp, c + 1)
                act.activation(A[:, 3, CW * c:CW * c + TPC * NKV * HD], ps[:, 3, 0:TPC * NKV * HD],
                               ACT.Copy, scale=1.0 / (SX * SW)).then_inc(s_V, 1)
                high_keys(c)

            def high_keys(c):
                act.wait_ge(s_kr, c + 1)
                act.activation(k16(c, 0), rope[0:NKV * HD, 5, :], ACT.Copy).then_inc(s_khi, 1)



            aggregate_copy(0)
            elu_exp(0)
            high1(0)
            aggregate_copy(1)
            high_queries(0)
            elu_exp(1)
            values_and_high_keys(0)
            high1(1)
            aggregate_copy(2)
            high_queries(1)
            elu_exp(2)
            values_and_high_keys(1)
            aggregate_copy(3)

            def high_of_rows(c):
                act.wait_ge(s_rm, unit_no[("tr", c)] + 1)
                act.activation(th[:, CW * c:CW * c + CW], ps[:, unit_bank(("tr", c)), :], ACT.Copy, scale=SX).then_inc(s_thi, 1)

            def router_exp(n, w):
                act.wait_ge(s_route, n * ROUTE_STEPS + 2)
                act.activation(lg1[:, 2, w], lg1[:, 1, w], ACT.Exp).then_inc(s_re, 1)

            for n, (c, j) in enumerate(steps):
                t0 = max(0, P * (j - TPC * c))
                for pair in range(2):
                    act.wait_ge(s_st, 2 * n + pair + 1)
                    if n >= 2:
                        act.wait_ge(s_pv, n - 1)
                    act.activation(Pb[:, n % 2, 2 * pair:2 * pair + 2, t0:CW], ps[:, 2 * pair:2 * pair + 2, t0:CW], ACT.Exp,
                                   scale=1.0 / (SQ * SQ * float(HD) ** 0.5)).then_inc(s_p, 1)
                for what in units_at[(c, j)]:
                    if what[0] == "tr":
                        high_of_rows(what[1])
                    if what[0] == "t":
                        act.wait_ge(s_rm, unit_no[what] + 1)
                        act.activation(th[:, CW * what[1]:CW * what[1] + CW], ps[:, unit_bank(what), :], ACT.Copy,
                                       scale=SX).then_inc(s_thi, 1)
                    if what[0] == "elu":
                        elu_exp(what[1])
                    if what[0] == "qsum":
                        high_queries(what[1])
                    if what[0] == "ksum":
                        high_keys(what[1])
                    if what == ("choose", 1):
                        router_exp(0, EARLY)
                if last_step(c, j):
                    act.wait_ge(s_pv, n + 1)
                    act.activation(o_sb[c], ps[:, 6, :], ACT.Copy)
                    act.activation(d_sb[c], ps[:, 7, :], ACT.Copy).then_inc(s_od, 1)

            act.sem_inc(s_silu, 3)

            def silu(i, u):
                k = u % 3
                r = KS1[k][1]
                act.wait_ge(s_h1, 24 * i + u + 1)
                act.wait_ge(s_hh, 24 * i + u + 1)
                act.activation(silu_sb[0:r, k, :], ps[0:r, k, :], ACT.Silu, scale=1.0 / (SX * SW)).then_inc(s_silu, 1)

            def high_hidden(i, u):
                gg, k = u // 3, u % 3
                r = KS1[k][1]
                act.wait_ge(s_hh, 24 * i + u + 1 + 3)
                act.wait_ge(s_y1, 8 * i + gg + 1)
                act.activation(g_hi(gg % 4, k)[0:r], g32[0:r, u % 6, :], ACT.Copy).then_inc(s_ghi, 1)

            silu(0, 0)
            for u in range(1, 24):
                silu(0, u)
                high_hidden(0, u - 1)
                if u == 5:
                    high_of_rows(NC - 1)
                if u == 10:
                    router_exp(1, LATE)
            with act.Fori(1, E1 // 2) as i:
                for u in range(24):
                    silu(i, u)
                    high_hidden(i, u - 1)
            high_hidden(E1 // 2 - 1, 23)

        @block.tensor
        def _(pe):
            def transpose_rows(g, bank):
                for q in range(TPC):
                    last = pe.transpose(ps[:, bank, P * q:P * q + P], xn[:, TPC * g + q, :], ident[:, :])
                last.then_inc(s_tr, 1)

            pe.wait_ge(s_const, 1)
            for g in range(NC):
                pe.wait_ge(s_xn, g + 1)
                transpose_rows(g, g)
            pe.wait_ge(s_first, 16 * len(first))
            for g in range(NC):
                pe.wait_ge(s_pre_ev, g + 1)
                pe.matmul(ps[:, 4 + g, :], wmat[:, 0, :], xT[:, CW * g:CW * g + CW], start=True, stop=True).then_inc(s_h2p, 1)
            for g in range(NC):
                pe.wait_ge(s_h2, g + 1)
                for q in range(TPC):
                    t = TPC * g + q
                    last = pe.matmul(ps[:, g, P * q:P * q + P], h2T[:, P * t:P * t + P], wmat[:, 1, :], start=True, stop=True)
                last.then_inc(s_gp, 1)
            for j in range(NT):
                if j == 0:
                    pe.wait_ge(s_G, NC)
                pe.wait_ge(s_F, j + 1)
                for c in range(NC):
                    last = pe.matmul(ps[:, c, :], G[:, j, :], fbuf[:, j % FB, CW * c:CW * c + CW],
                                     start=(j == 0), stop=(j == NT - 1))
                last.then_inc(s_aggp, 1)
                pe.wait_ge(s_mask, j + 1)
                for c in range(NC):
                    last = pe.matmul(ps[32 * c:32 * c + 32, 4, :], ones_b[:, :], mbuf[:, j % 2, CW * c:CW * c + CW],
                                     start=(j == 0), stop=(j == NT - 1))
                last.then_inc(s_cntp, 1)
            pe.wait_ge(s_cmax, 1)
            pe.transpose(ps[0:1, 6, 0:P], cnt[:, 0:1], ident[:, :]).then_inc(s_cmT, 1)
            with many_entries(pe):
                pe.sem_inc(g_mm, 2)
                pe.wait_ge(s_G, NC)
                agg = ps[:, 0:NC, :].rearrange("p c t -> p (c t)")
                with pe.Fori(0, NT) as i:
                    pe.wait_ge(g_row, i + 1)
                    for q in range(4):
                        for t in range(4 * q, 4 * q + 4):
                            last = pe.transpose(ps[:, 6 + q % 2, P * (t % 4):P * (t % 4) + P], e_row[:, P * t:P * t + P], ident[:, :])
                        last.then_inc(g_tr, 1)
                        pe.wait_ge(g_cp, 4 * i + q + 1)
                        for t in range(4 * q, 4 * q + 4):
                            last = pe.matmul(agg[:, bass.ds(P * i, P)], G[:, t, :], rT[:, q % 2, P * (t % 4):P * (t % 4) + P],
                                             start=(t == 0), stop=(t == NT - 1))
                        last.then_inc(g_mm, 1)
                pe.wait_ge(g_feat, NC)
            for g in range(NC):
                pe.wait_ge(s_feat, g + 1)
                if g == 0:
                    pe.wait_ge(s_flag, 1)
                if g >= 2:
                    pe.wait_ge(s_x1, g - 1)
                for q in range(TPC):
                    t = TPC * g + q
                    last = pe.transpose(ps[:, 6 + g % 2, P * q:P * q + P], xT[:, P * t:P * t + P], ident[:, :])
                last.then_inc(s_ftr, 1)
            def degrees():
                pe.wait_ge(s_asum, NT - 1)
                for t in range(NT):
                    last = pe.matmul(ps[:, 5, t:t + 1], asum[:, P * t:P * t + P], ones[:, 0:1], start=True, stop=True)
                last.then_inc(s_degc, 1)


            for g in range(NC):
                pe.wait_ge(s_xn, NC + g + 1)
                if g >= 2:
                    pe.wait_ge(s_xlo, g - 1)
                else:
                    pe.wait_ge(s_x1, NC - 1 + g)
                transpose_rows(g, 6 + g % 2)
            pe.wait_ge(s_wg, 1)
            for t in range(NT):
                if t % TPC == 0:
                    pe.wait_ge(s_xlo, t // TPC + 1)
                for n, (a, b) in enumerate(((xh, 0), (xl, 0), (xh, 1))):
                    last = pe.matmul(ps[:, 4, 8 * t:8 * t + 8], a[:, P * t:P * t + P], wg16[:, b, :], start=(n == 0), stop=(n == 2))
            last.then_inc(s_gate, 1)

            pe.sem_inc(s_y0, 4)

            def hidden(i, gg):
                s, g = gg // NC, gg % NC
                if g == 0:
                    if isinstance(i, int) and gg == 0:
                        pe.wait_ge(s_w00, 1)
                    else:
                        pe.wait_ge(s_w1s, 2 * i + s)
                for k in range(K0):
                    u = gg * K0 + k
                    pe.wait_ge(s_relu, 8 * K0 * i + u + 1)
                    for n, (w, a) in enumerate(((w1h, xh), (w1h, xl), (w1l, xh))):
                        last = pe.matmul(ps[:, H_BANKS[u % 4], :], w[:, s, P * k:P * k + P], a[:, CW * g:CW * g + CW],
                                         start=(n == 0), stop=(n == 2))
                    last.then_inc(s_h0, 1)

            def output(i, gg):
                s = gg // NC % 2
                if isinstance(i, int) and 8 * i + gg == 0:
                    pe.wait_ge(s_w00, 2)
                elif gg % NC == 0:
                    pe.wait_ge(s_w2, 2 * i + gg // NC)
                pe.wait_ge(s_hlo, 8 * K0 * i + (gg + 1) * K0 + 4)
                pe.wait_ge(s_add0, 8 * i + gg + 1)
                for q in range(TPC):
                    n = 0
                    for k in range(K0):
                        for a, w in ((hh_hi, w2h), (hh_hi, w2l), (hh_lo, w2h)):
                            last = pe.matmul(ps[:, 2 + gg % 2, P * q:P * q + P], a[:, gg % 4, k, P * q:P * q + P],
                                             w[:, s, k, :], start=(n == 0), stop=(n == 3 * K0 - 1))
                            n += 1
                last.then_inc(s_y0, 1)

            def bias2_transpose(half):
                pe.wait_ge(s_comb, 1)
                pe.wait_ge(s_degv, 1)
                if half:
                    pe.wait_ge(s_cTc, 1)
                for t in range(2 * TPC):
                    last = pe.transpose(ps[0:8, 4 + t // TPC, P * (t % TPC):P * (t % TPC) + P], comb[:, 2 * TPC * half + t, :],
                                        ident[:, :])
                last.then_inc(s_cT, 1)

            def bias2_product(half):
                pe.wait_ge(s_cTc, 2)
                if half:
                    pe.wait_ge(s_b2a, 1)
                for t in range(2 * TPC):
                    tt = 2 * TPC * half + t
                    last = pe.matmul(ps[:, 4 + t // TPC, P * (t % TPC):P * (t % TPC) + P], combT[:, P * tt:P * tt + P],
                                     b2_sb[:, :], start=True, stop=True)
                last.then_inc(s_b2, 1)

            for gg in range(2 * NC):
                hidden(0, gg)
                if gg >= 2:
                    output(0, gg - 2)
                if gg == 1:
                    degrees()
                if gg in (4, 5):
                    bias2_transpose(gg - 4)
                if gg in (6, 7):
                    bias2_product(gg - 6)
            with pe.Fori(1, E0 // 2) as i:
                for gg in range(2 * NC):
                    hidden(i, gg)
                    output(i, gg - 2)
            for gg in (2 * NC - 2, 2 * NC - 1):
                output(E0 // 2 - 1, gg)

            def aggregate(c):
                if c == 0:
                    pe.wait_ge(s_xn, 3 * NC)
                if c >= 2:
                    pe.wait_ge(s_hagg, c - 1)
                for j in range(NT):
                    if c >= 2 and j == 0:
                        query_products(c - 2)
                    if c >= 2 and j == 4:
                        key_value_products(c - 2)
                    if c in (1, 2) and j == 13:
                        transposed_rows(c - 1)
                    if c == NC - 1 and j >= 8:
                        for what in early[3 * (j - 8):3 * (j - 7)]:
                            unit(what)
                    if c >= 1 and j == 2:
                        times_w(c - 1)
                    if j // TPC == c:
                        q = j % TPC
                        pe.matmul(ps[:, c % 2, P * q:P * q + P], G[:, j, :], ident[:, :], start=(j == 0), stop=False,
                                  skip_group_check=True)
                    last = pe.matmul(ps[:, c % 2, :], G[:, j, :], A[:, j, CW * c:CW * c + CW],
                                     start=(j == 0 and c > 0), stop=(j == NT - 1), skip_group_check=True)
                last.then_inc(s_agg1, 1)

            def times_w(c):
                pe.wait_ge(s_hagg, c + 1)
                if c:
                    pe.wait_ge(s_x3, c)
                for q in range(TPC):
                    last = pe.matmul(ps[:, 2, P * q:P * q + P], hagg[:, c % 2, P * q:P * q + P], wmat[:, 2, :],
                                     start=True, stop=True)
                last.then_inc(s_z, 1)

            def transposed_rows(c):
                pe.wait_ge(s_hn, c + 1)
                if c:
                    pe.wait_ge(s_V, c)
                for q in range(TPC):
                    last = pe.transpose(ps[:, 3, P * q:P * q + P], frow[:, c % 2, P * q:P * q + P], ident[:, :])
                last.then_inc(s_tr1, 1)

            def product3(dst, w0, w1, g):
                for n, (b, a) in enumerate(((0, th), (0, tl), (1, th))):
                    last = pe.matmul(dst, watt[:, b, w0:w1], a[:, CW * g:CW * g + CW], start=(n == 0), stop=(n == 2))
                return last

            def query_products(c):
                if c == 0:
                    pe.wait_ge(s_attws, 1)
                else:
                    pe.wait_ge(s_kr, c)
                pe.wait_ge(s_tlo, c + 1)
                product3(ps[:, 6, :], WQ, WQR, c)
                product3(ps[:, 7, :], WQR, WK, c).then_inc(s_qp, 1)

            def value_products(bank, c):
                for q in range(TPC):
                    t = TPC * c + q
                    for n, (a, b) in enumerate(((th, 0), (tl, 0), (th, 1))):
                        last = pe.matmul(bank[:, NKV * HD * q:NKV * HD * (q + 1)], a[:, P * t:P * t + P],
                                         watt[:, b, WV:WR], start=(n == 0), stop=(n == 2))
                return last

            COLUMNS = {"qa": (WQ, WQR), "qb": (WQR, WK), "ka": (WK, WKR), "kb": (WKR, WV)}

            def key_value_products(c):
                value_products(ps[:, 3, :], c).then_inc(s_vp, 1)
                pe.wait_ge(s_qr, c + 1)
                product3(ps[0:NKV * HD, 6, :], WK, WKR, c)
                product3(ps[0:NKV * HD, 7, :], WKR, WV, c).then_inc(s_kp, 1)

            early = max_units(0) + neg_units(0)
            assert len(early) == 20

            def unit(what):
                n, bank = unit_no[what], unit_bank(what)
                if n >= 2:
                    pe.wait_ge(s_rmf, n if bank == TAIL_BANK else n - 1)
                if what[0] == "max":
                    _, t, h, b = what
                    if (t % TPC, h, b) == (0, 0, 0):
                        pe.wait_ge(s_stack[t // TPC], 16 * 3 * (NH + NKV))
                    diagonal = b == t // TPC
                    width = P * (t % TPC + 1) if diagonal else CW
                    pe.wait_ge(s_mc, 1)
                    if diagonal:
                        pe.matmul(ps[:, bank, width - P:width], ident_b[:, :], mask_ts[:, :], start=True, stop=False,
                                  skip_group_check=True)
                    last = pe.matmul(ps[:, bank, 0:width], queries(t // TPC, h)[0:KQ, P * (t % TPC):P * (t % TPC) + P],
                                     keys(b, h // (NH // NKV))[0:KQ, 0:width], start=not diagonal, stop=True,
                                     skip_group_check=True)
                elif what[0] == "neg":
                    _, c, h = what
                    pe.wait_ge(s_m, c + 1)
                    for q in range(TPC):
                        last = pe.matmul(ps[KQ:KQ + 1, bank, P * q:P * q + P], m16[:, h, q:q + 1], ident_h[:, :],
                                         start=True, stop=True)
                elif what[0] == "out":
                    c = what[1]
                    pe.wait_ge(s_yT, c + 1)
                    for q in range(TPC):
                        last = pe.matmul(ps[:, bank, P * q:P * q + P], yT[:, c, P * q:P * q + P], wo32, start=True, stop=True)
                elif what[0] == "tr":
                    c = what[1]
                    pe.wait_ge(s_fn, c + 1)
                    for q in range(TPC):
                        last = pe.transpose(ps[:, bank, P * q:P * q + P], G[:, TPC * c + q, :], ident[:, :])
                elif what[0] == "w":
                    c = what[1]
                    pe.wait_ge(s_hagg, c + 1)
                    for q in range(TPC):
                        last = pe.matmul(ps[:, bank, P * q:P * q + P], hagg[:, c % 2, P * q:P * q + P], wmat[:, 2, :],
                                         start=True, stop=True)
                elif what[0] == "t":
                    c = what[1]
                    pe.wait_ge(s_hn, c + 1)
                    for q in range(TPC):
                        last = pe.transpose(ps[:, bank, P * q:P * q + P], frow[:, c % 2, P * q:P * q + P], ident[:, :])
                elif what[0] in COLUMNS:
                    c = what[1]
                    pe.wait_ge(s_rmf, unit_no[("t", c)] + 1)
                    w0, w1 = COLUMNS[what[0]]
                    last = product3(ps[0:w1 - w0, bank, :], w0, w1, c)
                elif what[0] == "v":
                    c = what[1]
                    pe.wait_ge(s_rmf, unit_no[("t", c)] + 1)
                    last = value_products(ps[:, bank, :], c)
                else:
                    c = what[1]
                    pe.wait_ge(s_rmf, unit_no[("tr", c)] + 1)
                    for q in range(TPC):
                        t = TPC * c + q
                        for m, (a, b) in enumerate(((th, 0), (tl, 0), (th, 1))):
                            last = pe.matmul(ps[:, bank, 8 * q:8 * q + 8], a[:, P * t:P * t + P], watt[:, b, WR:WR + 8],
                                             start=(m == 0), stop=(m == 2))
                last.then_inc(s_rm, 1)

            for c in range(NC):
                aggregate(c)

            def scores(n, h):
                pair = h // 2
                c, j = steps[n]
                k = j - TPC * c
                t0 = max(0, P * k)
                if first_step(c, j):
                    pe.wait_ge(s_rmf, unit_no[("neg", c, NH - 1)] + 1)
                    pe.wait_ge(s_mc, c + 2)
                if n and h % 2 == 0:
                    pe.wait_ge(s_p, 2 * (n - 1) + pair + 1)
                if k >= 0:
                    pe.matmul(ps[:, h, t0:t0 + P], ident_b[:, :], mask_st[:, :], start=True, stop=False,
                              skip_group_check=True)
                last = pe.matmul(ps[:, h, t0:CW], keys(j // TPC, h // (NH // NKV))[0:KQ + 1, P * (j % TPC):P * (j % TPC) + P],
                                 queries(c, h)[0:KQ + 1, t0:CW], start=k < 0, stop=True, skip_group_check=True)
                if h % 2:
                    last.then_inc(s_st, 1)

            def weigh(n, bank, heads):
                c, j = steps[n]
                t0 = max(0, P * (j - TPC * c))
                pe.wait_ge(s_p, 2 * n + 2)
                if first_step(c, j) and c >= 2:
                    pe.wait_ge(s_rmf, unit_no[("v", c)] + 1)
                if first_step(c, j) and c:
                    pe.wait_ge(s_od, c)
                for h in heads:
                    kv = h // (NH // NKV)
                    w = values(j, kv) if bank == 6 else ones[:, :]
                    last = pe.matmul(ps[HD * h:HD * h + HD, bank, t0:CW], w, Pb[:, n % 2, h, t0:CW],
                                     start=first_step(c, j), stop=last_step(c, j), skip_group_check=True)
                if bank == 7 and h == NH - 1:
                    last.then_inc(s_pv, 1)

            pe.wait_ge(s_hagg, NC)
            pe.wait_ge(s_x3, NC - 1)
            pe.wait_ge(s_V, 2)
            pe.wait_ge(s_kr, 2)
            pe.wait_ge(s_mc, 3)
            for h in range(NH):
                scores(0, h)
            for n, step in enumerate(steps):
                todo = [what for what in units_at[step] if filled_by_pe(what)]
                ends = last_step(*step) and n + 1 < len(steps)
                parts = [4, 5, 6, 7, 0, 1, 2, 3] if ends else list(range(8))
                among = 4 if ends else 8
                done = 0
                for turn, part in enumerate(parts):
                    upto = min(len(todo), -(-len(todo) * (turn + 1) // among))
                    for what in todo[done:upto]:
                        unit(what)
                    done = upto
                    if part >= NH:
                        weigh(n, 6 + (part - NH) // 2, (0, 1) if part % 2 == 0 else (2, 3))
                    elif n + 1 < len(steps):
                        scores(n + 1, part)

            pe.sem_inc(s_y1, 4)

            def hidden1(i, gg):
                s, g = gg // NC, gg % NC
                if g == 0:
                    pe.wait_ge(s_w13, 2 * i + s + 1)
                for k, (k0, r) in enumerate(KS1):
                    u = 3 * gg + k
                    for m, (free, ready) in enumerate(((s_silu, s_h1), (s_hh, s_h3))):
                        pe.wait_ge(free, 24 * i + u + 1)
                        for n, (w, a) in enumerate(((v13h, th), (v13h, tl), (v13l, th))):
                            last = pe.matmul(ps[0:r, 3 * m + k, :], w[:, s, m, k0:k0 + r], a[:, CW * g:CW * g + CW],
                                             start=(n == 0), stop=(n == 2))
                        last.then_inc(ready, 1)

            def output1(i, gg):
                s = gg // NC % 2
                if gg % NC == 0:
                    pe.wait_ge(s_w22, 2 * i + gg // NC + 1)
                pe.wait_ge(s_glo, 24 * i + 3 * (gg + 1) + 6)
                pe.wait_ge(s_add1, 8 * i + gg + 1)
                for q in range(TPC):
                    n = 0
                    for k, (_, r) in enumerate(KS1):
                        for a, w in ((g_hi, v2h), (g_hi, v2l), (g_lo, v2h)):
                            last = pe.matmul(ps[:, 6 + gg % 2, P * q:P * q + P], a(gg % 4, k)[0:r, P * q:P * q + P],
                                             w[0:r, s, k, :], start=(n == 0), stop=(n == 8))
                            n += 1
                last.then_inc(s_y1, 1)

            pe.wait_ge(s_rmf, unit_no[("logit", NC - 2)] + 1)
            hidden1(0, 0)
            unit(("out", NC - 1))
            hidden1(0, 1)
            unit(("tr", NC - 1))
            output1(0, 0)
            hidden1(0, 2)
            unit(("logit", NC - 1))
            pe.wait_ge(s_rmf, unit_no[("logit", NC - 1)] + 1)
            output1(0, 1)
            for gg in range(3, 2 * NC):
                hidden1(0, gg)
                output1(0, gg - 1)
            with pe.Fori(1, E1 // 2) as i:
                for gg in range(2 * NC):
                    hidden1(i, gg)
                    output1(i, gg - 1)
            output1(E1 // 2 - 1, 2 * NC - 1)

        @block.vector
        def _(dve):
            chain = Chain(dve, s_dve)

            def rows(v, g):
                return v[:, TPC * g:TPC * g + TPC, :].rearrange("p a d -> p (a d)")

            def statistics(g, src):
                for t in range(TPC * g, TPC * g + TPC):
                    last = dve.bn_stats(bst[:, t, :], src[:, t, :])
                chain(last)
                for t in range(TPC * g, TPC * g + TPC):
                    last = dve.bn_aggr(mv[:, t, :], bst[:, t, :])
                chain(last)
                dve.tensor_scalar(ve[:, TPC * g:TPC * g + TPC], mv[:, TPC * g:TPC * g + TPC, 1], EPS_LN, None,
                                  ALU.add).then_inc(s_var, 1)

            def normalise(n, g, src, dst):
                dve.wait_ge(s_rstd, n)
                for t in range(TPC * g, TPC * g + TPC):
                    last = dve.tensor_scalar(dst[:, t, :], src[:, t, :], mv[:, t, 0:1], rstd[:, t:t + 1], ALU.subtract, ALU.mult)
                last.then_inc(s_xn, 1)

            for g in range(NC):
                dve.wait_ge(s_x[g], 16)
                statistics(g, x)
            for g in range(NC):
                normalise(g + 1, g, x, xn)
            for g in range(NC):
                dve.wait_ge(s_tr, g + 1)
                dve.tensor_copy(xT[:, CW * g:CW * g + CW], ps[:, g, :]).then_inc(s_pre_ev, 1)

            def square(j):
                dve.wait_ge(s_A[j], 16)
                if j >= FB:
                    dve.wait_ge(s_aggp, j - FB + 1)
                    dve.wait_ge(s_mask, j - FB + 1)
                dve.scalar_tensor_tensor(out=fbuf[:, j % FB, :], in0=A[:, j, :], scalar=0.0, in1=A[:, j, :],
                                         op0=ALU.max, op1=ALU.mult).then_inc(s_sq, 1)

            def mask(j):
                dve.wait_ge(s_F, j + 1)
                if j >= 2:
                    dve.wait_ge(s_cntp, j - 1)
                dve.tensor_scalar(mbuf[:, j % 2, :], fbuf[:, j % FB, :], 0.0, None, ALU.is_gt).then_inc(s_mask, 1)

            square(0)
            for g in range(NC):
                dve.wait_ge(s_gp, g + 1)
                dve.tensor_copy(rows(G, g), ps[:, g, :]).then_inc(s_G, 1)
            for j in range(1, NT):
                square(j)
                mask(j - 1)
            mask(NT - 1)
            dve.wait_ge(s_cntp, NT)
            dve.reduce_max(cnt[:, 0:1], ps[:, 4, :], AX_X).then_inc(s_cmax, 1)
            dve.wait_ge(s_cmT, 1)
            chain(dve.reduce_max(cnt[0:1, 1:2], ps[0:1, 6, 0:P], AX_X))
            dve.tensor_scalar(flag[:, :], cnt[0:1, 1:2], float(LIMIT), None, ALU.is_gt).then_inc(s_flag, 1)
            with many_entries(dve):
                W = 8
                B = 5
                step = Chain(dve, s_gen)
                dve.wait_ge(s_feat, NC)
                with dve.Fori(0, NT) as i:
                    step.turn(i, W + 31 * B)
                    dve.wait_ge(g_load, 16 * i + 16)
                    dve.scalar_tensor_tensor(out=f_row, in0=a_row, scalar=0.0, in1=a_row, op0=ALU.max, op1=ALU.mult).then_inc(g_sq, 1)
                    step(dve.memset(thr, 0))
                    dve.wait_ge(g_tanh, i + 1)
                    dve.memset(bit, 1 << 30).then_inc(s_gen, 1)
                    step.here += 1
                    with dve.Fori(0, 31) as b:
                        step.base = i * (W + 31 * B) + b * B
                        dve.wait_ge(s_gen, step.base + step.here)
                        step(dve.tensor_tensor(cand, thr, bit, ALU.bitwise_or))
                        step(dve.tensor_scalar(c_row, f_row, cand_f, 0.0, ALU.is_ge, ALU.add, accum_out=cnt_f))
                        step(dve.tensor_scalar(ge, cnt_f, float(TOP), -1.0, ALU.is_ge, ALU.mult))
                        step(dve.tensor_tensor(ge, ge, bit, ALU.bitwise_and))
                        dve.tensor_scalar(bit, bit, 1, None, ALU.logical_shift_right)
                        step(dve.tensor_tensor(thr, thr, ge, ALU.bitwise_or))
                    step.here -= B
                    step.base = i * (W + 31 * B) + 31 * B
                    step(dve.tensor_scalar(c_row, f_row, thr_f, 0.0, ALU.is_gt, ALU.add, accum_out=cnt_f))
                    step(dve.tensor_scalar(need_f, cnt_f, -1.0, float(TOP), ALU.mult, ALU.add))
                    step(dve.tensor_scalar(c_row, f_row, thr_f, None, ALU.is_equal))
                    dve.wait_ge(g_mm, 4 * i + 2)
                    step(dve.tensor_tensor_scan(e_row, c_row, c_row, 0.0, ALU.add, ALU.max))
                    step(dve.scalar_tensor_tensor(out=c_row, in0=e_row, scalar=need_f, in1=c_row, op0=ALU.is_le, op1=ALU.mult))
                    step(dve.scalar_tensor_tensor(out=c_row, in0=f_row, scalar=thr_f, in1=c_row, op0=ALU.is_gt, op1=ALU.add))
                    dve.tensor_tensor(e_row, f_row, c_row, ALU.mult).then_inc(g_row, 1)
                    dve.wait_ge(g_row, i + 1)
                    step.turn_ends(W)
            for g in range(NC):
                dve.wait_ge(s_ftr, g + 1)
                dve.tensor_tensor(x[:, TPC * g:TPC * g + TPC, :].rearrange("p a d -> p (a d)"), ps[:, 6 + g % 2, :],
                                  x[:, TPC * g:TPC * g + TPC, :].rearrange("p a d -> p (a d)"), ALU.add).then_inc(s_x1, 1)
                dve.wait_ge(s_x1, g + 1)
                statistics(g, x)
                if g:
                    normalise(NC + g, g - 1, x, xn)
            normalise(2 * NC, NC - 1, x, xn)

            def low_parts(n):
                g = n % NC
                dve.wait_ge(s_xhi, n + 1)
                dve.scalar_tensor_tensor(out=xl[:, CW * g:CW * g + CW], in0=ps[:, n % 2 + 6, :], scalar=SX,
                                         in1=xh[:, CW * g:CW * g + CW], op0=ALU.mult, op1=ALU.subtract).then_inc(s_xlo, 1)

            def split(hi, lo, src, scale):
                chain(dve.tensor_scalar(hi, src, scale, None, ALU.mult))
                return dve.scalar_tensor_tensor(out=lo, in0=src, scalar=scale, in1=hi, op0=ALU.mult, op1=ALU.subtract)

            dve.wait_ge(s_small, 16 * len(small))
            split(wg16[:, 0, :], wg16[:, 1, :], wg32[:, :], SW).then_inc(s_wg, 1)
            for g in range(NC):
                low_parts(g)
            dve.wait_ge(s_ld0[0], 48)
            dve.tensor_copy(b1[:, 0, :], st_b1[:, 0, :])
            dve.tensor_scalar(b1s[:, 0, :], st_b1[:, 0, :], SH, None, ALU.mult).then_inc(s_b1s, 1)
            split(w1h[:, 0], w1l[:, 0], st_w1[:, 0], SW).then_inc(s_w00, 1)
            split(w2h[:, 0], w2l[:, 0], st_w2[:, 0], SW).then_inc(s_w00, 1)
            dve.wait_ge(s_gate, 1)
            chain(dve.tensor_tensor(lg[:, 8, 0, :], gbias[:, 0, :], gbias[:, 1, :], ALU.add))
            dve.scalar_tensor_tensor(out=lg[:, 0], in0=ps[:, 4, 0:8 * NT].rearrange("p (t e) -> p t e", e=8),
                                     scalar=1.0 / (SX * SW), in1=lg[:, 8, 0, :].unsqueeze(1).broadcast_to([P, NT, 8]),
                                     op0=ALU.mult, op1=ALU.add).then_inc(s_logit, 1)
            dve.wait_ge(s_const, 2)
            dve.wait_ge(s_logit, 1)
            pick(chain, dve, 0, lg[:, 0], lg)

            dve.sem_inc(s_hlo, 4)
            dve.sem_inc(s_add0, 2)

            def low(i, gg):
                for k in range(K0):
                    u = gg * K0 + k
                    dve.wait_ge(s_relu, 8 * K0 * i + u + 1 + 4)
                    dve.wait_ge(s_y0, 8 * i + gg + 1)
                    dve.scalar_tensor_tensor(out=hh_lo[:, gg % 4, k, :], in0=h32[:, u % 4, :], scalar=SH,
                                             in1=hh_hi[:, gg % 4, k, :], op0=ALU.mult, op1=ALU.subtract).then_inc(s_hlo, 1)

            wcol = sm[:, 9:11, :]

            def weight_column(i, gg, w=slice(0, NT)):
                s = gg // NC
                chain(dve.tensor_scalar(wcol[:, s, w], comb[:, w, bass.ds(2 * i + s, 1)].rearrange("p t a -> p (t a)"),
                                        1.0 / (SH * SW), None, ALU.mult))

            def add(i, gg):
                s, g = gg // NC % 2, gg % NC
                dve.wait_ge(s_y0, 8 * i + gg + 1 + 4)
                if not (isinstance(i, int) and 8 * i + gg == 0):
                    dve.wait_ge(s_add0, 8 * i + gg + 2)
                for q in range(TPC):
                    t = TPC * g + q
                    last = dve.scalar_tensor_tensor(out=x[:, t, :], in0=ps[:, 2 + gg % 2, P * q:P * q + P],
                                                    scalar=wcol[:, s, t:t + 1], in1=x[:, t, :], op0=ALU.mult, op1=ALU.add)
                last.then_inc(s_add0, 1)

            def statistics_of_gnn1(g):
                dve.wait_ge(s_add0, (E0 - 1) * NC + g + 1 + 2)
                statistics(g, x)

            def turn(i, first, last):
                for gg in range(2 * NC):
                    low(i, gg)
                    if first and gg == 0:
                        pick(chain, dve, 1, lg[:, 5], lg)
                        dve.tensor_tensor(sm[:, 2], sm[:, 1], sm[:, 0], ALU.subtract).then_inc(s_diff, 1)
                    if first and gg == 1:
                        dve.wait_ge(s_ediff, 1)
                        chain(dve.tensor_scalar(sm[:, 6], sm[:, 3], 1.0, None, ALU.add))
                        chain(dve.reciprocal(sm[:, 7], sm[:, 6]))
                        chain(dve.tensor_tensor(sm[:, 8], sm[:, 3], sm[:, 7], ALU.mult))
                        combine_weights(chain, dve, sm[:, 7], sm[:, 8], lg).then_inc(s_comb, 1)
                        dve.wait_ge(s_comb, 1)
                        dve.wait_ge(s_degc, 1)
                        dve.tensor_scalar(sm[:, 11, :], ps[:, 5, 0:NT], 1.0, None, ALU.add).then_inc(s_degv, 1)
                    if gg in (2, 6):
                        weight_column(i, gg - 2)
                    if not first or gg >= 2:
                        add(i, gg - 2)
                    if last and gg >= NC + 2:
                        statistics_of_gnn1(gg - 2 - NC)
                    if first and gg in (6, 7):
                        half = gg - 6
                        w = slice(2 * TPC * half, 2 * TPC * half + 2 * TPC)
                        dve.wait_ge(s_b2, half + 1)
                        dve.wait_ge(s_add0, gg - 1 + 2)
                        dve.tensor_tensor(x[:, w, :].rearrange("p t d -> p (t d)"), ps[:, 4:6, :].rearrange("p c t -> p (c t)"),
                                          x[:, w, :].rearrange("p t d -> p (t d)"), ALU.add).then_inc(s_b2a, 1)
                        dve.wait_ge(s_b2a, half + 1)

            turn(0, True, False)
            with dve.Fori(1, E0 // 2 - 1) as i:
                chain.turn(i - 1, 2)
                turn(i, False, False)
                chain.turn_ends(2)
            chain.loop_ends(E0 // 2 - 2, 2)
            turn(E0 // 2 - 1, False, True)
            for gg in (2 * NC - 2, 2 * NC - 1):
                add(E0 // 2 - 1, gg)
                statistics_of_gnn1(gg - NC)

            for g in range(NC):
                dve.wait_ge(s_rstd, 2 * NC + g + 1)
                for t in range(TPC * g, TPC * g + TPC):
                    last = dve.tensor_scalar(G[:, t, :], x[:, t, :], mv[:, t, 0:1], rd[:, t:t + 1], ALU.subtract, ALU.mult)
                last.then_inc(s_xn, 1)

            dve.wait_ge(s_attw, 16 * (2 * NH + 5))
            for src, ln, a, b in ((wq32, 2, WQ, WQR), (wk32, 2, WK, WKR), (wv32, 2, WV, WR), (wr32, 3, WR, WR + 8)):
                chain(dve.tensor_scalar(src, src, cols[:, ln:ln + 1], SW, ALU.mult, ALU.mult))
                chain(split(watt[:, 0, a:b], watt[:, 1, a:b], src, 1.0))
            for part in range(2):
                for a, b, n in ((WQ, WQR, NH), (WK, WKR, NKV)):
                    w = HD * n
                    src = watt[:, part, a:a + w].rearrange("p (h s d) -> p h s d", h=n, s=2)
                    dst = watt[:, part, b:b + w].rearrange("p (h s d) -> p h s d", h=n, s=2)
                    dve.tensor_scalar(dst[:, :, 0, :], src[:, :, 1, :], -1.0, None, ALU.mult)
                    last = dve.tensor_copy(dst[:, :, 1, :], src[:, :, 0, :])
            last.then_inc(s_attws, 1)

            def scaled_product(c, bank):
                for q in range(TPC):
                    t = TPC * c + q
                    last = dve.tensor_scalar(zs[:, c % 2, P * q:P * q + P], ps[:, bank, P * q:P * q + P], dis[:, t:t + 1],
                                             None, ALU.mult)
                return last

            def elu(c, scaled=False):
                if not scaled:
                    dve.wait_ge(s_z, c + 1)
                    chain(scaled_product(c, 2))
                dve.tensor_scalar(ez[:, c % 2, :], zs[:, c % 2, :], 0.0, None, ALU.min).then_inc(s_zn, 1)
                chain(dve.scalar_tensor_tensor(out=rows(x, c), in0=zs[:, c % 2, :], scalar=0.0, in1=rows(x, c), op0=ALU.max, op1=ALU.add))
                dve.wait_ge(s_ez, c + 1)
                dve.scalar_tensor_tensor(out=rows(x, c), in0=ez[:, c % 2, :], scalar=-1.0, in1=rows(x, c), op0=ALU.add,
                                         op1=ALU.add).then_inc(s_x3, 1)



            def elu_and_statistics(c):
                elu(c)
                dve.wait_ge(s_x3, c + 1)
                statistics(c, x)

            def layer1_rows(c):
                normalise(3 * NC + c + 1, c, x, xn)
                if c >= 2:
                    dve.wait_ge(s_tr1, c - 1)
                for q in range(TPC):
                    t = TPC * c + q
                    last = dve.tensor_scalar(frow[:, c % 2, P * q:P * q + P], x[:, t, :], mv[:, t, 0:1], rd[:, t:t + 1],
                                             ALU.subtract, ALU.mult)
                last.then_inc(s_hn, 1)

            def low1(c):
                dve.wait_ge(s_thi, c + 1)
                dve.scalar_tensor_tensor(out=tl[:, CW * c:CW * c + CW], in0=ps[:, 3, :], scalar=SX,
                                         in1=th[:, CW * c:CW * c + CW], op0=ALU.mult, op1=ALU.subtract).then_inc(s_tlo, 1)

            def rotate(c, parts, b0, ready, done, high_done, low_done, dst):
                dve.wait_ge(ready, c + 1)
                for n, table in enumerate((cos_sb, sin_sb)):
                    last = dve.scalar_tensor_tensor(out=rope[0:parts, b0 + n, :], in0=ps[0:parts, 6 + n, :],
                                                    scalar=SQ / (SX * SW), in1=table[0:parts, CW * c:CW * c + CW],
                                                    op0=ALU.mult, op1=ALU.mult)
                chain(last)
                dve.tensor_tensor(rope[0:parts, b0 + 2, :], rope[0:parts, b0, :], rope[0:parts, b0 + 1, :],
                                  ALU.add).then_inc(done, 1)
                dve.wait_ge(high_done, c + 1)
                dve.tensor_tensor(dst(c, 1), rope[0:parts, b0 + 2, :], dst(c, 0), ALU.subtract).then_inc(low_done, 1)
                dve.wait_ge(low_done, c + 1)

            def rotate_queries(c):
                rotate(c, P, 0, s_qp, s_qr, s_qhi, s_qlo, q16)

            def rotate_keys(c):
                rotate(c, NKV * HD, 3, s_kp, s_kr, s_khi, s_klo, k16)

            def route(step, w, n):
                W = w.stop - w.start
                bc = lambda v: v.unsqueeze(2).broadcast_to([P, W, 8])
                at = n * ROUTE_STEPS + step
                logits, exps, eq, key = lg1[:, 0, w], lg1[:, 2, w], lg1[:, 1, w], lg1[:, 8, w]
                hot = (lg1[:, 3, w], lg1[:, 4, w])
                rest = lg1[:, 5, w]
                value = (sm[:, 0, w], sm[:, 1, w])
                a, b, km = sm[:, 2, w], sm[:, 3, w], sm[:, 5, w]
                if at:
                    dve.wait_ge(s_route, at)
                if step == 0:
                    dve.wait_ge(s_rmf, unit_no[("logit", (w.stop - 1) // TPC)] + 1)
                    i = dve.reduce_max(a, logits, AX_X)
                elif step == 1:
                    i = dve.tensor_tensor(eq, logits, bc(a), ALU.subtract)
                elif step == 2:
                    dve.wait_ge(s_re, n + 1)
                    i = dve.reduce_sum(a, exps, AX_X)
                elif step == 3:
                    i = dve.reciprocal(b, a)
                elif step == 4:
                    i = dve.tensor_tensor(logits, exps, bc(b), ALU.mult)
                elif step in (5, 11):
                    i = dve.reduce_max(value[step // 11], logits if step == 5 else rest, AX_X)
                elif step in (6, 12):
                    i = dve.tensor_tensor(eq, logits if step == 6 else rest, bc(value[step // 12]), ALU.is_equal)
                elif step in (7, 13):
                    i = dve.tensor_tensor(key, eq, rev[:, w, :], ALU.mult)
                elif step in (8, 14):
                    i = dve.reduce_max(km, key, AX_X)
                elif step in (9, 15):
                    i = dve.tensor_tensor(hot[step // 15], key, bc(km), ALU.is_equal)
                elif step == 10:
                    i = dve.scalar_tensor_tensor(out=rest, in0=hot[0], scalar=NEG, in1=logits, op0=ALU.mult, op1=ALU.add)
                elif step == 16:
                    i = dve.scalar_tensor_tensor(out=a, in0=value[0], scalar=1e-9, in1=value[1], op0=ALU.add, op1=ALU.add)
                elif step == 17:
                    i = dve.reciprocal(b, a)
                elif step in (18, 19):
                    i = dve.tensor_tensor(sm[:, 6 + step - 18, w], value[step - 18], b, ALU.mult)
                elif step in (20, 21):
                    i = dve.tensor_tensor(lg1[:, 6 + step - 20, w], hot[step - 20], bc(sm[:, 6 + step - 20, w]), ALU.mult)
                else:
                    i = dve.tensor_tensor(comb[:, w, :], lg1[:, 6, w], lg1[:, 7, w], ALU.add)
                i.then_inc(s_route, 1)

            def unit(what):
                if filled_by_pe(what):
                    n, bank = unit_no[what], unit_bank(what)
                    dve.wait_ge(s_rm, n + 1)
                if what[0] == "max":
                    _, t, h, b = what
                    width = P * (t % TPC + 1) if b == t // TPC else CW
                    dve.reduce_max(pm[:, h, t % TPC, b:b + 1], ps[:, bank, 0:width], AX_X).then_inc(s_rmf, 1)
                    c = t // TPC
                    if what == max_units(c)[-1]:
                        dve.wait_ge(s_rmf, n + 1)
                        chain(dve.reduce_max(m32[:, :, :], pm[:, :, :, 0:c + 1], AX_X))
                        dve.tensor_scalar(m16[:, :, :], m32[:, :, :], -1.0 / 16.0, None, ALU.mult).then_inc(s_m, 1)
                        dve.wait_ge(s_m, c + 1)
                elif what[0] == "neg":
                    _, c, h = what
                    dve.tensor_copy(queries(c, h)[KQ:KQ + 1], ps[KQ:KQ + 1, bank, :]).then_inc(s_rmf, 1)
                elif what[0] == "out":
                    c = what[1]
                    w = slice(TPC * c, TPC * c + TPC)
                    dve.tensor_tensor(rows(xn, c), ps[:, bank, :], rows(xn, c), ALU.add).then_inc(s_rmf, 1)
                    dve.wait_ge(s_rmf, n + 1)
                    for t in range(TPC * c, TPC * c + TPC):
                        last = dve.bn_stats(bst[:, t, :], xn[:, t, :])
                    chain(last)
                    for t in range(TPC * c, TPC * c + TPC):
                        last = dve.bn_aggr(mv[:, t, :], bst[:, t, :])
                    chain(last)
                    chain(dve.tensor_tensor(ve[:, w], mv[:, w, 0], mv[:, w, 0], ALU.mult))
                    dve.scalar_tensor_tensor(out=ve[:, w], in0=ve[:, w], scalar=EPS_RMS, in1=mv[:, w, 1], op0=ALU.add,
                                             op1=ALU.add).then_inc(s_ms, 1)
                elif what[0] == "div":
                    divide(what[1])
                elif what[0] == "rows":
                    c = what[1]
                    dve.wait_ge(s_r2, c + 1)
                    for t in range(TPC * c, TPC * c + TPC):
                        last = dve.tensor_scalar(G[:, t, :], xn[:, t, :], rd[:, t:t + 1], None, ALU.mult)
                    last.then_inc(s_fn, 1)
                    dve.tensor_tensor(rows(x, c), rows(x, c), rows(xn, c), ALU.add).then_inc(s_x4, 1)
                elif what[0] == "tr":
                    c = what[1]
                    dve.wait_ge(s_thi, NC + c + 1)
                    dve.scalar_tensor_tensor(out=tl[:, CW * c:CW * c + CW], in0=ps[:, bank, :], scalar=SX,
                                             in1=th[:, CW * c:CW * c + CW], op0=ALU.mult, op1=ALU.subtract).then_inc(s_rmf, 1)
                elif what[0] == "w":
                    scaled_product(what[1], bank).then_inc(s_rmf, 1)
                    dve.wait_ge(s_rmf, n + 1)
                elif what[0] == "elu":
                    elu(what[1], scaled=True)
                elif what[0] == "stat":
                    dve.wait_ge(s_x3, what[1] + 1)
                    statistics(what[1], x)
                elif what[0] == "rows1":
                    layer1_rows(what[1])
                elif what[0] == "t":
                    c = what[1]
                    dve.wait_ge(s_thi, c + 1)
                    dve.scalar_tensor_tensor(out=tl[:, CW * c:CW * c + CW], in0=ps[:, bank, :], scalar=SX,
                                             in1=th[:, CW * c:CW * c + CW], op0=ALU.mult, op1=ALU.subtract).then_inc(s_rmf, 1)
                elif what[0] in ("qa", "qb", "ka", "kb"):
                    c = what[1]
                    parts, b0 = (P, 0) if what[0][0] == "q" else (NKV * HD, 3)
                    swapped = what[0][1] == "b"
                    table = sin_sb if swapped else cos_sb
                    dve.scalar_tensor_tensor(out=rope[0:parts, b0 + swapped, :], in0=ps[0:parts, bank, :],
                                             scalar=SQ / (SX * SW), in1=table[0:parts, CW * c:CW * c + CW],
                                             op0=ALU.mult, op1=ALU.mult).then_inc(s_rmf, 1)
                elif what[0] in ("qsum", "ksum"):
                    parts, b0, done = (P, 0, s_qr) if what[0][0] == "q" else (NKV * HD, 3, s_kr)
                    dve.wait_ge(s_rmf, unit_no[(what[0][0] + "b", what[1])] + 1)
                    dve.tensor_tensor(rope[0:parts, b0 + 2, :], rope[0:parts, b0, :], rope[0:parts, b0 + 1, :],
                                      ALU.add).then_inc(done, 1)
                elif what[0] in ("qlow", "klow"):
                    c = what[1]
                    parts, b0, high_done, low_done, dst = ((P, 0, s_qhi, s_qlo, q16) if what[0][0] == "q" else
                                                           (NKV * HD, 3, s_khi, s_klo, k16))
                    dve.wait_ge(high_done, c + 1)
                    dve.tensor_tensor(dst(c, 1), rope[0:parts, b0 + 2, :], dst(c, 0), ALU.subtract).then_inc(low_done, 1)
                    dve.wait_ge(low_done, c + 1)
                elif what[0] == "v":
                    c = what[1]
                    dve.tensor_scalar(A[:, 3, CW * c:CW * c + TPC * NKV * HD], ps[:, bank, 0:TPC * NKV * HD],
                                      1.0 / (SX * SW), None, ALU.mult).then_inc(s_rmf, 1)
                elif what[0] == "logit":
                    c = what[1]
                    dve.tensor_scalar(lg1[:, 0, TPC * c:TPC * c + TPC], ps[:, bank, 0:8 * TPC].rearrange("p (t e) -> p t e", e=8),
                                      1.0 / (SX * SW), None, ALU.mult).then_inc(s_rmf, 1)
                elif what == ("choose", 0):
                    for step in (0, 1):
                        route(step, EARLY, 0)
                elif what == ("choose", 2):
                    for step in range(2, ROUTE_STEPS):
                        route(step, EARLY, 0)

            def divide(c):
                dve.wait_ge(s_od, c + 1)
                chain(dve.reciprocal(r_sb, d_sb[c]))
                dve.tensor_tensor(yT[:, c, :], o_sb[c], r_sb, ALU.mult).then_inc(s_yT, 1)
                dve.wait_ge(s_yT, c + 1)

            elu_and_statistics(0)
            layer1_rows(0)
            low1(0)
            rotate_queries(0)
            elu_and_statistics(1)
            rotate_keys(0)
            layer1_rows(1)
            low1(1)
            rotate_queries(1)
            elu_and_statistics(2)
            rotate_keys(1)
            for what in max_units(0) + neg_units(0):
                unit(what)
            layer1_rows(2)
            for step in steps:
                for what in units_at[step]:
                    unit(what)
            divide(NC - 1)

            dve.sem_inc(s_hh, 3)
            dve.sem_inc(s_glo, 6)
            dve.sem_inc(s_add1, 2)

            def hidden(i, u):
                k = u % 3
                r = KS1[k][1]
                dve.wait_ge(s_silu, 24 * i + u + 1 + 3)
                dve.wait_ge(s_h3, 24 * i + u + 1)
                dve.wait_ge(s_glo, 24 * i + u + 1)
                dve.scalar_tensor_tensor(out=g32[0:r, u % 6, :], in0=ps[0:r, 3 + k, :], scalar=SH / (SX * SW),
                                         in1=silu_sb[0:r, k, :], op0=ALU.mult, op1=ALU.mult).then_inc(s_hh, 1)

            def low_hidden(i, u):
                gg, k = u // 3, u % 3
                r = KS1[k][1]
                dve.wait_ge(s_ghi, 24 * i + u + 1)
                dve.tensor_tensor(g_lo(gg % 4, k)[0:r], g32[0:r, u % 6, :], g_hi(gg % 4, k)[0:r],
                                  ALU.subtract).then_inc(s_glo, 1)

            def add1(i, gg):
                s, g = gg // NC % 2, gg % NC
                if isinstance(i, int) and 8 * i + gg == 0:
                    weight_column(0, 0, EARLY)
                elif isinstance(i, int) and 8 * i + gg == NC - 1:
                    dve.wait_ge(s_route, 2 * ROUTE_STEPS)
                    weight_column(0, 0, LATE)
                elif g == 0:
                    weight_column(i, gg)
                dve.wait_ge(s_y1, 8 * i + gg + 1 + 4)
                dve.wait_ge(s_add1, 8 * i + gg + 2)
                for q in range(TPC):
                    t = TPC * g + q
                    last = dve.scalar_tensor_tensor(out=x[:, t, :], in0=ps[:, 6 + gg % 2, P * q:P * q + P],
                                                    scalar=wcol[:, s, t:t + 1], in1=x[:, t, :], op0=ALU.mult, op1=ALU.add)
                last.then_inc(s_add1, 1)

            AT_UNIT = {2: "out", 3: "rows", 5: "tr", 8: "logit"}

            def turn1(i, first):
                for u in range(24):
                    hidden(i, u)
                    if u or not first:
                        low_hidden(i, u - 1)
                    if u % 3 == 0 and (u // 3 >= 2 or not first):
                        add1(i, u // 3 - 2)
                    if first and u in AT_UNIT:
                        unit((AT_UNIT[u], NC - 1))
                    if first and u == 9:
                        route(0, LATE, 1)
                        route(1, LATE, 1)
                    if first and 10 <= u < 15:
                        for step in range(2 + 5 * (u - 10), min(7 + 5 * (u - 10), ROUTE_STEPS)):
                            route(step, LATE, 1)

            turn1(0, True)
            with dve.Fori(1, E1 // 2) as i:
                chain.turn(i - 1, 2)
                turn1(i, False)
                chain.turn_ends(2)
            chain.loop_ends(E1 // 2 - 1, 2)
            low_hidden(E1 // 2 - 1, 23)
            add1(E1 // 2 - 1, 2 * NC - 2)
            add1(E1 // 2 - 1, 2 * NC - 1)


_NAMES = ["x_in", "adj_t", "adj_in", "w_proj", "b_proj", "w_gcn", "b_gcn", "f0_wg", "f0_bg", "f0_bias", "f0_w1", "f0_b1",
          "f0_w2", "f0_b2", "g1_w", "ln1", "ln2", "wq", "wk", "wv", "wo", "w_router", "f1_w1", "f1_w2", "f1_w3",
          "cos_t", "sin_t"]


def lay_out(a):
    import numpy as np

    def rows(v):
        return v.reshape(NT, P, -1).transpose(1, 0, 2)

    freq = np.float32(1.0) / np.float32(10000.0) ** (np.arange(0, HD, 2, dtype=np.float32) / HD)
    emb = np.outer(np.arange(T, dtype=np.float32), np.concatenate([freq, freq]))
    col = lambda v: v.reshape(P, 1)
    d = {
        "x_in": rows(a["x"]), "adj_t": a["adj"].T.reshape(NT, P, T), "adj_in": a["adj"].reshape(NT, P, T),
        "w_proj": a["L0_gnn_W_proj"], "b_proj": col(a["L0_gnn_b_proj"]), "w_gcn": a["L0_gnn_W_gcn"],
        "b_gcn": col(a["L0_gnn_b_gcn"]), "f0_wg": a["L0_ffn_Wg"], "f0_bg": a["L0_ffn_bg"], "f0_bias": a["L0_ffn_bias"],
        "f0_w1": a["L0_ffn_W1"], "f0_b1": a["L0_ffn_b1"].reshape(E0, K0, P).transpose(0, 2, 1),
        "f0_w2": a["L0_ffn_W2"].reshape(E0, K0, P, D).transpose(0, 2, 1, 3), "f0_b2": a["L0_ffn_b2"],
        "g1_w": a["L1_gnn_w"], "ln1": col(a["L1_ffn_ln1_w"]), "ln2": col(a["L1_ffn_ln2_w"]),
        "wq": a["L1_ffn_wq"].T, "wk": a["L1_ffn_wk"].T, "wv": a["L1_ffn_wv"].T, "wo": a["L1_ffn_wo"].T,
        "w_router": a["L1_ffn_router_w"].T, "f1_w1": a["L1_ffn_w1"].transpose(0, 2, 1),
        "f1_w2": a["L1_ffn_w2"].transpose(0, 2, 1), "f1_w3": a["L1_ffn_w3"].transpose(0, 2, 1),
        "cos_t": np.cos(emb).T, "sin_t": np.sin(emb).T,
    }
    return {k: np.ascontiguousarray(v) for k, v in d.items()}


def kernel(**inputs):
    import numpy as np
    import concourse.bacc as bacc
    from concourse.bass_utils import run_bass_kernel_spmd

    arrays = lay_out({k: np.asarray(v) for k, v in inputs.items()})
    nc = bacc.Bacc("TRN2", target_bir_lowering=False, num_devices=1)
    args = [nc.dram_tensor(f"in_{n}", arrays[n].shape, mybir.dt.from_np(arrays[n].dtype), kind="ExternalInput").ap()
            for n in _NAMES]
    args.append(nc.dram_tensor("out", (P, NT, D), F32, kind="ExternalOutput").ap())
    program(nc, *args)
    r = run_bass_kernel_spmd(nc, [{f"in_{n}": arrays[n] for n in _NAMES}], core_ids=[0])
    return np.ascontiguousarray(r.results[0]["out"].transpose(1, 0, 2).reshape(T, D))
```
